# Optimizing a Trainium2 kernel written in Bass

```python
import numpy as np
import jax
import jax.numpy as jnp

def _softmax(x, axis=-1):
    return jax.nn.softmax(x, axis=axis)

def _gelu(x):
    return jax.nn.gelu(x, approximate=True)

def _silu(x):
    return jax.nn.silu(x)

def _sigmoid(x):
    return jax.nn.sigmoid(x)

def _layernorm(x, axis=-1, eps=1e-05):
    m = jnp.mean(x, axis=axis, keepdims=True)
    v = jnp.var(x, axis=axis, keepdims=True)
    return (x - m) / jnp.sqrt(v + eps)

def _scatter_add(tgt, idx, src, axis=0):
    return tgt.at[idx].add(src)

def _segment_sum(src, seg, n):
    return jax.ops.segment_sum(src, seg, n)
kernel_name = 'mk_vit_tower_d2_tok_img768_r4_3a9c8f'

def setup_inputs(seed: int=0):
    np.random.seed(seed)
    _w = jnp.asarray

    def _rec_inputs():
        import jax
        import jax.numpy as jnp
        _rk = jax.random.key(seed)
        x = 7.57192e-06 + 1.00007 * jax.random.normal(jax.random.fold_in(_rk, 1), (64, 3, 96, 96), jnp.float32)
        return x
    x = _rec_inputs()

    def _L0_tok_setup():
        import jax, jax.numpy as jnp
        import numpy as np
        K = 4
        STRIDE = 4
        EPS = 1e-05
        SLOPE = 0.01

        def conv2d(x, w, b, stride):
            out = jax.lax.conv_general_dilated(x, w, (stride, stride), 'VALID', dimension_numbers=('NCHW', 'OIHW', 'NCHW'))
            return out + b[None, :, None, None]

        def batchnorm(x, g, b, m, v):
            inv = g / jnp.sqrt(v + EPS)
            return x * inv[None, :, None, None] + (b - m * inv)[None, :, None, None]

        def leaky_relu(x):
            return jnp.where(x >= 0, x, SLOPE * x)

        def deform_conv(x, offset, w, b):
            B, C, H, W = x.shape
            Ho, Wo = (offset.shape[2], offset.shape[3])
            KK = K * K
            off = offset.reshape(B, KK, 2, Ho, Wo)
            kh = jnp.repeat(jnp.arange(K), K).astype(x.dtype)
            kw = jnp.tile(jnp.arange(K), K).astype(x.dtype)
            base_y = (jnp.arange(Ho) * STRIDE).astype(x.dtype)
            base_x = (jnp.arange(Wo) * STRIDE).astype(x.dtype)
            py = base_y[None, None, :, None] + kh[None, :, None, None] + off[:, :, 0]
            px = base_x[None, None, None, :] + kw[None, :, None, None] + off[:, :, 1]
            y0 = jnp.floor(py)
            x0 = jnp.floor(px)
            wy = py - y0
            wx = px - x0

            def corner(yc, xc):
                yi = yc.astype(jnp.int32)
                xi = xc.astype(jnp.int32)
                valid = (yi >= 0) & (yi < H) & (xi >= 0) & (xi < W)
                yi = jnp.clip(yi, 0, H - 1)
                xi = jnp.clip(xi, 0, W - 1)
                v = jax.vmap(lambda img, a, c: img[:, a, c])(x, yi, xi)
                return v * valid[:, None].astype(x.dtype)
            v00 = corner(y0, x0)
            v01 = corner(y0, x0 + 1)
            v10 = corner(y0 + 1, x0)
            v11 = corner(y0 + 1, x0 + 1)
            wy_ = wy[:, None]
            wx_ = wx[:, None]
            sampled = v00 * (1 - wy_) * (1 - wx_) + v01 * (1 - wy_) * wx_ + v10 * wy_ * (1 - wx_) + v11 * wy_ * wx_
            out = jnp.einsum('bckhw,ock->bohw', sampled, w.reshape(w.shape[0], C, KK))
            return out + b[None, :, None, None]
        key = jax.random.key(seed)
        ks = jax.random.split(key, 16)
        f32 = jnp.float32
        inp = {'x': jax.random.normal(ks[0], (64, 3, 224, 224), f32), 'stem_w': jax.random.normal(ks[1], (96, 3, 4, 4), f32) * 0.1, 'stem_b': jax.random.normal(ks[2], (96,), f32) * 0.05, 'bn1_g': jax.random.uniform(ks[3], (96,), f32, 0.5, 1.5), 'bn1_b': jax.random.normal(ks[4], (96,), f32) * 0.05, 'bn1_m': jax.random.normal(ks[5], (96,), f32) * 0.05, 'bn1_v': jax.random.uniform(ks[6], (96,), f32, 0.5, 1.5), 'off_w': jax.random.normal(ks[7], (32, 96, 4, 4), f32) * 0.02, 'off_b': jax.random.normal(ks[8], (32,), f32) * 0.02, 'dcn_w': jax.random.normal(ks[9], (192, 96, 4, 4), f32) * 0.05, 'dcn_b': jax.random.normal(ks[10], (192,), f32) * 0.05, 'bn2_g': jax.random.uniform(ks[11], (192,), f32, 0.5, 1.5), 'bn2_b': jax.random.normal(ks[12], (192,), f32) * 0.05, 'bn2_m': jax.random.normal(ks[13], (192,), f32) * 0.05, 'bn2_v': jax.random.uniform(ks[14], (192,), f32, 0.5, 1.5)}
        return inp
    _L0_tok_all = _L0_tok_setup()
    _L0_tok_in = {k: v for k, v in _L0_tok_all.items() if k in ('stem_w', 'stem_b', 'bn1_g', 'bn1_b', 'bn1_m', 'bn1_v', 'off_w', 'off_b', 'dcn_w', 'dcn_b', 'bn2_g', 'bn2_b', 'bn2_m', 'bn2_v')}
    del _L0_tok_all

    def _L0_attn_setup():
        import jax, jax.numpy as jnp
        import numpy as np
        import math
        D_MODEL = 192
        D_STATE = 16
        D_CONV = 4
        EXPAND = 2
        D_INNER = EXPAND * D_MODEL
        DT_RANK = math.ceil(D_MODEL / 16)
        BATCH = 2
        SEQ = 512
        EPS = 1e-05

        def _mamba(h, in_w, conv_w, conv_b, xproj_w, dt_w, dt_b, A_log, Dp, out_w):
            Bb, Ls, _ = h.shape
            xz = h @ in_w.T
            u, z = jnp.split(xz, 2, axis=-1)
            up = jnp.pad(u, ((0, 0), (D_CONV - 1, 0), (0, 0)))
            uc = conv_b + sum((conv_w[:, k] * up[:, k:k + Ls, :] for k in range(D_CONV)))
            u = jax.nn.silu(uc)
            dbl = u @ xproj_w.T
            dt = dbl[..., :DT_RANK]
            Bm = dbl[..., DT_RANK:DT_RANK + D_STATE]
            Cm = dbl[..., DT_RANK + D_STATE:]
            delta = jax.nn.softplus(dt @ dt_w.T + dt_b)
            A = -jnp.exp(A_log)

            def step(hst, ins):
                d_t, B_t, C_t, u_t = ins
                dA = jnp.exp(d_t[..., None] * A)
                hst = dA * hst + (d_t * u_t)[..., None] * B_t[:, None, :]
                y = jnp.einsum('bds,bs->bd', hst, C_t)
                return (hst, y)
            h0 = jnp.zeros((Bb, D_INNER, D_STATE), h.dtype)
            xs = (delta.transpose(1, 0, 2), Bm.transpose(1, 0, 2), Cm.transpose(1, 0, 2), u.transpose(1, 0, 2))
            _, ys = jax.lax.scan(step, h0, xs)
            y = ys.transpose(1, 0, 2) + u * Dp
            y = y * jax.nn.silu(z)
            return y @ out_w.T
        key = jax.random.key(seed)
        ks = jax.random.split(key, 8)
        s = lambda k, shape, sc: jax.random.normal(k, shape, jnp.float32) * sc
        dt_tgt = 0.001 + (0.1 - 0.001) * jax.random.uniform(ks[5], (D_INNER,), jnp.float32)
        return {'x': s(ks[0], (BATCH, SEQ, D_MODEL), 1.0), 'norm_w': jnp.ones((D_MODEL,), jnp.float32), 'norm_b': jnp.zeros((D_MODEL,), jnp.float32), 'in_w': s(ks[1], (2 * D_INNER, D_MODEL), D_MODEL ** (-0.5)), 'conv_w': s(ks[2], (D_INNER, D_CONV), D_CONV ** (-0.5)), 'conv_b': jnp.zeros((D_INNER,), jnp.float32), 'xproj_w': s(ks[3], (DT_RANK + 2 * D_STATE, D_INNER), D_INNER ** (-0.5)), 'dt_w': s(ks[4], (D_INNER, DT_RANK), DT_RANK ** (-0.5)), 'dt_b': jnp.log(jnp.expm1(dt_tgt)), 'A_log': jnp.log(jnp.tile(jnp.arange(1, D_STATE + 1, dtype=jnp.float32), (D_INNER, 1))), 'D': jnp.ones((D_INNER,), jnp.float32), 'out_w': s(ks[6], (D_MODEL, D_INNER), D_INNER ** (-0.5))}
    _L0_attn_all = _L0_attn_setup()
    _L0_attn_in = {k: v for k, v in _L0_attn_all.items() if k in ('norm_w', 'norm_b', 'in_w', 'conv_w', 'conv_b', 'xproj_w', 'dt_w', 'dt_b', 'A_log', 'D', 'out_w')}
    del _L0_attn_all

    def _L0_ffn_setup():
        import jax, jax.numpy as jnp
        import numpy as np
        B, L, D, H, F = (4, 512, 192, 12, 768)
        ROUTE_FRAC = 0.15
        LN_EPS = 1e-05

        def _ln(x, g, b):
            m = jnp.mean(x, axis=-1, keepdims=True)
            v = jnp.mean((x - m) ** 2, axis=-1, keepdims=True)
            return (x - m) * jax.lax.rsqrt(v + LN_EPS) * g + b
        key = jax.random.key(seed)
        ks = jax.random.split(key, 20)
        s = 0.02
        return {'hidden_states': jax.random.normal(ks[0], (B, L, D), dtype=jnp.float32), 'g1': jnp.ones((D,), jnp.float32), 'b1': jnp.zeros((D,), jnp.float32), 'g2': jnp.ones((D,), jnp.float32), 'b2': jnp.zeros((D,), jnp.float32), 'Wr': jax.random.normal(ks[1], (D,), jnp.float32) * s, 'br': jnp.zeros((), jnp.float32), 'Wq': jax.random.normal(ks[2], (D, D), jnp.float32) * s, 'bq': jnp.zeros((D,), jnp.float32), 'Wk': jax.random.normal(ks[3], (D, D), jnp.float32) * s, 'bk': jnp.zeros((D,), jnp.float32), 'Wv': jax.random.normal(ks[4], (D, D), jnp.float32) * s, 'bv': jnp.zeros((D,), jnp.float32), 'Wo': jax.random.normal(ks[5], (D, D), jnp.float32) * s, 'bo': jnp.zeros((D,), jnp.float32), 'Wm': jax.random.normal(ks[6], (D, D), jnp.float32) * s, 'bm': jnp.zeros((D,), jnp.float32), 'W1': jax.random.normal(ks[7], (D, F), jnp.float32) * s, 'bf1': jnp.zeros((F,), jnp.float32), 'W2': jax.random.normal(ks[8], (F, D), jnp.float32) * s, 'bf2': jnp.zeros((D,), jnp.float32)}
    _L0_ffn_all = _L0_ffn_setup()
    _L0_ffn_in = {k: v for k, v in _L0_ffn_all.items() if k in ('g1', 'b1', 'g2', 'b2', 'Wr', 'br', 'Wq', 'bq', 'Wk', 'bk', 'Wv', 'bv', 'Wo', 'bo', 'Wm', 'bm', 'W1', 'bf1', 'W2', 'bf2')}
    del _L0_ffn_all

    def _L1_attn_setup():
        import jax, jax.numpy as jnp
        import numpy as np
        HEADS = 12
        ROPE_THETA = 10000.0

        def _rope(t):
            B, H, N, D = t.shape
            inv_freq = 1.0 / ROPE_THETA ** (jnp.arange(0, D, 2, dtype=jnp.float32) / D)
            freqs = jnp.arange(N, dtype=jnp.float32)[:, None] * inv_freq[None, :]
            freqs = jnp.repeat(freqs, 2, axis=-1)
            cos, sin = (jnp.cos(freqs), jnp.sin(freqs))
            tp = t.reshape(B, H, N, D // 2, 2)
            rot = jnp.stack([-tp[..., 1], tp[..., 0]], axis=-1).reshape(B, H, N, D)
            return t * cos + rot * sin
        key = jax.random.key(seed)
        k1, k2, k3 = jax.random.split(key, 3)
        dim = 192
        x = jax.random.normal(k1, (2, 512, dim), dtype=jnp.float32)
        w_qkv = jax.random.normal(k2, (3 * dim, dim), dtype=jnp.float32) * dim ** (-0.5)
        w_proj = jax.random.normal(k3, (dim, dim), dtype=jnp.float32) * dim ** (-0.5)
        b_proj = jnp.zeros((dim,), dtype=jnp.float32)
        return {'x': x, 'w_qkv': w_qkv, 'w_proj': w_proj, 'b_proj': b_proj}
    _L1_attn_all = _L1_attn_setup()
    _L1_attn_in = {k: v for k, v in _L1_attn_all.items() if k in ('w_qkv', 'w_proj', 'b_proj')}
    del _L1_attn_all

    def _L1_ffn_setup():
        import jax, jax.numpy as jnp
        import numpy as np
        B, S, D = (2, 256, 192)
        I = 96
        E = 8
        G = 4
        TOPK_GROUPS = 2
        K = 2
        ROUTE_SCALE = 1.0
        ALPHA, LIMIT = (1.702, 7.0)

        def swiglu(h):
            xg = jnp.minimum(h[..., ::2], LIMIT)
            xl = jnp.clip(h[..., 1::2], -LIMIT, LIMIT)
            return xg * jax.nn.sigmoid(ALPHA * xg) * (xl + 1.0)

        def gate(x, gate_w, gate_b):
            scores = jax.nn.softmax(jnp.einsum('td,ed->te', x, gate_w).astype(jnp.float32), axis=-1)
            original_scores = scores
            s = scores + gate_b
            T = x.shape[0]
            sg = s.reshape(T, G, E // G)
            group_scores = jnp.sum(jax.lax.top_k(sg, 2)[0], axis=-1)
            _, gidx = jax.lax.top_k(group_scores, TOPK_GROUPS)
            keep = jnp.any(jax.nn.one_hot(gidx, G, dtype=jnp.bool_), axis=1)
            sg = jnp.where(keep[:, :, None], sg, -jnp.inf)
            s = sg.reshape(T, E)
            _, idx = jax.lax.top_k(s, K)
            w = jnp.take_along_axis(original_scores, idx, axis=1) * ROUTE_SCALE
            return (w.astype(x.dtype), idx)

        def expert_ffn(x, W1, B1, W3, B3, W2, B2):
            h1 = jnp.einsum('td,edh->teh', x, W1) + B1
            h3 = jnp.einsum('td,edh->teh', x, W3) + B3
            g = swiglu(h1 * h3)
            return jnp.einsum('tei,eid->ted', g, W2) + B2

        def shared_ffn(x, Ws1, Bs1, Ws3, Bs3, Ws2, Bs2):
            h = (x @ Ws1 + Bs1) * (x @ Ws3 + Bs3)
            return swiglu(h) @ Ws2 + Bs2
        key = jax.random.key(seed)
        ks = jax.random.split(key, 16)
        sc = 0.02
        inp = {'x': jax.random.normal(ks[0], (B, S, D), jnp.float32), 'gate_w': jax.random.normal(ks[1], (E, D), jnp.float32) * sc, 'gate_b': jax.random.normal(ks[2], (E,), jnp.float32) * sc, 'W1': jax.random.normal(ks[3], (E, D, 2 * I), jnp.float32) * sc, 'B1': jax.random.normal(ks[4], (E, 2 * I), jnp.float32) * sc, 'W3': jax.random.normal(ks[5], (E, D, 2 * I), jnp.float32) * sc, 'B3': jax.random.normal(ks[6], (E, 2 * I), jnp.float32) * sc, 'W2': jax.random.normal(ks[7], (E, I, D), jnp.float32) * sc, 'B2': jax.random.normal(ks[8], (E, D), jnp.float32) * sc, 'Ws1': jax.random.normal(ks[9], (D, 2 * I), jnp.float32) * sc, 'Bs1': jax.random.normal(ks[10], (2 * I,), jnp.float32) * sc, 'Ws3': jax.random.normal(ks[11], (D, 2 * I), jnp.float32) * sc, 'Bs3': jax.random.normal(ks[12], (2 * I,), jnp.float32) * sc, 'Ws2': jax.random.normal(ks[13], (I, D), jnp.float32) * sc, 'Bs2': jax.random.normal(ks[14], (D,), jnp.float32) * sc}
        return inp
    _L1_ffn_all = _L1_ffn_setup()
    _L1_ffn_in = {k: v for k, v in _L1_ffn_all.items() if k in ('gate_w', 'gate_b', 'W1', 'B1', 'W3', 'B3', 'W2', 'B2', 'Ws1', 'Bs1', 'Ws3', 'Bs3', 'Ws2', 'Bs2')}
    del _L1_ffn_all
    return {'x': x, 'L0_tok_stem_w': _L0_tok_in['stem_w'], 'L0_tok_stem_b': _L0_tok_in['stem_b'], 'L0_tok_bn1_g': _L0_tok_in['bn1_g'], 'L0_tok_bn1_b': _L0_tok_in['bn1_b'], 'L0_tok_bn1_m': _L0_tok_in['bn1_m'], 'L0_tok_bn1_v': _L0_tok_in['bn1_v'], 'L0_tok_off_w': _L0_tok_in['off_w'], 'L0_tok_off_b': _L0_tok_in['off_b'], 'L0_tok_dcn_w': _L0_tok_in['dcn_w'], 'L0_tok_dcn_b': _L0_tok_in['dcn_b'], 'L0_tok_bn2_g': _L0_tok_in['bn2_g'], 'L0_tok_bn2_b': _L0_tok_in['bn2_b'], 'L0_tok_bn2_m': _L0_tok_in['bn2_m'], 'L0_tok_bn2_v': _L0_tok_in['bn2_v'], 'L0_attn_norm_w': _L0_attn_in['norm_w'], 'L0_attn_norm_b': _L0_attn_in['norm_b'], 'L0_attn_in_w': _L0_attn_in['in_w'], 'L0_attn_conv_w': _L0_attn_in['conv_w'], 'L0_attn_conv_b': _L0_attn_in['conv_b'], 'L0_attn_xproj_w': _L0_attn_in['xproj_w'], 'L0_attn_dt_w': _L0_attn_in['dt_w'], 'L0_attn_dt_b': _L0_attn_in['dt_b'], 'L0_attn_A_log': _L0_attn_in['A_log'], 'L0_attn_D': _L0_attn_in['D'], 'L0_attn_out_w': _L0_attn_in['out_w'], 'L0_ffn_g1': _L0_ffn_in['g1'], 'L0_ffn_b1': _L0_ffn_in['b1'], 'L0_ffn_g2': _L0_ffn_in['g2'], 'L0_ffn_b2': _L0_ffn_in['b2'], 'L0_ffn_Wr': _L0_ffn_in['Wr'], 'L0_ffn_br': _L0_ffn_in['br'], 'L0_ffn_Wq': _L0_ffn_in['Wq'], 'L0_ffn_bq': _L0_ffn_in['bq'], 'L0_ffn_Wk': _L0_ffn_in['Wk'], 'L0_ffn_bk': _L0_ffn_in['bk'], 'L0_ffn_Wv': _L0_ffn_in['Wv'], 'L0_ffn_bv': _L0_ffn_in['bv'], 'L0_ffn_Wo': _L0_ffn_in['Wo'], 'L0_ffn_bo': _L0_ffn_in['bo'], 'L0_ffn_Wm': _L0_ffn_in['Wm'], 'L0_ffn_bm': _L0_ffn_in['bm'], 'L0_ffn_W1': _L0_ffn_in['W1'], 'L0_ffn_bf1': _L0_ffn_in['bf1'], 'L0_ffn_W2': _L0_ffn_in['W2'], 'L0_ffn_bf2': _L0_ffn_in['bf2'], 'L1_attn_w_qkv': _L1_attn_in['w_qkv'], 'L1_attn_w_proj': _L1_attn_in['w_proj'], 'L1_attn_b_proj': _L1_attn_in['b_proj'], 'L1_ffn_gate_w': _L1_ffn_in['gate_w'], 'L1_ffn_gate_b': _L1_ffn_in['gate_b'], 'L1_ffn_W1': _L1_ffn_in['W1'], 'L1_ffn_B1': _L1_ffn_in['B1'], 'L1_ffn_W3': _L1_ffn_in['W3'], 'L1_ffn_B3': _L1_ffn_in['B3'], 'L1_ffn_W2': _L1_ffn_in['W2'], 'L1_ffn_B2': _L1_ffn_in['B2'], 'L1_ffn_Ws1': _L1_ffn_in['Ws1'], 'L1_ffn_Bs1': _L1_ffn_in['Bs1'], 'L1_ffn_Ws3': _L1_ffn_in['Ws3'], 'L1_ffn_Bs3': _L1_ffn_in['Bs3'], 'L1_ffn_Ws2': _L1_ffn_in['Ws2'], 'L1_ffn_Bs2': _L1_ffn_in['Bs2']}

def reference(x, L0_tok_stem_w, L0_tok_stem_b, L0_tok_bn1_g, L0_tok_bn1_b, L0_tok_bn1_m, L0_tok_bn1_v, L0_tok_off_w, L0_tok_off_b, L0_tok_dcn_w, L0_tok_dcn_b, L0_tok_bn2_g, L0_tok_bn2_b, L0_tok_bn2_m, L0_tok_bn2_v, L0_attn_norm_w, L0_attn_norm_b, L0_attn_in_w, L0_attn_conv_w, L0_attn_conv_b, L0_attn_xproj_w, L0_attn_dt_w, L0_attn_dt_b, L0_attn_A_log, L0_attn_D, L0_attn_out_w, L0_ffn_g1, L0_ffn_b1, L0_ffn_g2, L0_ffn_b2, L0_ffn_Wr, L0_ffn_br, L0_ffn_Wq, L0_ffn_bq, L0_ffn_Wk, L0_ffn_bk, L0_ffn_Wv, L0_ffn_bv, L0_ffn_Wo, L0_ffn_bo, L0_ffn_Wm, L0_ffn_bm, L0_ffn_W1, L0_ffn_bf1, L0_ffn_W2, L0_ffn_bf2, L1_attn_w_qkv, L1_attn_w_proj, L1_attn_b_proj, L1_ffn_gate_w, L1_ffn_gate_b, L1_ffn_W1, L1_ffn_B1, L1_ffn_W3, L1_ffn_B3, L1_ffn_W2, L1_ffn_B2, L1_ffn_Ws1, L1_ffn_Bs1, L1_ffn_Ws3, L1_ffn_Bs3, L1_ffn_Ws2, L1_ffn_Bs2):
    import jax
    import jax.numpy as jnp

    def _L0_tok_ref(x, stem_w, stem_b, bn1_g, bn1_b, bn1_m, bn1_v, off_w, off_b, dcn_w, dcn_b, bn2_g, bn2_b, bn2_m, bn2_v):
        import jax, jax.numpy as jnp
        import numpy as np
        K = 4
        STRIDE = 4
        EPS = 1e-05
        SLOPE = 0.01

        def conv2d(x, w, b, stride):
            out = jax.lax.conv_general_dilated(x, w, (stride, stride), 'VALID', dimension_numbers=('NCHW', 'OIHW', 'NCHW'))
            return out + b[None, :, None, None]

        def batchnorm(x, g, b, m, v):
            inv = g / jnp.sqrt(v + EPS)
            return x * inv[None, :, None, None] + (b - m * inv)[None, :, None, None]

        def leaky_relu(x):
            return jnp.where(x >= 0, x, SLOPE * x)

        def deform_conv(x, offset, w, b):
            B, C, H, W = x.shape
            Ho, Wo = (offset.shape[2], offset.shape[3])
            KK = K * K
            off = offset.reshape(B, KK, 2, Ho, Wo)
            kh = jnp.repeat(jnp.arange(K), K).astype(x.dtype)
            kw = jnp.tile(jnp.arange(K), K).astype(x.dtype)
            base_y = (jnp.arange(Ho) * STRIDE).astype(x.dtype)
            base_x = (jnp.arange(Wo) * STRIDE).astype(x.dtype)
            py = base_y[None, None, :, None] + kh[None, :, None, None] + off[:, :, 0]
            px = base_x[None, None, None, :] + kw[None, :, None, None] + off[:, :, 1]
            y0 = jnp.floor(py)
            x0 = jnp.floor(px)
            wy = py - y0
            wx = px - x0

            def corner(yc, xc):
                yi = yc.astype(jnp.int32)
                xi = xc.astype(jnp.int32)
                valid = (yi >= 0) & (yi < H) & (xi >= 0) & (xi < W)
                yi = jnp.clip(yi, 0, H - 1)
                xi = jnp.clip(xi, 0, W - 1)
                v = jax.vmap(lambda img, a, c: img[:, a, c])(x, yi, xi)
                return v * valid[:, None].astype(x.dtype)
            v00 = corner(y0, x0)
            v01 = corner(y0, x0 + 1)
            v10 = corner(y0 + 1, x0)
            v11 = corner(y0 + 1, x0 + 1)
            wy_ = wy[:, None]
            wx_ = wx[:, None]
            sampled = v00 * (1 - wy_) * (1 - wx_) + v01 * (1 - wy_) * wx_ + v10 * wy_ * (1 - wx_) + v11 * wy_ * wx_
            out = jnp.einsum('bckhw,ock->bohw', sampled, w.reshape(w.shape[0], C, KK))
            return out + b[None, :, None, None]
        h = conv2d(x, stem_w, stem_b, 4)
        h = leaky_relu(batchnorm(h, bn1_g, bn1_b, bn1_m, bn1_v))
        offset = conv2d(h, off_w, off_b, 4)
        h = deform_conv(h, offset, dcn_w, dcn_b)
        h = leaky_relu(batchnorm(h, bn2_g, bn2_b, bn2_m, bn2_v))
        B, C, Ho, Wo = h.shape
        return h.reshape(B, C, Ho * Wo).transpose(0, 2, 1)

    def _L0_attn_ref(x, norm_w, norm_b, in_w, conv_w, conv_b, xproj_w, dt_w, dt_b, A_log, D, out_w):
        import jax, jax.numpy as jnp
        import numpy as np
        import math
        D_MODEL = 192
        D_STATE = 16
        D_CONV = 4
        EXPAND = 2
        D_INNER = EXPAND * D_MODEL
        DT_RANK = math.ceil(D_MODEL / 16)
        BATCH = 2
        SEQ = 512
        EPS = 1e-05

        def _mamba(h, in_w, conv_w, conv_b, xproj_w, dt_w, dt_b, A_log, Dp, out_w):
            Bb, Ls, _ = h.shape
            xz = h @ in_w.T
            u, z = jnp.split(xz, 2, axis=-1)
            up = jnp.pad(u, ((0, 0), (D_CONV - 1, 0), (0, 0)))
            uc = conv_b + sum((conv_w[:, k] * up[:, k:k + Ls, :] for k in range(D_CONV)))
            u = jax.nn.silu(uc)
            dbl = u @ xproj_w.T
            dt = dbl[..., :DT_RANK]
            Bm = dbl[..., DT_RANK:DT_RANK + D_STATE]
            Cm = dbl[..., DT_RANK + D_STATE:]
            delta = jax.nn.softplus(dt @ dt_w.T + dt_b)
            A = -jnp.exp(A_log)

            def step(hst, ins):
                d_t, B_t, C_t, u_t = ins
                dA = jnp.exp(d_t[..., None] * A)
                hst = dA * hst + (d_t * u_t)[..., None] * B_t[:, None, :]
                y = jnp.einsum('bds,bs->bd', hst, C_t)
                return (hst, y)
            h0 = jnp.zeros((Bb, D_INNER, D_STATE), h.dtype)
            xs = (delta.transpose(1, 0, 2), Bm.transpose(1, 0, 2), Cm.transpose(1, 0, 2), u.transpose(1, 0, 2))
            _, ys = jax.lax.scan(step, h0, xs)
            y = ys.transpose(1, 0, 2) + u * Dp
            y = y * jax.nn.silu(z)
            return y @ out_w.T
        mu = x.mean(-1, keepdims=True)
        var = ((x - mu) ** 2).mean(-1, keepdims=True)
        h = (x - mu) * jax.lax.rsqrt(var + EPS) * norm_w + norm_b
        params = (in_w, conv_w, conv_b, xproj_w, dt_w, dt_b, A_log, D, out_w)
        fwd = _mamba(h, *params)
        bwd = jnp.flip(_mamba(jnp.flip(h, 1), *params), 1)
        return x + 0.5 * (fwd + bwd)

    def _L0_ffn_ref(hidden_states, g1, b1, g2, b2, Wr, br, Wq, bq, Wk, bk, Wv, bv, Wo, bo, Wm, bm, W1, bf1, W2, bf2):
        import jax, jax.numpy as jnp
        import numpy as np
        B, L, D, H, F = (4, 512, 192, 12, 768)
        ROUTE_FRAC = 0.15
        LN_EPS = 1e-05

        def _ln(x, g, b):
            m = jnp.mean(x, axis=-1, keepdims=True)
            v = jnp.mean((x - m) ** 2, axis=-1, keepdims=True)
            return (x - m) * jax.lax.rsqrt(v + LN_EPS) * g + b
        b, l, d = hidden_states.shape
        dh = d // H
        normed = _ln(hidden_states, g1, b1)
        scores = jax.nn.sigmoid(jnp.einsum('bld,d->bl', normed, Wr) + br)
        k = max(1, int(round(ROUTE_FRAC * l)))
        _, idx = jax.lax.top_k(-scores, k)
        attn_mask = jnp.zeros((b, l), bool).at[jnp.arange(b)[:, None], idx].set(True)
        q = (normed @ Wq + bq).reshape(b, l, H, dh)
        kk = (normed @ Wk + bk).reshape(b, l, H, dh)
        v = (normed @ Wv + bv).reshape(b, l, H, dh)
        logits = jnp.einsum('blhd,bmhd->bhlm', q, kk) / jnp.sqrt(jnp.float32(dh))
        probs = jax.nn.softmax(logits, axis=-1)
        ctx = jnp.einsum('bhlm,bmhd->blhd', probs, v).reshape(b, l, d)
        attn_out = ctx @ Wo + bo
        w = scores / (jnp.sum(scores, axis=1, keepdims=True) + 1e-06)
        pooled = jnp.einsum('bl,bld->bd', w, normed)
        mix_out = (normed + scores[..., None] * pooled[:, None, :]) @ Wm + bm
        merged = jnp.where(attn_mask[..., None], attn_out, mix_out)
        h = hidden_states + merged
        n2 = _ln(h, g2, b2)
        ffn = jax.nn.gelu(n2 @ W1 + bf1, approximate=False) @ W2 + bf2
        return h + ffn

    def _L1_attn_ref(x, w_qkv, w_proj, b_proj):
        import jax, jax.numpy as jnp
        import numpy as np
        HEADS = 12
        ROPE_THETA = 10000.0

        def _rope(t):
            B, H, N, D = t.shape
            inv_freq = 1.0 / ROPE_THETA ** (jnp.arange(0, D, 2, dtype=jnp.float32) / D)
            freqs = jnp.arange(N, dtype=jnp.float32)[:, None] * inv_freq[None, :]
            freqs = jnp.repeat(freqs, 2, axis=-1)
            cos, sin = (jnp.cos(freqs), jnp.sin(freqs))
            tp = t.reshape(B, H, N, D // 2, 2)
            rot = jnp.stack([-tp[..., 1], tp[..., 0]], axis=-1).reshape(B, H, N, D)
            return t * cos + rot * sin
        B, N, C = x.shape
        H = HEADS
        d = C // H
        scale = d ** (-0.5)
        qkv = x @ w_qkv.T
        q, k, v = jnp.split(qkv, 3, axis=-1)

        def to_heads(t):
            return t.reshape(B, N, H, d).transpose(0, 2, 1, 3)
        q, k, v = map(to_heads, (q, k, v))
        q = _rope(q * scale)
        k = _rope(k)
        attn = jnp.einsum('bhid,bhjd->bhij', q, k)
        attn = jax.nn.softmax(attn, axis=-1)
        out = jnp.einsum('bhij,bhjd->bhid', attn, v)
        out = out.transpose(0, 2, 1, 3).reshape(B, N, C)
        return out @ w_proj.T + b_proj

    def _L1_ffn_ref(x, gate_w, gate_b, W1, B1, W3, B3, W2, B2, Ws1, Bs1, Ws3, Bs3, Ws2, Bs2):
        import jax, jax.numpy as jnp
        import numpy as np
        B, S, D = (2, 256, 192)
        I = 96
        E = 8
        G = 4
        TOPK_GROUPS = 2
        K = 2
        ROUTE_SCALE = 1.0
        ALPHA, LIMIT = (1.702, 7.0)

        def swiglu(h):
            xg = jnp.minimum(h[..., ::2], LIMIT)
            xl = jnp.clip(h[..., 1::2], -LIMIT, LIMIT)
            return xg * jax.nn.sigmoid(ALPHA * xg) * (xl + 1.0)

        def gate(x, gate_w, gate_b):
            scores = jax.nn.softmax(jnp.einsum('td,ed->te', x, gate_w).astype(jnp.float32), axis=-1)
            original_scores = scores
            s = scores + gate_b
            T = x.shape[0]
            sg = s.reshape(T, G, E // G)
            group_scores = jnp.sum(jax.lax.top_k(sg, 2)[0], axis=-1)
            _, gidx = jax.lax.top_k(group_scores, TOPK_GROUPS)
            keep = jnp.any(jax.nn.one_hot(gidx, G, dtype=jnp.bool_), axis=1)
            sg = jnp.where(keep[:, :, None], sg, -jnp.inf)
            s = sg.reshape(T, E)
            _, idx = jax.lax.top_k(s, K)
            w = jnp.take_along_axis(original_scores, idx, axis=1) * ROUTE_SCALE
            return (w.astype(x.dtype), idx)

        def expert_ffn(x, W1, B1, W3, B3, W2, B2):
            h1 = jnp.einsum('td,edh->teh', x, W1) + B1
            h3 = jnp.einsum('td,edh->teh', x, W3) + B3
            g = swiglu(h1 * h3)
            return jnp.einsum('tei,eid->ted', g, W2) + B2

        def shared_ffn(x, Ws1, Bs1, Ws3, Bs3, Ws2, Bs2):
            h = (x @ Ws1 + Bs1) * (x @ Ws3 + Bs3)
            return swiglu(h) @ Ws2 + Bs2
        inp_shape = x.shape
        xt = x.reshape(-1, D)
        w, idx = gate(xt, gate_w, gate_b)
        combine = jnp.einsum('tk,tke->te', w, jax.nn.one_hot(idx, E, dtype=w.dtype))
        per_expert = expert_ffn(xt, W1, B1, W3, B3, W2, B2)
        routed = jnp.einsum('ted,te->td', per_expert, combine)
        out = routed + shared_ffn(xt, Ws1, Bs1, Ws3, Bs3, Ws2, Bs2)
        return out.reshape(inp_shape)
    h = _L0_tok_ref(x, L0_tok_stem_w, L0_tok_stem_b, L0_tok_bn1_g, L0_tok_bn1_b, L0_tok_bn1_m, L0_tok_bn1_v, L0_tok_off_w, L0_tok_off_b, L0_tok_dcn_w, L0_tok_dcn_b, L0_tok_bn2_g, L0_tok_bn2_b, L0_tok_bn2_m, L0_tok_bn2_v)
    h = h + _L0_attn_ref(_layernorm(h, axis=-1), L0_attn_norm_w, L0_attn_norm_b, L0_attn_in_w, L0_attn_conv_w, L0_attn_conv_b, L0_attn_xproj_w, L0_attn_dt_w, L0_attn_dt_b, L0_attn_A_log, L0_attn_D, L0_attn_out_w)
    h = h + _L0_ffn_ref(_layernorm(h, axis=-1), L0_ffn_g1, L0_ffn_b1, L0_ffn_g2, L0_ffn_b2, L0_ffn_Wr, L0_ffn_br, L0_ffn_Wq, L0_ffn_bq, L0_ffn_Wk, L0_ffn_bk, L0_ffn_Wv, L0_ffn_bv, L0_ffn_Wo, L0_ffn_bo, L0_ffn_Wm, L0_ffn_bm, L0_ffn_W1, L0_ffn_bf1, L0_ffn_W2, L0_ffn_bf2)
    h = h + _L1_attn_ref(_layernorm(h, axis=-1), L1_attn_w_qkv, L1_attn_w_proj, L1_attn_b_proj)
    h = h + _L1_ffn_ref(_layernorm(h, axis=-1), L1_ffn_gate_w, L1_ffn_gate_b, L1_ffn_W1, L1_ffn_B1, L1_ffn_W3, L1_ffn_B3, L1_ffn_W2, L1_ffn_B2, L1_ffn_Ws1, L1_ffn_Bs1, L1_ffn_Ws3, L1_ffn_Bs3, L1_ffn_Ws2, L1_ffn_Bs2)
    return h

_drawn_inputs = setup_inputs


def setup_inputs(seed=0):
    import zlib

    import numpy as np

    out = dict(_drawn_inputs(seed))
    spreads = {'L0_attn_norm_w': (1.0, 0.2),
     'L0_attn_norm_b': (0.0, 0.1),
     'L0_attn_conv_b': (0.0, 0.1),
     'L0_attn_D': (1.0, 0.2),
     'L0_ffn_g1': (1.0, 0.2),
     'L0_ffn_b1': (0.0, 0.567),
     'L0_ffn_g2': (1.0, 0.6),
     'L0_ffn_b2': (0.0, 0.8),
     'L0_ffn_bq': (0.0, 0.8),
     'L0_ffn_bk': (0.0, 2.0),
     'L0_ffn_bv': (0.0, 0.8),
     'L0_ffn_bo': (0.0, 0.576),
     'L0_ffn_bm': (0.0, 0.1),
     'L0_ffn_bf1': (0.0, 0.683),
     'L0_ffn_bf2': (0.0, 0.1),
     'L1_attn_b_proj': (0.0, 0.1)}
    factors = {'L0_ffn_Wq': 8.0,
     'L0_ffn_Wk': 8.0,
     'L0_ffn_Wv': 7.544,
     'L0_ffn_Wo': 7.265,
     'L1_ffn_gate_w': 8.0,
     'L1_ffn_gate_b': 8.0,
     'L1_ffn_W1': 8.0,
     'L1_ffn_B1': 8.0,
     'L1_ffn_W3': 8.0,
     'L1_ffn_B3': 8.0,
     'L1_ffn_W2': 8.0,
     'L1_ffn_B2': 64.0,
     'L1_ffn_Ws1': 8.0,
     'L1_ffn_Bs1': 8.0,
     'L1_ffn_Ws3': 8.0,
     'L1_ffn_Bs3': 8.0,
     'L1_ffn_Ws2': 8.0,
     'L1_ffn_Bs2': 50.642}
    for name, (base, spread) in spreads.items():
        noise = np.random.default_rng([zlib.crc32(name.encode()), seed]).standard_normal(out[name].shape)
        drawn = base * np.exp(spread * noise) if base else spread * noise
        out[name] = jnp.asarray(drawn.astype(out[name].dtype))
    for name, factor in factors.items():
        out[name] = (out[name] * factor).astype(out[name].dtype)
    return out
```

```python
from contextlib import ExitStack

import concourse.bass as bass
from concourse import mybir
import numpy as np

F32 = mybir.dt.float32
ALU = mybir.AluOpType
ACT = mybir.ActivationFunctionType
AX_X = mybir.AxisListType.X
ds = bass.ds

IMGS = 64
IN_CH, IN_SIDE = 3, 96
KS = 4
SIDE1 = IN_SIDE // KS
PIX = SIDE1 * SIDE1
CH1 = 96
SIDE2 = SIDE1 // KS
POS = SIDE2 * SIDE2
TAPS = KS * KS
D = 192
DH = D // 2
TOK = IMGS * POS
P = 128
TILES = TOK // P
EPS = 1e-5
SLOPE = 0.01

STEM_K = IN_CH * TAPS + 1
GRP = 4
GRPS = IMGS // GRP
ROWS_K = 5
PT = ROWS_K * SIDE1
KT = -(-SIDE1 // ROWS_K)
PT_LAST = (SIDE1 - (KT - 1) * ROWS_K) * SIDE1
SMP = TAPS * POS
HALF_SMP = SMP // 2
OFF_CH = 2 * TAPS
GPIX = GRP * PIX
GPOS = GRP * POS
CP_COLS = 384
CP_PIECES = GPIX // CP_COLS

N_STATE = 16
D_INNER = 2 * D
DT = D_INNER // P
DT_RANK = -(-D // 16)
XP = DT_RANK + 2 * N_STATE
CH_IMGS = 16
CHUNKS = IMGS // CH_IMGS
CT = CH_IMGS * POS
HC = CT // 2
COLS = 384
PIECES = TOK // COLS
FAR = 1e30
CLAMP = 20.0

HEADS = 12
HD = D // HEADS
HH = HEADS // 2
H3 = 3
PAIRS = IMGS // 2
PAIR = 2 * POS
ROW_B = 64
PROWS = ROW_B + POS
K3 = H3 * POS
GS = HEADS // H3
KEEP = max(1, round(0.15 * POS))
PAD = 4
FFN = 4 * D
FT = FFN // P
RP = 8 * POS
RPIECES = TOK // RP
EXPERTS, TOPK, GROUPS, TOPK_GROUPS = 8, 2, 4, 2
INTER = 96
EG = 4
HT = EG * INTER // P
QT = EXPERTS // EG * HT
EP = 2 * P
EPIECES = TOK // EP
ALPHA, LIMIT = 1.702, 7.0
OUT_OF = 1e30



class Mem:

    def __init__(self, nc, ctx, tag):
        self.nc, self.ctx, self.tag, self.sems = nc, ctx, tag, []
        ctx.callback(self.clear)

    def clear(self):
        self.nc.clear_and_free_semaphores(self.sems)
        self.nc.all_engine_barrier()

    def sb(self, name, shape, dt=F32):
        return self.ctx.enter_context(self.nc.sbuf_tensor(f"{self.tag}_{name}", shape, dt))

    def ps(self, name, shape, dt=F32):
        return self.ctx.enter_context(self.nc.psum_tensor(f"{self.tag}_{name}", shape, dt))

    def sem(self, name):
        self.sems.append(self.nc.alloc_semaphore(name=f"{self.tag}_{name}"))
        return self.sems[-1]


def tokenizer(nc, A, featD, offD):
    with ExitStack() as ctx:
        m = Mem(nc, ctx, "tok")
        w_stem = m.sb("w_stem", [STEM_K, CH1])
        bn_rows = m.sb("bn_rows", [STEM_K, 5, CH1])
        bn_inv = m.sb("bn_inv", [STEM_K, CH1])
        bn_tmp = m.sb("bn_tmp", [STEM_K, CH1])
        w_off = m.sb("w_off", [CH1, TAPS, OFF_CH])
        b_off = m.sb("b_off", [OFF_CH, 1])
        grid = m.sb("grid", [OFF_CH, POS])
        w_dcn = m.sb("w_dcn", [CH1, TAPS, D])
        bn2 = m.sb("bn2", [DH, 5, 2])
        bn2_inv = m.sb("bn2_inv", [DH, 2])
        bn2_tmp = m.sb("bn2_tmp", [DH, 2])
        bn2_add = m.sb("bn2_add", [DH, 2])
        pix_xy = m.sb("pix_xy", [PT, 1 + KT])
        patches = [m.sb(f"patches{u}", [STEM_K, GPIX + PT - PT_LAST]) for u in range(2)]
        cp_tmp = [m.sb(f"cp_tmp{u}", [CH1, CP_COLS]) for u in range(2)]
        stem_cp = m.sb("stem_cp", [CH1, GPIX])
        coords = m.sb("coords", [OFF_CH, GRP, POS])
        coords_b = [m.sb(f"coords_b{u}", [PT, GRP, 2, SMP]) for u in range(2)]
        hat_x = [m.sb(f"hat_x{u}", [PT, GRP, SMP]) for u in range(2)]
        hat_y = [m.sb(f"hat_y{u}", [PT, KT, SMP]) for u in range(2)]
        wts = [m.sb(f"wts{u}", [PT, KT, SMP]) for u in range(2)]
        pt_tmp = [m.sb(f"pt_tmp{u}", [PT, KT, CH1]) for u in range(2)]
        stem_pt = [m.sb(f"stem_pt{u}", [PT, KT, CH1]) for u in range(2)]
        sampled = [m.sb(f"sampled{u}", [CH1, TAPS, GRP, POS]) for u in range(2)]
        dcn_tmp = m.sb("dcn_tmp", [DH, 2, GPOS])
        dcn_out = [m.sb(f"dcn_out{u}", [DH, 2, GPOS]) for u in range(2)]
        ps_cp = [m.ps(f"ps_cp{u}", [CH1, 512]) for u in range(2)]
        ps_off = m.ps("ps_off", [OFF_CH, 512])
        ps_pt = [m.ps(f"ps_pt{u}", [PT, 512]) for u in range(2)]
        ps_smp = [m.ps(f"ps_smp{u}", [CH1, 512]) for u in range(2)]
        ps_dcn = m.ps("ps_dcn", [DH, 512])

        w_loaded = m.sem("w_loaded")
        var_ready = m.sem("var_ready")
        std_ready = m.sem("std_ready")
        fold = m.sem("fold")
        bias_row = m.sem("bias_row")
        patches_in = [m.sem(f"patches_in{u}") for u in range(2)]
        cp_mm, cp_copied, cp_done = m.sem("cp_mm"), m.sem("cp_copied"), m.sem("cp_done")
        off_mm, off_done, off_stored = m.sem("off_mm"), m.sem("off_done"), m.sem("off_stored")
        coords_in = [m.sem(f"coords_in{u}") for u in range(2)]
        absx_done, hatx_done = m.sem("absx_done"), m.sem("hatx_done")
        coords_used = m.sem("coords_used")
        absy_done, haty_done, wts_done = m.sem("absy_done"), m.sem("haty_done"), m.sem("wts_done")
        pt_mm, pt_copied, pt_done = m.sem("pt_mm"), m.sem("pt_copied"), m.sem("pt_done")
        smp_mm, smp_copied = m.sem("smp_mm"), m.sem("smp_copied")
        dcn_mm, dcn_copied, dcn_done = m.sem("dcn_mm"), m.sem("dcn_copied"), m.sem("dcn_done")
        feat_out = [m.sem(f"feat_out{u}") for u in range(2)]
        pad_set, coords_free = m.sem("pad_set"), m.sem("coords_free")
        SMALL_LOADS = 16 * 17

        block = ctx.enter_context(nc.Block())

        @block.sync
        def _(sp):
            for dst, src in ((w_stem[0:STEM_K - 1, :], A["stem_w"]), (w_off[:], A["off_w"]),
                             (b_off[:], A["off_b"]), (grid[:], A["grid"]), (w_dcn[:], A["dcn_w"]),
                             (pix_xy[:], A["pix_xy"])):
                sp.dma_start(dst, src).then_inc(w_loaded, 16)
            for k, name in enumerate(("bn1_g", "bn1_b", "bn1_m", "bn1_v", "stem_b")):
                sp.dma_start(bn_rows[:, k, :], A[name].partition_broadcast(STEM_K)).then_inc(w_loaded, 16)
            for k, name in enumerate(("bn2_g", "bn2_b", "bn2_m", "bn2_v", "dcn_b")):
                sp.dma_start(bn2[:, k, :], A[name]).then_inc(w_loaded, 16)
            sp.dma_start(patches[0][STEM_K - 1:STEM_K, :], A["ones"]).then_inc(w_loaded, 16)
            sp.wait_ge(fold, 4)
            sp.dma_start(w_stem[STEM_K - 1:STEM_K, :], bn_tmp[0:1, :]).then_inc(bias_row, 16)

            def exchange(g, u):
                sp.wait_ge(off_done, g + 1)
                sp.dma_start(offD[ds(g * GRP, GRP)].rearrange("i c p -> c i p"), coords[:]).then_inc(off_stored, 16)
                sp.wait_ge(off_stored, 16 * (g + 1))
                sp.dma_start(coords_b[u][:].rearrange("p i y s -> p (i y s)"),
                             offD[ds(g * GRP, GRP)].rearrange("i c p -> (i c p)").partition_broadcast(PT)
                             ).then_inc(coords_in[u], 16)

            def store(g, u):
                sp.wait_ge(dcn_done, g + 2)
                sp.dma_start(featD.rearrange("h c t -> c h t")[:, :, ds(g * GPOS, GPOS)], dcn_out[u][:]
                             ).then_inc(feat_out[u], 16)

            exchange(0, 0)
            exchange(1, 1)
            with sp.Fori(1, GRPS // 2) as i:
                for u in range(2):
                    sp.wait_ge(coords_used, 2 * i + u - 1)
                    sp.sem_inc(coords_free, 1)
                    exchange(2 * i + u, u)
                    store(2 * i + u - 2, u)
            for u in range(2):
                store(GRPS - 2 + u, u)
            for u in range(2):
                sp.wait_ge(feat_out[u], 16 * (GRPS // 2 + 1))

        @block.gpsimd
        def _(pool):
            def load(g, u):
                pool.dma_start(patches[u][0:STEM_K - 1, 0:GPIX], A["patches"][:, ds(g * GPIX, GPIX)]
                               ).then_inc(patches_in[u], 16)

            for u in range(2):
                pool.memset(patches[u][0:STEM_K - 1, GPIX:], 0.0).then_inc(pad_set, 1)
            pool.dma_start(patches[1][STEM_K - 1:STEM_K, :], A["ones"]).then_inc(patches_in[1], 16)
            load(0, 0)
            load(1, 1)
            with pool.Fori(1, GRPS // 2) as i:
                for u in range(2):
                    pool.wait_ge(pt_mm, GRP * (2 * i + u - 1))
                    load(2 * i + u, u)

        @block.tensor
        def _(pe):
            def stem_cp_mm(g, u, i):
                pe.wait_ge(patches_in[u], 16 * (i + 1 + u))
                for q in range(CP_PIECES):
                    if q >= 2 or not isinstance(g, int) or g > 0:
                        pe.wait_ge(cp_copied, CP_PIECES * g + q - 1)
                    pe.matmul(ps_cp[q % 2][:, 0:CP_COLS], w_stem[:], patches[u][:, q * CP_COLS:(q + 1) * CP_COLS],
                              start=True, stop=True).then_inc(cp_mm, 1)

            def off_mm_(g):
                pe.wait_ge(cp_done, CP_PIECES * (g + 1))
                if not isinstance(g, int) or g > 0:
                    pe.wait_ge(off_done, g)
                px = stem_cp[:].rearrange("c (r ky q kx) -> c r ky q kx", ky=KS, kx=KS, q=SIDE2)
                for t in range(TAPS):
                    last = pe.matmul(ps_off[:, 0:GPOS], w_off[:, t, :], px[:, :, t // KS, :, t % KS],
                                     start=t == 0, stop=t == TAPS - 1)
                last.then_inc(off_mm, 1)

            def stem_pt_mm(g, u, j, first=False):
                n = GRP * g + j
                if not first:
                    if not isinstance(g, int) or n >= 2:
                        pe.wait_ge(pt_copied, n - 1)
                pe.wait_ge(patches_in[u], 16 * (g // 2 + 1 + u) if isinstance(g, int) else 16 * (cur[0] + 1 + u))
                for k in range(KT):
                    at = j * PIX + k * PT
                    last = pe.matmul(ps_pt[j % 2][:, k * CH1:(k + 1) * CH1], patches[u][:, at:at + PT], w_stem[:],
                                     start=True, stop=True)
                last.then_inc(pt_mm, 1)

            def sample_mm(g, u, j):
                n = GRP * g + j
                pe.wait_ge(pt_done, n + 1)
                pe.wait_ge(wts_done, n + 1)
                for h in range(2):
                    if not isinstance(n, int) or n > 0:
                        pe.wait_ge(smp_copied, 2 * n + h - 1)
                    for k in range(KT):
                        rows = PT if k < KT - 1 else PT_LAST
                        last = pe.matmul(ps_smp[h][:, 0:HALF_SMP], stem_pt[j % 2][0:rows, k, :],
                                         wts[j % 2][0:rows, k, h * HALF_SMP:(h + 1) * HALF_SMP],
                                         start=k == 0, stop=k == KT - 1)
                    last.then_inc(smp_mm, 1)

            def dcn_half(g, u, h):
                if h == 0:
                    pe.wait_ge(smp_copied, 2 * GRP * (g + 1))
                    pe.wait_ge(dcn_copied, g + 1)
                for t in range(TAPS):
                    last = pe.matmul(ps_dcn[:, h * GPOS:(h + 1) * GPOS], w_dcn[:, t, h * DH:(h + 1) * DH],
                                     sampled[u][:, t, :, :], start=t == 0, stop=t == TAPS - 1)
                if h == 1:
                    last.then_inc(dcn_mm, 1)

            cur = [0]

            def step(g, u, j, nxt, front, dcn):
                half = (g // 2 if isinstance(g, int) else cur[0])
                if nxt:
                    g2, u2, j2 = (g, u, j + 1) if j < GRP - 1 else (g + 1, 1 - u, 0)
                    cur[0] = half if j < GRP - 1 else half + u
                    stem_pt_mm(g2, u2, j2)
                    cur[0] = half
                if front and j == 0:
                    stem_cp_mm(g + 1, 1 - u, half + u)
                if front and j == 1:
                    off_mm_(g + 1)
                if dcn and j >= GRP - 2:
                    dcn_half(g - 1, 1 - u, j - (GRP - 2))
                sample_mm(g, u, j)

            def rest(g, u, more, i, dcn=True):
                cur[0] = i
                for j in range(1, GRP):
                    step(g, u, j, True, j == 1, dcn)
                cur[0] = i + u
                step(g + 1, 1 - u, 0, True, more, False)

            pe.sem_inc(dcn_mm, 1)
            pe.wait_ge(w_loaded, SMALL_LOADS)
            pe.wait_ge(bias_row, 16)
            pe.wait_ge(fold, 6)
            pe.wait_ge(pad_set, 2)
            stem_cp_mm(0, 0, 0)
            stem_pt_mm(0, 0, 0, True)
            off_mm_(0)
            step(0, 0, 0, True, True, False)
            rest(0, 0, True, 0, False)
            rest(1, 1, True, 0)
            with pe.Fori(1, GRPS // 2 - 1) as i:
                rest(2 * i, 0, True, i)
                rest(2 * i + 1, 1, True, i)
            rest(GRPS - 2, 0, False, GRPS // 2 - 1)
            for j in range(1, GRP):
                step(GRPS - 1, 1, j, j < GRP - 1, False, True)
            for h in range(2):
                dcn_half(GRPS - 1, 1, h)

        @block.scalar
        def _(act):
            def cp_copy(g):
                for q in range(CP_PIECES):
                    act.wait_ge(cp_mm, CP_PIECES * g + q + 1)
                    if q >= 2 or not isinstance(g, int) or g > 0:
                        act.wait_ge(cp_done, CP_PIECES * g + q - 1)
                    act.activation(cp_tmp[q % 2][:], ps_cp[q % 2][:, 0:CP_COLS], ACT.Copy).then_inc(cp_copied, 1)

            def pt_copy(g, j):
                n = GRP * g + j
                act.wait_ge(pt_mm, n + 1)
                if not isinstance(n, int) or n >= 2:
                    act.wait_ge(pt_done, n - 1)
                act.activation(pt_tmp[j % 2][:].rearrange("p k c -> p (k c)"), ps_pt[j % 2][:, 0:KT * CH1], ACT.Copy
                               ).then_inc(pt_copied, 1)

            def abs_x(g, u, i):
                act.wait_ge(coords_in[u], 16 * (i + 1))
                if not isinstance(g, int) or g >= 2:
                    act.wait_ge(wts_done, GRP * (g - 1))
                act.activation(hat_x[u][:], coords_b[u][:, :, 1, :], ACT.Abs, bias=pix_xy[:, 0:1]).then_inc(absx_done, 1)

            def abs_y(g, u, j):
                n = GRP * g + j
                if not isinstance(n, int) or n >= 2:
                    act.wait_ge(wts_done, n - 1)
                for k in range(KT):
                    last = act.activation(hat_y[j % 2][:, k, :], coords_b[u][:, j, 0, :], ACT.Abs,
                                          bias=pix_xy[:, 1 + k:2 + k])
                last.then_inc(absy_done if j < GRP - 1 else coords_used, 1)

            def smp_copy(g, u, j):
                n = GRP * g + j
                if j == 0 and (not isinstance(g, int) or g >= 2):
                    act.wait_ge(dcn_mm, g)
                for h in range(2):
                    act.wait_ge(smp_mm, 2 * n + h + 1)
                    act.activation(sampled[u][:, h * TAPS // 2:(h + 1) * TAPS // 2, j, :],
                                   ps_smp[h][:, 0:HALF_SMP].rearrange("c (t q) -> c t q", q=POS), ACT.Copy
                                   ).then_inc(smp_copied, 1)

            def dcn_copy(g):
                act.wait_ge(dcn_mm, g + 2)
                act.wait_ge(dcn_done, g + 1)
                for h in range(2):
                    last = act.activation(dcn_tmp[:, h, :], ps_dcn[:, h * GPOS:(h + 1) * GPOS], ACT.Identity,
                                          scale=bn2_inv[:, h:h + 1], bias=bn2_add[:, h:h + 1])
                last.then_inc(dcn_copied, 1)

            def step(g, u, j, nxt, front, dcn, i):
                if nxt:
                    g2, u2, j2 = (g, u, j + 1) if j < GRP - 1 else (g + 1, 1 - u, 0)
                    pt_copy(g2, j2)
                if front and j == 0:
                    cp_copy(g + 1)
                if nxt:
                    if j2 == 0:
                        abs_x(g2, u2, i + u)
                    abs_y(g2, u2, j2)
                smp_copy(g, u, j)
                if dcn and j == GRP - 1:
                    dcn_copy(g - 1)

            def rest(g, u, more, i, dcn=True):
                for j in range(1, GRP):
                    step(g, u, j, True, j == 1, dcn, i)
                step(g + 1, 1 - u, 0, True, more, False, i + u)

            act.sem_inc(dcn_copied, 1)
            act.wait_ge(w_loaded, SMALL_LOADS)
            act.wait_ge(var_ready, 2)
            act.activation(bn_inv[:], bn_tmp[:], ACT.Sqrt).then_inc(std_ready, 1)
            act.activation(bn2_inv[:], bn2_tmp[:], ACT.Sqrt).then_inc(std_ready, 1)
            act.wait_ge(fold, 7)
            cp_copy(0)
            pt_copy(0, 0)
            abs_x(0, 0, 0)
            abs_y(0, 0, 0)
            step(0, 0, 0, True, True, False, 0)
            rest(0, 0, True, 0, False)
            rest(1, 1, True, 0)
            with act.Fori(1, GRPS // 2 - 1) as i:
                rest(2 * i, 0, True, i)
                rest(2 * i + 1, 1, True, i)
            rest(GRPS - 2, 0, False, GRPS // 2 - 1)
            for j in range(1, GRP):
                step(GRPS - 1, 1, j, j < GRP - 1, False, True, GRPS // 2 - 1)
            dcn_copy(GRPS - 1)

        @block.vector
        def _(dve):
            def leaky(out, x):
                return dve.scalar_tensor_tensor(out=out, in0=x, scalar=SLOPE, in1=x, op0=ALU.mult, op1=ALU.max)

            def cp_leaky(g):
                if not isinstance(g, int) or g > 0:
                    dve.wait_ge(off_mm, g)
                for q in range(CP_PIECES):
                    dve.wait_ge(cp_copied, CP_PIECES * g + q + 1)
                    leaky(stem_cp[:, q * CP_COLS:(q + 1) * CP_COLS], cp_tmp[q % 2][:]).then_inc(cp_done, 1)

            def off_add(g):
                dve.wait_ge(off_mm, g + 1)
                if not isinstance(g, int) or g > 0:
                    dve.wait_ge(off_stored, 16 * g)
                dve.scalar_tensor_tensor(out=coords[:], in0=ps_off[:, 0:GPOS].rearrange("c (i q) -> c i q", q=POS),
                                         scalar=b_off[:, 0:1], in1=grid[:].unsqueeze(1).to_broadcast([OFF_CH, GRP, POS]),
                                         op0=ALU.add, op1=ALU.add).then_inc(off_done, 1)

            def pt_leaky(g, j):
                n = GRP * g + j
                dve.wait_ge(pt_copied, n + 1)
                if not isinstance(n, int) or n >= 2:
                    dve.wait_ge(smp_mm, 2 * (n - 1))
                leaky(stem_pt[j % 2][:], pt_tmp[j % 2][:]).then_inc(pt_done, 1)

            def hat_x_(g, u):
                dve.wait_ge(absx_done, g + 1)
                dve.tensor_scalar(hat_x[u][:], hat_x[u][:], 1.0, 1.0, ALU.min, ALU.subtract).then_inc(hatx_done, 1)

            def weights(g, u, j):
                n = GRP * g + j
                if j < GRP - 1:
                    dve.wait_ge(absy_done, (GRP - 1) * g + j + 1)
                else:
                    dve.wait_ge(coords_used, g + 1)
                dve.tensor_scalar(hat_y[j % 2][:], hat_y[j % 2][:], 1.0, 1.0, ALU.min, ALU.subtract).then_inc(haty_done, 1)
                dve.wait_ge(haty_done, n + 1)
                dve.wait_ge(hatx_done, g + 1)
                if not isinstance(n, int) or n >= 2:
                    dve.wait_ge(smp_mm, 2 * (n - 1))
                dve.tensor_tensor(wts[j % 2][:], hat_y[j % 2][:],
                                  hat_x[u][:, j, :].unsqueeze(1).to_broadcast([PT, KT, SMP]), ALU.mult).then_inc(wts_done, 1)

            def dcn_leaky(g, u, i):
                dve.wait_ge(dcn_copied, g + 2)
                if not isinstance(g, int) or g >= 2:
                    dve.wait_ge(feat_out[u], 16 * (i + 1))
                leaky(dcn_out[u][:], dcn_tmp[:]).then_inc(dcn_done, 1)

            def step(g, u, j, nxt, front, dcn, i):
                if nxt:
                    g2, u2, j2 = (g, u, j + 1) if j < GRP - 1 else (g + 1, 1 - u, 0)
                    pt_leaky(g2, j2)
                if front and j == 0:
                    cp_leaky(g + 1)
                if front and j == 1:
                    off_add(g + 1)
                if nxt:
                    if j2 == 0:
                        hat_x_(g2, u2)
                    weights(g2, u2, j2)
                if dcn and j == GRP - 1:
                    dcn_leaky(g - 1, 1 - u, i - 1 + u)

            def rest(g, u, more, i, dcn=True):
                for j in range(1, GRP):
                    step(g, u, j, True, j == 1, dcn, i)
                step(g + 1, 1 - u, 0, True, more, False, i + u)

            dve.sem_inc(dcn_done, 1)
            for u in range(2):
                dve.sem_inc(feat_out[u], 16)
            dve.wait_ge(w_loaded, SMALL_LOADS)
            dve.tensor_scalar(bn_tmp[:], bn_rows[:, 3, :], EPS, None, ALU.add).then_inc(var_ready, 1)
            dve.tensor_scalar(bn2_tmp[:], bn2[:, 3, :], EPS, None, ALU.add).then_inc(var_ready, 1)
            dve.wait_ge(std_ready, 2)
            dve.reciprocal(bn_tmp[:], bn_inv[:]).then_inc(fold, 1)
            dve.wait_ge(fold, 1)
            dve.tensor_tensor(bn_inv[:], bn_tmp[:], bn_rows[:, 0, :], ALU.mult).then_inc(fold, 1)
            dve.wait_ge(fold, 2)
            dve.tensor_tensor(bn_tmp[:], bn_rows[:, 4, :], bn_rows[:, 2, :], ALU.subtract).then_inc(var_ready, 1)
            dve.wait_ge(var_ready, 3)
            dve.tensor_tensor(bn_tmp[:], bn_tmp[:], bn_inv[:], ALU.mult).then_inc(fold, 1)
            dve.wait_ge(fold, 3)
            dve.tensor_tensor(bn_tmp[:], bn_tmp[:], bn_rows[:, 1, :], ALU.add).then_inc(fold, 1)
            dve.tensor_tensor(w_stem[0:STEM_K - 1, :], w_stem[0:STEM_K - 1, :], bn_inv[0:STEM_K - 1, :], ALU.mult
                              ).then_inc(fold, 1)
            dve.reciprocal(bn2_tmp[:], bn2_inv[:]).then_inc(var_ready, 1)
            dve.wait_ge(var_ready, 4)
            dve.tensor_tensor(bn2_inv[:], bn2_tmp[:], bn2[:, 0, :], ALU.mult).then_inc(fold, 1)
            dve.tensor_tensor(bn2_add[:], bn2[:, 4, :], bn2[:, 2, :], ALU.subtract).then_inc(var_ready, 1)
            dve.wait_ge(fold, 6)
            dve.wait_ge(var_ready, 5)
            dve.tensor_tensor(bn2_add[:], bn2_add[:], bn2_inv[:], ALU.mult).then_inc(var_ready, 1)
            dve.wait_ge(var_ready, 6)
            dve.tensor_tensor(bn2_add[:], bn2_add[:], bn2[:, 1, :], ALU.add).then_inc(fold, 1)
            cp_leaky(0)
            pt_leaky(0, 0)
            off_add(0)
            hat_x_(0, 0)
            weights(0, 0, 0)
            step(0, 0, 0, True, True, False, 0)
            rest(0, 0, True, 0, False)
            rest(1, 1, True, 0)
            with dve.Fori(1, GRPS // 2 - 1) as i:
                rest(2 * i, 0, True, i)
                rest(2 * i + 1, 1, True, i)
            rest(GRPS - 2, 0, False, GRPS // 2 - 1)
            for j in range(1, GRP):
                step(GRPS - 1, 1, j, j < GRP - 1, False, True, GRPS // 2 - 1)
            dcn_leaky(GRPS - 1, 1, GRPS // 2 - 1)



def layer_norm(nc, tag, ident, src, featT, x1=None, add_to=None, affine=None, twice=False):
    with ExitStack() as ctx:
        m = Mem(nc, ctx, tag)
        stats = m.sb("stats", [P, TILES, 6])
        mv = m.sb("mv", [P, TILES, 2])
        ve, sd, r1 = (m.sb(n, [P, TILES]) for n in ("ve", "sd", "r1"))
        v2, sd2, r2 = (m.sb(n, [P, TILES]) for n in ("v2", "sd2", "r2"))
        x1 = x1 if x1 is not None else m.sb("x1", [P, TILES, D])
        x2 = m.sb("x2", [P, TILES, D]) if twice else x1
        gb = m.sb("gb", [DH, 2, 2])
        QUADS = -(-TILES // 4)
        ps_t = [m.ps(f"ps_t{u}", [DH, 512]) for u in range(4)]
        stat, link, var_in, sd_out = m.sem("stat"), m.sem("link"), m.sem("var_in"), m.sem("sd_out")
        gb_in, normed, turned = m.sem("gb_in"), m.sem("normed"), m.sem("turned")
        copied = [m.sem(f"copied{h}") for h in range(2)]
        x1_done, added = m.sem("x1_done"), m.sem("added")
        block = ctx.enter_context(nc.Block())

        @block.sync
        def _(sp):
            if affine:
                for k in range(2):
                    sp.dma_start(gb[:, k, :], affine[k]).then_inc(gb_in, 16)
                sp.wait_ge(gb_in, 32)

        @block.gpsimd
        def _(pool):
            if add_to is not None:
                if twice:
                    pool.wait_ge(x1_done, TILES)
                pool.wait_ge(normed, TILES)
                pool.tensor_tensor(add_to[:], add_to[:], x1[:], ALU.add).then_inc(added, 1)

        @block.scalar
        def _(act):
            act.wait_ge(var_in, 1)
            act.activation(sd[:], ve[:], ACT.Sqrt).then_inc(sd_out, 1)
            if twice:
                act.wait_ge(var_in, 2)
                act.activation(sd2[:], v2[:], ACT.Sqrt).then_inc(sd_out, 1)
            if affine:
                act.wait_ge(gb_in, 32)
            for q in range(QUADS):
                w = min(4, TILES - 4 * q) * P
                act.wait_ge(turned, 2 * q + 1)
                o, i = featT[:, 0, 4 * q * P:4 * q * P + w], ps_t[(2 * q) % 4][:, 0:w]
                if affine:
                    act.activation(o, i, ACT.Identity, scale=gb[:, 0, 0:1], bias=gb[:, 1, 0:1]).then_inc(copied[0], 1)
                else:
                    act.activation(o, i, ACT.Copy).then_inc(copied[0], 1)

        @block.tensor
        def _(pe):
            for q in range(QUADS):
                n = min(4, TILES - 4 * q)
                pe.wait_ge(normed, 4 * q + n)
                for h in range(2):
                    if q >= 2:
                        pe.wait_ge(copied[h], q - 1)
                    for k in range(n):
                        last = pe.transpose(ps_t[(2 * q + h) % 4][:, k * P:(k + 1) * P],
                                            x2[:, 4 * q + k, h * DH:(h + 1) * DH], ident[:])
                    last.then_inc(turned, 1)

        @block.vector
        def _(dve):
            n_link = [0]

            def linked(ins):
                n_link[0] += 1
                ins.then_inc(link, 1)
                dve.wait_ge(link, n_link[0])

            for t in range(TILES):
                dve.bn_stats(stats[:, t, :], src[:, t, :]).then_inc(stat, 1)
            for t in range(TILES):
                dve.wait_ge(stat, t + 1)
                dve.bn_aggr(mv[:, t, :], stats[:, t, :]).then_inc(stat, 1)
            dve.wait_ge(stat, 2 * TILES)
            dve.tensor_scalar(ve[:], mv[:, :, 1], EPS, None, ALU.add).then_inc(var_in, 1)
            dve.wait_ge(sd_out, 1)
            linked(dve.reciprocal(r1[:], sd[:]))
            if twice:
                linked(dve.reciprocal(v2[:], ve[:]))
                linked(dve.tensor_tensor(v2[:], v2[:], mv[:, :, 1], ALU.mult))
                n_link[0] += 1
                dve.tensor_scalar(sd2[:], v2[:], EPS, None, ALU.add).then_inc(link, 1)
                dve.wait_ge(link, n_link[0])
                dve.tensor_copy(v2[:], sd2[:]).then_inc(var_in, 1)
                dve.wait_ge(sd_out, 2)
                linked(dve.reciprocal(r2[:], sd2[:]))
                linked(dve.tensor_tensor(r2[:], r2[:], r1[:], ALU.mult))
            for t in range(TILES):
                ins = dve.tensor_scalar(x1[:, t, :], src[:, t, :], mv[:, t, 0:1], r1[:, t:t + 1],
                                        ALU.subtract, ALU.mult)
                if twice:
                    ins.then_inc(x1_done, 1)
                    dve.tensor_scalar(x2[:, t, :], src[:, t, :], mv[:, t, 0:1], r2[:, t:t + 1],
                                      ALU.subtract, ALU.mult).then_inc(normed, 1)
                else:
                    ins.then_inc(normed, 1)
            if affine:
                dve.wait_ge(gb_in, 32)
            for q in range(QUADS):
                w = min(4, TILES - 4 * q) * P
                dve.wait_ge(turned, 2 * q + 2)
                o, i = featT[:, 1, 4 * q * P:4 * q * P + w], ps_t[(2 * q + 1) % 4][:, 0:w]
                if affine:
                    dve.tensor_scalar(o, i, gb[:, 0, 1:2], gb[:, 1, 1:2], ALU.mult, ALU.add).then_inc(copied[1], 1)
                else:
                    dve.tensor_copy(o, i).then_inc(copied[1], 1)


def in_projection(nc, A, featT, u_pre, z_gate):
    with ExitStack() as ctx:
        m = Mem(nc, ctx, "inp")
        w = m.sb("w", [DH, 2, 2 * D_INNER])
        ps = [m.ps(f"ps{k}", [P, 512]) for k in range(2 * DT)]
        w_in = m.sem("w_in")
        mm = m.sem("mm")
        u_copied, z_copied = m.sem("u_copied"), m.sem("z_copied")
        block = ctx.enter_context(nc.Block())

        @block.sync
        def _(sp):
            sp.dma_start(w[:], A["in_w"]).then_inc(w_in, 16)

        @block.tensor
        def _(pe):
            pe.wait_ge(w_in, 16)
            with pe.Fori(0, PIECES) as c:
                for k in range(2 * DT):
                    pe.wait_ge(u_copied if k < DT else z_copied, DT * c + k % DT + 1)
                    for h in range(2):
                        last = pe.matmul(ps[k][:, 0:COLS], w[:, h, k * P:(k + 1) * P], featT[:, h, ds(c * COLS, COLS)],
                                         start=h == 0, stop=h == 1)
                    last.then_inc(mm, 1)

        @block.scalar
        def _(act):
            act.sem_inc(z_copied, DT)
            with act.Fori(0, PIECES) as c:
                for k in range(DT):
                    act.wait_ge(mm, 2 * DT * c + DT + k + 1)
                    act.activation(z_gate[:, k, ds(c * COLS, COLS)], ps[DT + k][:, 0:COLS], ACT.Silu).then_inc(z_copied, 1)

        @block.vector
        def _(dve):
            dve.sem_inc(u_copied, DT)
            with dve.Fori(0, PIECES) as c:
                for k in range(DT):
                    dve.wait_ge(mm, 2 * DT * c + k + 1)
                    dve.tensor_copy(u_pre[:, k, ds(c * COLS, COLS)], ps[k][:, 0:COLS]).then_inc(u_copied, 1)


def scan(nc, A, bcD, u_pre, z_gate):
    with ExitStack() as ctx:
        m = Mem(nc, ctx, "scn")
        taps = m.sb("taps", [P, DT, KS])
        diag = m.sb("diag", [P, DT, KS, P])
        eye = m.sb("eye", [P, P])
        conv_b = m.sb("conv_b", [P, DT])
        w_x = m.sb("w_x", [P, DT, XP])
        w_dt = m.sb("w_dt", [DT_RANK, D_INNER])
        b_dt = m.sb("b_dt", [P, DT])
        a_log = m.sb("a_log", [P, DT, N_STATE])
        a_neg = m.sb("a_neg", [P, DT, N_STATE])
        skip = m.sb("skip", [P, DT])
        u = [m.sb(f"u{v}", [P, DT, CT]) for v in range(2)]
        delta = [m.sb(f"delta{v}", [P, DT, CT]) for v in range(2)]
        du = [m.sb(f"du{v}", [P, DT, CT]) for v in range(2)]
        far = m.sb("far", [P, CH_IMGS])
        dbl = m.sb("dbl", [XP, CT])
        RING = 4
        decay = [m.sb(f"decay{v}", [P, DT, CT]) for v in range(RING)]
        state = [m.sb(f"state{v}", [P, DT, CT]) for v in range(RING)]
        prod = [m.sb(f"prod{v}", [P, DT, CT]) for v in range(2)]
        b_row = [m.sb(f"b_row{v}", [P, CT]) for v in range(RING)]
        c_row = [m.sb(f"c_row{v}", [P, CT]) for v in range(RING)]
        YCOLS = DT * CT
        ps_y = m.ps("ps_y", [P, -(-YCOLS // 512) * 512])
        ps_p = [m.ps(f"ps_p{v}", [P, 2, 512]) for v in range(2)]

        w_in, eye_set, diag_set, a_exp, a_done = (m.sem(n) for n in ("w_in", "eye_set", "diag_set", "a_exp", "a_done"))
        conv_mm, silu_done, x_mm, x_copied, bc_stored = (
            m.sem(n) for n in ("conv_mm", "silu_done", "x_mm", "x_copied", "bc_stored"))
        dt_mm, dt_read, soft_done, delta_sum, delta_done, du_done = (
            m.sem(n) for n in ("dt_mm", "dt_read", "soft_done", "delta_sum", "delta_done", "du_done"))
        soft_link = m.sem("soft_link")
        b_in = [m.sem(f"b_in{v}") for v in range(RING)]
        c_in = [m.sem(f"c_in{v}") for v in range(RING)]
        decay_done, bu_done, scan_done, c_done, sum_done = (
            m.sem(n) for n in ("decay_done", "bu_done", "scan_done", "c_done", "sum_done"))
        sp_link, far_set = m.sem("sp_link"), m.sem("far_set")
        y_out, joined, y_gated = m.sem("y_out"), m.sem("joined"), m.sem("y_gated")
        W_LOADS = 16 * 7
        S = N_STATE
        EXP_LN = "natural_log_exp_and_others"
        block = ctx.enter_context(nc.Block())

        def run(eng, prep_all, units):
            prep_all(0)
            units(0, 0, True)
            with eng.Fori(0, CHUNKS - 1) as c:
                units(c, 1, True)
                units(c + 1, 0, True)
            units(CHUNKS - 1, 1, False)

        def after(c, d):
            return (c, 1) if d == 0 else (c + 1, 0)

        def flat(t):
            return t[:].rearrange("p d t -> p (d t)")

        def two(t, k):
            return t[:, k, :].rearrange("p (h t) -> p h t", h=2)

        @block.sync
        def _(sp):
            for dst, name in ((taps, "conv_w"), (conv_b, "conv_b"), (w_x, "xproj_w"), (w_dt, "dt_w"), (b_dt, "dt_b"),
                              (a_log, "A_log"), (skip, "D")):
                sp.dma_start(dst[:], A[name]).then_inc(w_in, 16)

            def load_b(d, s):
                sp.dma_start(b_row[s % RING][:], bcD[d, s].partition_broadcast(P)).then_inc(b_in[s % RING], 16)

            def load_c(d, s):
                sp.dma_start(c_row[s % RING][:], bcD[d, S + s].partition_broadcast(P)).then_inc(c_in[s % RING], 16)

            def store(c, d):
                sp.wait_ge(x_copied, 2 * c + d + 1)
                sp.dma_start(bcD[d], dbl[DT_RANK:XP, :]).then_inc(bc_stored, 16)

            def prep_all(_):
                store(0, 0)
                sp.wait_ge(bc_stored, 16)
                for s in range(3):
                    load_b(0, s)
                load_c(0, 0)

            def units(c, d, more):
                for s in range(S):
                    n = (2 * c + d) * S + s
                    if s == 10 and more:
                        store(*after(c, d))
                        sp.wait_ge(bc_stored, 16 * (2 * c + d + 2))
                        sp.sem_inc(sp_link, 1)
                    if s + 3 < S or more:
                        if not (isinstance(n, int) and n == 0):
                            sp.wait_ge(bu_done, n)
                        load_b(d if s + 3 < S else 1 - d, (s + 3) % S)
                    if s + 1 < S or more:
                        if not (isinstance(n, int) and n < 3):
                            sp.wait_ge(c_done, n - 2)
                        load_c(d if s + 1 < S else 1 - d, (s + 1) % S)

            run(sp, prep_all, units)

        @block.tensor
        def _(pe):
            def conv(c, d, k):
                b = 2 * c + d
                if k == 2:
                    pe.wait_ge(silu_done, DT * b + 1)
                elif not (isinstance(b, int) and b == 0):
                    pe.wait_ge(dt_read, DT * b - 1 + k)
                bank = ps_p[(d + k) % 2]
                for h in range(2):
                    for j in range(KS):
                        sh, tap = j, KS - 1 - j
                        o = bank[:, h, 0:HC].rearrange("p (i t) -> p i t", t=POS)
                        x = u_pre[:, k, ds(c * CT + h * HC, HC)].rearrange("p (i t) -> p i t", t=POS)
                        if d == 0:
                            o, x = o[:, :, sh:POS], x[:, :, 0:POS - sh]
                        else:
                            o, x = o[:, :, 0:POS - sh], x[:, :, sh:POS]
                        last = pe.matmul(o, diag[:, k, tap, :], x, start=j == 0, stop=j == KS - 1)
                last.then_inc(conv_mm, 1)

            def xproj(c, d):
                pe.wait_ge(silu_done, DT * (2 * c + d) + DT)
                for h in range(2):
                    for k in range(DT):
                        last = pe.matmul(ps_p[(d + 3) % 2][0:XP, h, 0:HC], w_x[:, k, :], u[d][:, k, h * HC:(h + 1) * HC],
                                         start=k == 0, stop=k == DT - 1)
                last.then_inc(x_mm, 1)

            def dt_(c, d, k):
                pe.wait_ge(x_copied, 2 * c + d + 1)
                if k == 2:
                    pe.wait_ge(dt_read, DT * (2 * c + d) + 1)
                for h in range(2):
                    last = pe.matmul(ps_p[(d + k) % 2][:, h, 0:HC], w_dt[:, k * P:(k + 1) * P], dbl[0:DT_RANK, h * HC:(h + 1) * HC],
                                     start=True, stop=True)
                last.then_inc(dt_mm, 1)

            def prep_all(_):
                pe.wait_ge(w_in, W_LOADS)
                pe.wait_ge(diag_set, 1)
                for k in range(DT):
                    conv(0, 0, k)
                xproj(0, 0)
                for k in range(DT):
                    dt_(0, 0, k)

            def units(c, d, more):
                b2 = after(c, d)
                for s in range(S):
                    n = (2 * c + d) * S + s
                    if more:
                        if s in (0, 1, 3):
                            conv(*b2, (s + 1) // 2 if s < 3 else 2)
                        if s == 5:
                            xproj(*b2)
                        if s in (8, 9, 10):
                            dt_(*b2, s - 8)
                    pe.wait_ge(c_done, n + 1)
                    if s == 0 and not (isinstance(n, int) and n == 0):
                        pe.wait_ge(y_out, 2 * c + d)
                    for at in range(0, YCOLS, 512):
                        cols = slice(at, min(at + 512, YCOLS))
                        last = pe.matmul(ps_y[:, cols], eye[:], flat(prod[s % 2])[:, cols], start=s == 0, stop=s == S - 1)
                    last.then_inc(sum_done, 1)

            run(pe, prep_all, units)

        @block.scalar
        def _(act):
            def silu(c, d, k):
                act.wait_ge(conv_mm, DT * (2 * c + d) + k + 1)
                if k == 0 and not (isinstance(c, int) and c == 0):
                    if d == 0:
                        act.wait_ge(y_out, 2 * c - 1)
                    else:
                        act.wait_ge(joined, c)
                act.activation(two(u[d], k), ps_p[(d + k) % 2][:, :, 0:HC], ACT.Silu, bias=conv_b[:, k:k + 1]).then_inc(silu_done, 1)
                act.preload_act_table_set(EXP_LN)

            def x_copy(c, d):
                act.wait_ge(x_mm, 2 * c + d + 1)
                if not (isinstance(c, int) and c == 0 and d == 0):
                    act.wait_ge(bc_stored, 16 * (2 * c + d))
                    act.wait_ge(dt_mm, DT * (2 * c + d))
                act.activation(dbl[:].rearrange("p (h t) -> p h t", h=2), ps_p[(d + 3) % 2][0:XP, :, 0:HC], ACT.Copy
                               ).then_inc(x_copied, 1)

            def softplus(c, d, k):
                r = DT * (2 * c + d) + k
                act.wait_ge(dt_mm, r + 1)
                if not (isinstance(c, int) and c == 0) and k == 0:
                    act.wait_ge(decay_done, (2 * c + d - 1) * S)
                    act.wait_ge(bu_done, (2 * c + d - 1) * S)
                x = ps_p[(d + k) % 2][:, :, 0:HC]
                act.activation(two(du[d], k), x, ACT.Relu, bias=b_dt[:, k:k + 1])
                act.activation(two(delta[d], k), x, ACT.Abs, bias=b_dt[:, k:k + 1]).then_inc(dt_read, 1)
                act.wait_ge(dt_read, r + 1)
                act.activation(delta[d][:, k, :], delta[d][:, k, :], ACT.Exp, scale=-1.0).then_inc(soft_link, 1)
                act.wait_ge(soft_link, r + 1)
                act.activation(delta[d][:, k, :], delta[d][:, k, :], ACT.Ln, bias=1.0).then_inc(soft_done, 1)

            def prep_all(_):
                act.wait_ge(w_in, W_LOADS)
                act.preload_act_table_set(EXP_LN)
                act.activation(a_log[:], a_log[:], ACT.Exp).then_inc(a_exp, 1)
                for k in range(DT):
                    silu(0, 0, k)
                x_copy(0, 0)
                for k in range(DT):
                    softplus(0, 0, k)
                act.wait_ge(a_done, 1)

            def units(c, d, more):
                b2 = after(c, d)
                for s in range(S):
                    n = (2 * c + d) * S + s
                    if s == 0:
                        act.wait_ge(delta_done, DT * (2 * c + d + 1))
                    if not (isinstance(n, int) and n < RING):
                        act.wait_ge(scan_done, n - RING + 1)
                    for k in range(DT):
                        last = act.activation(decay[s % RING][:, k, :], delta[d][:, k, :], ACT.Exp, scale=a_neg[:, k, s:s + 1])
                    last.then_inc(decay_done, 1)
                    if more:
                        if s in (4, 5, 6):
                            silu(*b2, s - 4)
                        if s == 8:
                            x_copy(*b2)
                        if s in (11, 12, 13):
                            softplus(*b2, s - 11)

            run(act, prep_all, units)

        @block.gpsimd
        def _(pool):
            def delta_(c, d, k):
                r = DT * (2 * c + d) + k
                pool.wait_ge(soft_done, r + 1)
                pool.tensor_tensor(delta[d][:, k, :], delta[d][:, k, :], du[d][:, k, :], ALU.add).then_inc(delta_sum, 1)

            def prep_all(_):
                pool.memset(eye[:], 0.0).then_inc(eye_set, 1)
                pool.wait_ge(eye_set, 1)
                pool.affine_select(out=eye[:], in_=eye[:], compare_op=ALU.not_equal, fill=1.0, base=0,
                                   pattern=[[-1, P]], channel_multiplier=1).then_inc(eye_set, 1)
                pool.memset(far[:], FAR).then_inc(far_set, 1)
                for k in range(DT):
                    delta_(0, 0, k)

            def join(c):
                pool.wait_ge(y_out, 2 * c + 2)
                at = ds(c * CT, CT)
                pool.tensor_tensor(u_pre[:, :, at], u_pre[:, :, at], u[1][:], ALU.add).then_inc(joined, 1)

            def units(c, d, more):
                b2 = after(c, d)
                for s in range(S):
                    n = (2 * c + d) * S + s
                    uses = S // RING * (2 * c + d) + s // RING
                    pool.wait_ge(b_in[s % RING], 16 * (uses + 1))
                    if s == 0:
                        pool.wait_ge(du_done, DT * (2 * c + d + 1))
                    if not (isinstance(n, int) and n < RING):
                        pool.wait_ge(c_done, n - RING + 1)
                    pool.tensor_tensor(state[s % RING][:], du[d][:], b_row[s % RING][:].unsqueeze(1).to_broadcast([P, DT, CT]),
                                       ALU.mult).then_inc(bu_done, 1)
                    if more and s in (11, 12, 13):
                        delta_(*b2, s - 11)
                    if d == 0 and s == 3 and not (isinstance(c, int) and c == 0):
                        join(c - 1)

            run(pool, prep_all, units)
            join(CHUNKS - 1)

        @block.vector
        def _(dve):
            def c_mul(blk, s):
                n = blk * S + s
                dve.wait_ge(scan_done, n + 1)
                dve.wait_ge(c_in[s % RING], 16 * (S // RING * blk + s // RING + 1))
                if not (isinstance(n, int) and n < 2):
                    dve.wait_ge(sum_done, n - 1)
                dve.tensor_tensor(prod[s % 2][:], state[s % RING][:],
                                  c_row[s % RING][:].unsqueeze(1).to_broadcast([P, DT, CT]), ALU.mult).then_inc(c_done, 1)

            def read_y(c, d):
                dve.wait_ge(sum_done, S * (2 * c + d + 1))
                if d == 0:
                    dve.wait_ge(conv_mm, DT * (2 * c + 2))
                for k in range(DT):
                    o = u_pre[:, k, ds(c * CT, CT)] if d == 0 else u[1][:, k, :]
                    last = dve.scalar_tensor_tensor(out=o, in0=u[d][:, k, :], scalar=skip[:, k:k + 1],
                                                    in1=ps_y[:, k * CT:(k + 1) * CT], op0=ALU.mult, op1=ALU.add)
                last.then_inc(y_out, 1)

            def gate(c):
                dve.wait_ge(joined, c + 1)
                at = ds(c * CT, CT)
                dve.tensor_tensor(u_pre[:, :, at], u_pre[:, :, at], z_gate[:, :, at], ALU.mult).then_inc(y_gated, 1)

            def du_(c, d, k):
                r = DT * (2 * c + d) + k
                dve.wait_ge(delta_sum, r + 1)
                dve.tensor_tensor(du[d][:, k, :], delta[d][:, k, :], u[d][:, k, :], ALU.mult).then_inc(du_done, 1)
                dve.wait_ge(du_done, r + 1)
                first = (0 if d == 0 else POS - 1)
                starts = delta[d][:, k, first:CT:POS]
                dve.tensor_tensor(starts, starts, far[:], ALU.add).then_inc(delta_done, 1)

            def prep_all(_):
                dve.wait_ge(a_exp, 1)
                dve.tensor_scalar(a_neg[:], a_log[:], -1.0, None, ALU.mult).then_inc(a_done, 1)
                dve.wait_ge(eye_set, 2)
                dve.wait_ge(far_set, 1)
                for k in range(DT):
                    for j in range(KS):
                        last = dve.tensor_scalar(diag[:, k, j, :], eye[:], taps[:, k, j:j + 1], None, ALU.mult)
                last.then_inc(diag_set, 1)
                for k in range(DT):
                    du_(0, 0, k)

            def one(c, d, s, first=False):
                n = (2 * c + d) * S + s
                dve.wait_ge(decay_done, n + 1)
                dve.wait_ge(bu_done, n + 1)
                x, a = flat(state[s % RING]), flat(decay[s % RING])
                if d == 1:
                    x, a = x[:, ::-1], a[:, ::-1]
                dve.tensor_tensor_scan(x, a, x, 0.0, ALU.mult, ALU.add).then_inc(scan_done, 1)
                if not first:
                    c_mul(2 * c + d - (s == 0), (s - 1) % S)

            def units(c, d, first=False, more=True):
                for s in range(S):
                    one(c, d, s, first and s == 0)
                    if more and s in (11, 12, 13):
                        du_(*after(c, d), s - 11)
                    if d == 0 and s == 6 and not (isinstance(c, int) and c == 0):
                        gate(c - 1)
                    if s == 1 and not first:
                        read_y(*((c - 1, 1) if d == 0 else (c, 0)))

            dve.wait_ge(w_in, W_LOADS)
            prep_all(0)
            units(0, 0, True)
            with dve.Fori(0, CHUNKS - 1) as c:
                units(c, 1)
                units(c + 1, 0)
            units(CHUNKS - 1, 1, more=False)
            c_mul(2 * CHUNKS - 1, S - 1)
            read_y(CHUNKS - 1, 1)
            gate(CHUNKS - 1)


def out_projection(nc, A, y, R):
    with ExitStack() as ctx:
        m = Mem(nc, ctx, "outp")
        w = m.sb("w", [P, DT, D])
        ps = [m.ps(f"ps{v}", [P, 512]) for v in range(4)]
        w_in, mm, added = m.sem("w_in"), m.sem("mm"), m.sem("added")
        block = ctx.enter_context(nc.Block())

        @block.sync
        def _(sp):
            sp.dma_start(w[:], A["out_w"]).then_inc(w_in, 16)

        @block.tensor
        def _(pe):
            pe.wait_ge(w_in, 16)
            for t in range(TILES):
                if t >= 4:
                    pe.wait_ge(added, t - 3)
                for k in range(DT):
                    last = pe.matmul(ps[t % 4][:, 0:D], y[:, k, t * P:(t + 1) * P], w[:, k, :],
                                     start=k == 0, stop=k == DT - 1)
                last.then_inc(mm, 1)

        @block.vector
        def _(dve):
            for t in range(TILES):
                dve.wait_ge(mm, t + 1)
                dve.scalar_tensor_tensor(out=R[:, t, :], in0=ps[t % 4][:, 0:D], scalar=0.5, in1=R[:, t, :],
                                         op0=ALU.mult, op1=ALU.add).then_inc(added, 1)


def mamba(nc, A, R, ident, bcD):
    with ExitStack() as ctx:
        u_pre = ctx.enter_context(nc.sbuf_tensor("u_pre", [P, DT, TOK], F32))
        z_gate = ctx.enter_context(nc.sbuf_tensor("z_gate", [P, DT, TOK], F32))
        with nc.sbuf_tensor("m_feat", [DH, 2, TOK], F32) as featT:
            layer_norm(nc, "mln", ident, R, featT, add_to=R, affine=(A["norm_w"], A["norm_b"]), twice=True)
            in_projection(nc, A, featT, u_pre, z_gate)
        scan(nc, A, bcD, u_pre, z_gate)
        out_projection(nc, A, u_pre, R)



def scores_and_mixer(nc, A, ident, normT, mixT, mask, scD, maskD):
    with ExitStack() as ctx:
        m = Mem(nc, ctx, "sc")
        wr = m.sb("wr", [DH, 2, DH])
        br = m.sb("br", [DH, 1])
        score = m.sb("score", [DH, TOK])
        prod = m.sb("prod", [DH, 2, TOK])
        pooled = m.sb("pooled", [DH, 2, IMGS])
        total = m.sb("total", [DH, IMGS])
        inv = m.sb("inv", [DH, IMGS])
        ranks = m.sb("ranks", [IMGS, POS + PAD])
        neg = m.sb("neg", [IMGS, POS + PAD])
        low = m.sb("low", [IMGS, 8])
        marked = m.sb("marked", [IMGS, POS + PAD])
        mask_rows = m.sb("mask_rows", [TILES, P])
        ps = [m.ps(f"ps{v}", [DH, 512]) for v in range(PIECES)]
        ps_m = m.ps("ps_m", [P, 512])
        mask_turned = m.sem("mask_turned")
        w_in, mm, sig, sc_out, sc_in = (m.sem(n) for n in ("w_in", "mm", "sig", "sc_out", "sc_in"))
        link, mask_done, mask_out, mask_in = (m.sem(n) for n in ("link", "mask_done", "mask_out", "mask_in"))
        weighed, summed, pool_link, inv_done, mixed = (
            m.sem(n) for n in ("weighed", "summed", "pool_link", "inv_done", "mixed"))
        block = ctx.enter_context(nc.Block())

        def imgs(t):
            return t.rearrange("c (i q) -> c i q", q=POS)

        @block.sync
        def _(sp):
            sp.dma_start(wr[:], A["Wr"]).then_inc(w_in, 16)
            sp.dma_start(br[:], A["br"].partition_broadcast(DH)).then_inc(w_in, 16)
            sp.wait_ge(sig, PIECES)
            sp.dma_start(scD, score[0:1, :]).then_inc(sc_out, 16)
            sp.wait_ge(sc_out, 16)
            sp.dma_start(ranks[:, 0:POS], scD.rearrange("o (i q) -> (o i) q", q=POS)).then_inc(sc_in, 16)
            sp.wait_ge(mask_done, 1)
            sp.dma_start(maskD.rearrange("o (i q) -> (o i) q", q=POS), marked[:, 0:POS]).then_inc(mask_out, 16)
            sp.wait_ge(mask_out, 16)
            sp.dma_start(mask_rows[:], maskD.rearrange("o (t p) -> (o t) p", p=P)).then_inc(mask_in, 16)

        @block.tensor
        def _(pe):
            pe.wait_ge(w_in, 32)
            for c in range(PIECES):
                for h in range(2):
                    last = pe.matmul(ps[c][:, 0:COLS], wr[:, h, :], normT[:, h, c * COLS:(c + 1) * COLS],
                                     start=h == 0, stop=h == 1)
                last.then_inc(mm, 1)
            pe.wait_ge(mask_in, 16)
            pe.transpose(ps_m[:, 0:TILES], mask_rows[:], ident[0:TILES, 0:TILES]).then_inc(mask_turned, 1)

        @block.scalar
        def _(act):
            act.wait_ge(w_in, 32)
            for c in range(PIECES):
                act.wait_ge(mm, c + 1)
                act.activation(score[:, c * COLS:(c + 1) * COLS], ps[c][:, 0:COLS], ACT.Sigmoid, bias=br[:, 0:1]
                               ).then_inc(sig, 1)

        @block.gpsimd
        def _(pool):
            pool.wait_ge(sig, PIECES)
            pool.tensor_tensor(prod[:, 1, :], normT[:, 1, :], score[:], ALU.mult).then_inc(weighed, 1)
            pool.wait_ge(pool_link, 2)
            pool.tensor_tensor(imgs(prod[:, 1, :]), imgs(score[:]), pooled[:, 1, :].unsqueeze(2).to_broadcast([DH, IMGS, POS]),
                               ALU.mult).then_inc(weighed, 1)
            pool.wait_ge(weighed, 2)
            pool.tensor_tensor(mixT[:, 1, :], prod[:, 1, :], normT[:, 1, :], ALU.add).then_inc(mixed, 1)

        @block.vector
        def _(dve):
            n = [0]

            def linked(ins):
                n[0] += 1
                ins.then_inc(link, 1)
                dve.wait_ge(link, n[0])

            dve.memset(neg[:], -2.0).then_inc(link, 1)
            n[0] += 1
            dve.wait_ge(sig, PIECES)
            linked(dve.tensor_tensor(prod[:, 0, :], normT[:, 0, :], score[:], ALU.mult))
            dve.tensor_reduce(pooled[:, 0, :], imgs(prod[:, 0, :]), AX_X, ALU.add).then_inc(summed, 1)
            dve.tensor_reduce(total[:], imgs(score[:]), AX_X, ALU.add).then_inc(summed, 1)
            dve.wait_ge(weighed, 1)
            dve.tensor_reduce(pooled[:, 1, :], imgs(prod[:, 1, :]), AX_X, ALU.add).then_inc(summed, 1)
            dve.wait_ge(summed, 3)
            linked(dve.tensor_scalar(total[:], total[:], 1e-6, None, ALU.add))
            linked(dve.reciprocal(inv[:], total[:]))
            for h in range(2):
                dve.tensor_tensor(pooled[:, h, :], pooled[:, h, :], inv[:], ALU.mult).then_inc(pool_link, 1)
            dve.wait_ge(pool_link, 2)
            linked(dve.tensor_tensor(imgs(prod[:, 0, :]), imgs(score[:]),
                                     pooled[:, 0, :].unsqueeze(2).to_broadcast([DH, IMGS, POS]), ALU.mult))
            dve.tensor_tensor(mixT[:, 0, :], prod[:, 0, :], normT[:, 0, :], ALU.add).then_inc(mixed, 1)
            dve.wait_ge(sc_in, 16)
            linked(dve.tensor_scalar(neg[:, 0:POS], ranks[:, 0:POS], -1.0, None, ALU.mult))
            linked(dve.max(low[:], neg[:]))
            linked(dve.memset(low[:, KEEP:8], -2.0))
            linked(dve.match_replace(out=marked[:], in_to_replace=low[:], in_values=neg[:], imm_value=5.0))
            dve.tensor_scalar(marked[:], marked[:], 1.0, None, ALU.is_ge).then_inc(mask_done, 1)
            dve.wait_ge(mask_turned, 1)
            dve.tensor_copy(mask[:, 0, :], ps_m[:, 0:TILES]).then_inc(mask_done, 1)
            dve.tensor_scalar(mask[:, 1, :], ps_m[:, 0:TILES], -1.0, 1.0, ALU.mult, ALU.add).then_inc(mask_done, 1)


def qkv_projection(nc, A, featT, q, k, v):
    outs = [(t, h) for t in (q, k, v) for h in range(2)]
    with ExitStack() as ctx:
        m = Mem(nc, ctx, "qkv")
        w = m.sb("w", [DH, 2, 3 * D])
        b = m.sb("b", [DH, 6])
        ps = [m.ps(f"ps{n}", [DH, 512]) for n in range(6)]
        w_in, mm = m.sem("w_in"), m.sem("mm")
        copied = [m.sem(f"copied{e}") for e in range(2)]
        block = ctx.enter_context(nc.Block())

        @block.sync
        def _(sp):
            sp.dma_start(w[:], A["ffn_qkv_w"]).then_inc(w_in, 16)
            sp.dma_start(b[:], A["ffn_qkv_b"]).then_inc(w_in, 16)

        @block.tensor
        def _(pe):
            pe.wait_ge(w_in, 32)
            with pe.Fori(0, PIECES) as c:
                for n in range(6):
                    pe.wait_ge(copied[n % 2], 3 * c + n // 2 + 1)
                    for h in range(2):
                        last = pe.matmul(ps[n][:, 0:COLS], w[:, h, n * DH:(n + 1) * DH], featT[:, h, ds(c * COLS, COLS)],
                                         start=h == 0, stop=h == 1)
                    last.then_inc(mm, 1)

        @block.scalar
        def _(act):
            act.sem_inc(copied[0], 3)
            act.wait_ge(w_in, 32)
            with act.Fori(0, PIECES) as c:
                for n in range(0, 6, 2):
                    t, h = outs[n]
                    act.wait_ge(mm, 6 * c + n + 1)
                    act.activation(t[:, h, ds(c * COLS, COLS)], ps[n][:, 0:COLS], ACT.Identity, bias=b[:, n:n + 1]
                                   ).then_inc(copied[0], 1)

        @block.vector
        def _(dve):
            dve.sem_inc(copied[1], 3)
            dve.wait_ge(w_in, 32)
            with dve.Fori(0, PIECES) as c:
                for n in range(1, 6, 2):
                    t, h = outs[n]
                    dve.wait_ge(mm, 6 * c + n + 1)
                    dve.tensor_scalar(t[:, h, ds(c * COLS, COLS)], ps[n][:, 0:COLS], b[:, n:n + 1], None, ALU.add
                                      ).then_inc(copied[1], 1)


def attention(nc, A, tag, ident, q, k, v, ctxT):
    with ExitStack() as ctx:
        m = Mem(nc, ctx, tag)
        kmask = m.sb("kmask", [DH, HH])
        vmask = m.sb("vmask", [K3, D])
        qs = [m.sb(f"qs{u}", [DH, 2, PAIR]) for u in range(2)]
        vs = [m.sb(f"vs{u}", [DH, 2, 2, H3, POS]) for u in range(2)]
        kb = [m.sb(f"kb{u}", [DH, 2, 2, HH, POS]) for u in range(2)]
        prob = [m.sb(f"prob{u}", [PROWS, HEADS, POS]) for u in range(2)]
        top = [m.sb(f"top{u}", [PROWS, HEADS]) for u in range(2)]
        den = [m.sb(f"den{u}", [PROWS, HEADS]) for u in range(2)]
        rden = [m.sb(f"rden{u}", [PROWS, HEADS]) for u in range(2)]
        probT = [m.sb(f"probT{u}", [K3, GS, PROWS]) for u in range(2)]
        vb = [m.sb(f"vb{u}", [K3, 2, D]) for u in range(2)]
        cx = [m.sb(f"cx{u}", [PROWS, D]) for u in range(2)]
        ps_s = [m.ps(f"ps_s{u}", [PROWS, 512]) for u in range(2)]
        ps_p = [m.ps(f"ps_p{u}", [K3, 512]) for u in range(2)]
        ps_v = m.ps("ps_v", [K3, 512])
        ps_c = m.ps("ps_c", [PROWS, 512])
        ps_t = m.ps("ps_t", [DH, 512])
        masks_in = m.sem("masks_in")
        qk_ready, v_ready, qk_mm, sub_done, exp_done = (
            m.sem(n) for n in ("qk_ready", "v_ready", "qk_mm", "sub_done", "exp_done"))
        p_turned, p_copied, v_turned, vb_done, pv_mm, cx_done, c_turned, c_copied = (
            m.sem(n) for n in ("p_turned", "p_copied", "v_turned", "vb_done", "pv_mm", "cx_done", "c_turned", "c_copied"))
        top_done, den_done, rden_done = m.sem("top_done"), m.sem("den_done"), m.sem("rden_done")
        block = ctx.enter_context(nc.Block())

        def skewed(eng, stages):
            depth = len(stages)

            def step(p, parity):
                for lag, stage in enumerate(stages):
                    if stage and not (isinstance(p, int) and not 0 <= p - lag < PAIRS):
                        stage(p - lag, (parity + lag) % 2)
            for p in range(4):
                step(p, p % 2)
            with eng.Fori(2, PAIRS // 2) as i:
                for u in range(2):
                    step(2 * i + u, u)
            for p in range(PAIRS, PAIRS + depth - 1):
                step(p, p % 2)

        def late(p, n):
            return not (isinstance(p, int) and p < n)

        @block.sync
        def _(sp):
            sp.dma_start(kmask[:], A["kmask"]).then_inc(masks_in, 16)
            sp.dma_start(vmask[:], A["vmask"]).then_inc(masks_in, 16)

        @block.gpsimd
        def _(pool):
            def stage(p, u):
                if late(p, 2):
                    pool.wait_ge(qk_mm, p - 1)
                at = ds(p * PAIR, PAIR)
                pool.tensor_copy(qs[u][:], q[:, :, at])
                for h in range(2):
                    last = pool.tensor_tensor(
                        kb[u][:, h],
                        k[:, h, at].rearrange("c (i t) -> c i t", i=2).unsqueeze(2).to_broadcast([DH, 2, HH, POS]),
                        kmask[:].unsqueeze(1).unsqueeze(3).to_broadcast([DH, 2, HH, POS]), ALU.mult)
                last.then_inc(qk_ready, 1)

            pool.wait_ge(masks_in, 32)
            skewed(pool, [stage])

        @block.tensor
        def _(pe):
            def scores(p, u):
                pe.wait_ge(qk_ready, p + 1)
                if late(p, 2):
                    pe.wait_ge(sub_done, p - 1)
                for h in range(2):
                    cols = slice(h * HH * POS, (h + 1) * HH * POS)
                    pe.matmul(ps_s[u][0:ROW_B, cols], qs[u][:, h, 0:ROW_B], kb[u][:, h, 0], start=True, stop=True)
                    last = pe.matmul(ps_s[u][ROW_B:PROWS, cols], qs[u][:, h, POS:PAIR], kb[u][:, h, 1],
                                     start=True, stop=True)
                last.then_inc(qk_mm, 1)

            def turn(p, u):
                pe.wait_ge(exp_done, p + 1)
                if late(p, 2):
                    pe.wait_ge(p_copied, p - 1)
                for g in range(GS):
                    last = pe.transpose(ps_p[u][:, g * PROWS:(g + 1) * PROWS], prob[u][:, g * H3:(g + 1) * H3, :],
                                        ident[0:PROWS, 0:PROWS])
                last.then_inc(p_turned, 1)
                pe.wait_ge(v_ready, p + 1)
                if late(p, 1):
                    pe.wait_ge(vb_done, p)
                for i in range(2):
                    for h in range(2):
                        last = pe.transpose(ps_v[:, i * D + h * DH:i * D + (h + 1) * DH],
                                            vs[u][:, h, i].rearrange("c r t -> c (r t)"),
                                            ident[0:DH, 0:DH])
                last.then_inc(v_turned, 1)

            def values(p, u):
                pe.wait_ge(p_copied, p + 1)
                pe.wait_ge(vb_done, p + 1)
                if late(p, 1):
                    pe.wait_ge(cx_done, p)
                W3 = H3 * HD
                for g in range(GS):
                    cols = slice(g * W3, (g + 1) * W3)
                    pe.matmul(ps_c[0:ROW_B, cols], probT[u][:, g, 0:ROW_B], vb[u][:, 0, cols], start=True, stop=True)
                    last = pe.matmul(ps_c[ROW_B:PROWS, cols], probT[u][:, g, ROW_B:PROWS], vb[u][:, 1, cols],
                                     start=True, stop=True)
                last.then_inc(pv_mm, 1)

            def turn_back(p, u):
                pe.wait_ge(cx_done, p + 1)
                if late(p, 1):
                    pe.wait_ge(c_copied, p)
                for h in range(2):
                    last = pe.transpose(ps_t[:, h * PROWS:(h + 1) * PROWS], cx[u][:, h * DH:(h + 1) * DH],
                                        ident[0:PROWS, 0:PROWS])
                last.then_inc(c_turned, 1)

            skewed(pe, [scores, turn, values, turn_back])

        @block.scalar
        def _(act):
            def exps(p, u):
                act.wait_ge(sub_done, p + 1)
                act.activation(prob[u][:], prob[u][:], ACT.Exp, scale=float(HD) ** -0.5).then_inc(exp_done, 1)

            def copy_p(p, u):
                act.wait_ge(p_turned, p + 1)
                if late(p, 2):
                    act.wait_ge(pv_mm, p - 1)
                act.activation(probT[u][:].rearrange("c g t -> c (g t)"), ps_p[u][:, 0:GS * PROWS], ACT.Copy
                               ).then_inc(p_copied, 1)

            def copy_c(p, u):
                act.wait_ge(c_turned, p + 1)
                for h in range(2):
                    src = ps_t[:, h * PROWS:(h + 1) * PROWS]
                    src = bass.AP(tensor=src.tensor, offset=src.offset, ap=[src.ap[0], [ROW_B, 2], [1, POS]])
                    last = act.activation(ctxT[:, h, ds(p * PAIR, PAIR)].rearrange("c (i t) -> c i t", i=2), src, ACT.Copy)
                last.then_inc(c_copied, 1)

            def stage_v(p, u):
                if late(p, 2):
                    act.wait_ge(v_turned, p - 1)
                for h in range(2):
                    src = v[:, h, ds(p * PAIR, PAIR)].rearrange("c (i t) -> c i t", i=2)
                    last = act.activation(vs[u][:, h], src.unsqueeze(2).to_broadcast([DH, 2, H3, POS]), ACT.Copy)
                last.then_inc(v_ready, 1)

            def values_and_exps(p, u):
                stage_v(p, u)
                exps(p, u)

            skewed(act, [values_and_exps, copy_p, None, copy_c])

        @block.vector
        def _(dve):
            def center(p, u):
                dve.wait_ge(qk_mm, p + 1)
                s = ps_s[u][:, 0:HEADS * POS].rearrange("q (h t) -> q h t", t=POS)
                dve.tensor_reduce(top[u][:], s, AX_X, ALU.max).then_inc(top_done, 1)
                dve.wait_ge(top_done, p + 1)
                if late(p, 2):
                    dve.wait_ge(p_turned, p - 1)
                    dve.wait_ge(den_done, p - 1)
                dve.tensor_tensor(prob[u][:], s, top[u][:].unsqueeze(2).to_broadcast([PROWS, HEADS, POS]), ALU.subtract
                                  ).then_inc(sub_done, 1)

            def sums_and_values(p, u):
                dve.wait_ge(exp_done, p + 1)
                dve.tensor_reduce(den[u][:], prob[u][:], AX_X, ALU.add).then_inc(den_done, 1)
                dve.wait_ge(v_turned, p + 1)
                if late(p, 2):
                    dve.wait_ge(pv_mm, p - 1)
                dve.tensor_tensor(vb[u][:], ps_v[:, 0:2 * D].rearrange("c (i f) -> c i f", i=2),
                                  vmask[:].unsqueeze(1).to_broadcast([K3, 2, D]), ALU.mult).then_inc(vb_done, 1)
                dve.wait_ge(den_done, p + 1)
                if late(p, 2):
                    dve.wait_ge(cx_done, p - 1)
                dve.reciprocal(rden[u][:], den[u][:]).then_inc(rden_done, 1)

            def normalise(p, u):
                dve.wait_ge(pv_mm, p + 1)
                dve.wait_ge(rden_done, p + 1)
                if late(p, 2):
                    dve.wait_ge(c_turned, p - 1)
                dve.tensor_tensor(cx[u][:].rearrange("q (h f) -> q h f", f=HD),
                                  ps_c[:, 0:D].rearrange("q (h f) -> q h f", f=HD),
                                  rden[u][:].unsqueeze(2).to_broadcast([PROWS, HEADS, HD]), ALU.mult).then_inc(cx_done, 1)

            skewed(dve, [center, sums_and_values, normalise])


def merge(nc, A, ctxT, mixT, mask, h):
    with ExitStack() as ctx:
        m = Mem(nc, ctx, "mrg")
        w = m.sb("w", [DH, 2, 2, D])
        b = m.sb("b", [1, 2, D])
        ones = m.sb("ones", [1, P])
        ps = [[m.ps(f"ps{v}_{u}", [P, 512]) for u in range(4)] for v in range(2)]
        w_in, ones_set, mm, half_done, done = (m.sem(n) for n in ("w_in", "ones_set", "mm", "half_done", "done"))
        block = ctx.enter_context(nc.Block())

        @block.sync
        def _(sp):
            sp.dma_start(w[:], A["ffn_om_w"]).then_inc(w_in, 16)
            sp.dma_start(b[:], A["ffn_om_b"]).then_inc(w_in, 16)

        @block.gpsimd
        def _(pool):
            pool.memset(ones[:], 1.0).then_inc(ones_set, 1)

        @block.tensor
        def _(pe):
            pe.wait_ge(w_in, 32)
            pe.wait_ge(ones_set, 1)
            for t in range(TILES):
                if t >= 4:
                    pe.wait_ge(done, t - 3)
                for v, src in enumerate((ctxT, mixT)):
                    o = ps[v][t % 4][:, 0:D]
                    for hh in range(2):
                        pe.matmul(o, src[:, hh, t * P:(t + 1) * P], w[:, hh, v, :], start=hh == 0, stop=False)
                    last = pe.matmul(o, ones[:], b[:, v, :], start=False, stop=True)
                last.then_inc(mm, 1)

        @block.vector
        def _(dve):
            for t in range(TILES):
                dve.wait_ge(mm, t + 1)
                dve.scalar_tensor_tensor(out=h[:, t, :], in0=ps[0][t % 4][:, 0:D], scalar=mask[:, 0, t:t + 1],
                                         in1=h[:, t, :], op0=ALU.mult, op1=ALU.add).then_inc(half_done, 1)
                dve.wait_ge(half_done, t + 1)
                dve.scalar_tensor_tensor(out=h[:, t, :], in0=ps[1][t % 4][:, 0:D], scalar=mask[:, 1, t:t + 1],
                                         in1=h[:, t, :], op0=ALU.mult, op1=ALU.add).then_inc(done, 1)


def mlp(nc, A, featT, h, R):
    with ExitStack() as ctx:
        m = Mem(nc, ctx, "mlp")
        w1 = m.sb("w1", [DH, 2, FFN])
        b1 = m.sb("b1", [P, FT])
        w2 = m.sb("w2", [P, FT, D])
        b2 = m.sb("b2", [P, D])
        hid = [m.sb(f"hid{u}", [P, FT, COLS]) for u in range(2)]
        ps1 = [m.ps(f"ps1_{u}", [P, 512]) for u in range(4)]
        ps2 = [m.ps(f"ps2_{u}", [P, 512]) for u in range(4)]
        w_in, mm1, act_done, mm2, added, base = (
            m.sem(n) for n in ("w_in", "mm1", "act_done", "mm2", "added", "base"))
        PT_ = COLS // P
        block = ctx.enter_context(nc.Block())

        @block.sync
        def _(sp):
            for t, n in ((w1, "ffn_w1"), (b1, "ffn_b1"), (w2, "ffn_w2")):
                sp.dma_start(t[:], A[n]).then_inc(w_in, 16)
            sp.dma_start(b2[:], A["ffn_b2"].partition_broadcast(P)).then_inc(w_in, 16)

        @block.gpsimd
        def _(pool):
            pool.wait_ge(w_in, 64)
            pool.tensor_tensor(h[:], h[:], b2[:].unsqueeze(1).to_broadcast([P, TILES, D]), ALU.add).then_inc(base, 1)
            pool.wait_ge(base, 1)
            pool.tensor_tensor(R[:], R[:], h[:], ALU.add).then_inc(base, 1)

        @block.tensor
        def _(pe):
            def first(c):
                for k in range(FT):
                    n = c * FT + k
                    if n >= 4:
                        pe.wait_ge(act_done, n - 3)
                    for hh in range(2):
                        last = pe.matmul(ps1[n % 4][:, 0:COLS], w1[:, hh, k * P:(k + 1) * P],
                                         featT[:, hh, c * COLS:(c + 1) * COLS], start=hh == 0, stop=hh == 1)
                    last.then_inc(mm1, 1)

            def second(c):
                pe.wait_ge(act_done, FT * (c + 1))
                for t in range(PT_):
                    n = c * PT_ + t
                    if n >= 4:
                        pe.wait_ge(added, n - 3)
                    for k in range(FT):
                        last = pe.matmul(ps2[n % 4][:, 0:D], hid[c % 2][:, k, t * P:(t + 1) * P], w2[:, k, :],
                                         start=k == 0, stop=k == FT - 1)
                    last.then_inc(mm2, 1)

            pe.wait_ge(w_in, 64)
            first(0)
            for c in range(1, PIECES):
                first(c)
                second(c - 1)
            second(PIECES - 1)

        @block.scalar
        def _(act):
            act.wait_ge(w_in, 64)
            for c in range(PIECES):
                if c >= 2:
                    act.wait_ge(mm2, PT_ * (c - 1))
                for k in range(FT):
                    act.wait_ge(mm1, c * FT + k + 1)
                    act.activation(hid[c % 2][:, k, :], ps1[(c * FT + k) % 4][:, 0:COLS], ACT.Gelu, bias=b1[:, k:k + 1]
                                   ).then_inc(act_done, 1)

        @block.vector
        def _(dve):
            dve.wait_ge(base, 2)
            for t in range(TILES):
                dve.wait_ge(mm2, t + 1)
                dve.tensor_tensor(R[:, t, :], R[:, t, :], ps2[t % 4][:, 0:D], ALU.add).then_inc(added, 1)


def routed_ffn(nc, A, R, ident):
    scD = nc.dram_tensor("score_scratch", [1, TOK], F32).ap()
    maskD = nc.dram_tensor("mask_scratch", [1, TOK], F32).ap()
    with ExitStack() as ctx:
        h = ctx.enter_context(nc.sbuf_tensor("f_h", [P, TILES, D], F32))
        mask = ctx.enter_context(nc.sbuf_tensor("f_mask", [P, 2, TILES], F32))
        with ExitStack() as inner:
            def feat(name):
                return inner.enter_context(nc.sbuf_tensor(name, [DH, 2, TOK], F32))

            normT, mixT = feat("f_norm"), feat("f_mix")
            layer_norm(nc, "fln", ident, R, normT, x1=h, affine=(A["g1"], A["b1"]), twice=True)
            scores_and_mixer(nc, A, ident, normT, mixT, mask, scD, maskD)
            q, k, v, ctxT = feat("f_q"), feat("f_k"), feat("f_v"), feat("f_ctx")
            qkv_projection(nc, A, normT, q, k, v)
            attention(nc, A, "fat", ident, q, k, v, ctxT)
            merge(nc, A, ctxT, mixT, mask, h)
        with nc.sbuf_tensor("f_norm2", [DH, 2, TOK], F32) as n2T:
            layer_norm(nc, "fln2", ident, h, n2T, affine=(A["g2"], A["b2"]))
            mlp(nc, A, n2T, h, R)



def rotary_projection(nc, A, featT, q, k, v):
    with ExitStack() as ctx:
        m = Mem(nc, ctx, "rot")
        w = m.sb("w", [DH, 2, 5 * D])
        cs = m.sb("cs", [DH, 2, POS])
        swapped = [m.sb(f"swapped{u}", [DH, RP]) for u in range(2)]
        plain = [m.sb(f"plain{u}", [DH, RP]) for u in range(2)]
        ps = [m.ps(f"ps{n}", [DH, 512]) for n in range(8)]
        w_in, mm, cosd, sind, turned, v_copied = (m.sem(n) for n in ("w_in", "mm", "cosd", "sind", "turned", "v_copied"))
        block = ctx.enter_context(nc.Block())
        dst = [(t, h) for t in (q, k) for h in range(2)]

        def imgs(t):
            return t.rearrange("c (i q) -> c i q", q=POS)

        @block.sync
        def _(sp):
            sp.dma_start(w[:], A["rot_w"]).then_inc(w_in, 16)
            sp.dma_start(cs[:], A["rot_cs"]).then_inc(w_in, 16)

        @block.tensor
        def _(pe):
            def product(bank, col, c):
                for h in range(2):
                    last = pe.matmul(ps[bank][:, 0:RP], w[:, h, col:col + DH], featT[:, h, ds(c * RP, RP)],
                                     start=h == 0, stop=h == 1)
                last.then_inc(mm, 1)

            pe.wait_ge(w_in, 32)
            with pe.Fori(0, RPIECES) as c:
                for n in range(4):
                    if n == 0:
                        pe.wait_ge(v_copied, 2 * c + 2)
                    else:
                        pe.wait_ge(sind, 4 * c + n + 1)
                    product(2 * n, n * DH, c)
                    product(2 * n + 1, (6 + n) * DH, c)
                for h in range(2):
                    pe.wait_ge(sind, 4 * c + 5)
                    product(h, (4 + h) * DH, c)

        @block.scalar
        def _(act):
            act.sem_inc(v_copied, 2)
            with act.Fori(0, RPIECES) as c:
                for h in range(2):
                    act.wait_ge(mm, 10 * c + 9 + h)
                    act.activation(v[:, h, ds(c * RP, RP)], ps[h][:, 0:RP], ACT.Copy).then_inc(v_copied, 1)

        @block.vector
        def _(dve):
            dve.sem_inc(sind, 4)
            dve.wait_ge(w_in, 32)
            with dve.Fori(0, RPIECES) as c:
                for n in range(4):
                    dve.wait_ge(mm, 10 * c + 2 * n + 2)
                    dve.wait_ge(turned, 4 * c + n + 1)
                    dve.tensor_tensor(imgs(plain[n % 2][:]), imgs(ps[2 * n][:, 0:RP]),
                                      cs[:, 0, :].unsqueeze(1).to_broadcast([DH, RP // POS, POS]), ALU.mult
                                      ).then_inc(cosd, 1)
                    dve.tensor_tensor(imgs(swapped[n % 2][:]), imgs(ps[2 * n + 1][:, 0:RP]),
                                      cs[:, 1, :].unsqueeze(1).to_broadcast([DH, RP // POS, POS]), ALU.mult
                                      ).then_inc(sind, 1)

        @block.gpsimd
        def _(pool):
            pool.sem_inc(turned, 2)
            with pool.Fori(0, RPIECES) as c:
                for n in range(4):
                    t, h = dst[n]
                    pool.wait_ge(cosd, 4 * c + n + 1)
                    pool.wait_ge(sind, 4 * c + n + 5)
                    pool.tensor_tensor(t[:, h, ds(c * RP, RP)], plain[n % 2][:], swapped[n % 2][:], ALU.add
                                       ).then_inc(turned, 1)


def project_out(nc, A, ctxT, R):
    with ExitStack() as ctx:
        m = Mem(nc, ctx, "prj")
        w = m.sb("w", [DH, 2, D])
        b = m.sb("b", [P, D])
        ps = [m.ps(f"ps{u}", [P, 512]) for u in range(4)]
        w_in, mm, base, done = (m.sem(n) for n in ("w_in", "mm", "base", "done"))
        block = ctx.enter_context(nc.Block())

        @block.sync
        def _(sp):
            sp.dma_start(w[:], A["proj_w"]).then_inc(w_in, 16)
            sp.dma_start(b[:], A["proj_b"].partition_broadcast(P)).then_inc(w_in, 16)

        @block.gpsimd
        def _(pool):
            pool.wait_ge(w_in, 32)
            for t in range(TILES):
                pool.tensor_tensor(R[:, t, :], R[:, t, :], b[:], ALU.add).then_inc(base, 1)

        @block.tensor
        def _(pe):
            pe.wait_ge(w_in, 32)
            for t in range(TILES):
                if t >= 4:
                    pe.wait_ge(done, t - 3)
                for h in range(2):
                    last = pe.matmul(ps[t % 4][:, 0:D], ctxT[:, h, t * P:(t + 1) * P], w[:, h, :],
                                     start=h == 0, stop=h == 1)
                last.then_inc(mm, 1)

        @block.vector
        def _(dve):
            for t in range(TILES):
                dve.wait_ge(mm, t + 1)
                dve.wait_ge(base, t + 1)
                dve.tensor_tensor(R[:, t, :], R[:, t, :], ps[t % 4][:, 0:D], ALU.add).then_inc(done, 1)


def rotary_attention(nc, A, R, ident):
    with ExitStack() as ctx:
        def feat(name):
            return ctx.enter_context(nc.sbuf_tensor(name, [DH, 2, TOK], F32))

        normT, q, k, v, ctxT = (feat("a_" + n) for n in ("norm", "q", "k", "v", "ctx"))
        layer_norm(nc, "aln", ident, R, normT)
        rotary_projection(nc, A, normT, q, k, v)
        attention(nc, A, "aat", ident, q, k, v, ctxT)
        project_out(nc, A, ctxT, R)



def gate_experts(nc, A, ident, featT, combT):
    with ExitStack() as ctx:
        m = Mem(nc, ctx, "gat")
        E, G = EXPERTS, GROUPS
        w = m.sb("w", [DH, 2, E])
        b = m.sb("b", [P, E])
        before = m.sb("before", [P, E, E])
        before_g = m.sb("before_g", [P, G, G])
        logit, prob, biased = (m.sb(n, [P, TILES, E]) for n in ("logit", "prob", "biased"))
        top, den, rden = (m.sb(n, [P, TILES]) for n in ("top", "den", "rden"))
        grp, grank = m.sb("grp", [P, TILES, G]), m.sb("grank", [P, TILES, G])
        rank = m.sb("rank", [P, TILES, E])
        wins, ties = m.sb("wins", [P, TILES, E * E]), m.sb("ties", [P, TILES, E * E])
        ps_l = m.ps("ps_l", [P, TILES, E])
        ps_c = [m.ps(f"ps_c{u}", [E, 512]) for u in range(4)]
        w_in, mm, link, centered, exped, comb, turned, copied, ones_set = (
            m.sem(n) for n in ("w_in", "mm", "link", "centered", "exped", "comb", "turned", "copied", "ones_set"))
        QUADS = -(-TILES // 4)
        block = ctx.enter_context(nc.Block())

        @block.sync
        def _(sp):
            sp.dma_start(w[:], A["gate_w"]).then_inc(w_in, 16)
            for dst, name in ((b, "gate_b"), (before, "before"), (before_g, "before_g")):
                src = A[name]
                flat = dst[:] if len(src.shape) == 1 else dst[:].rearrange("p j i -> p (j i)")
                src = src if len(src.shape) == 1 else src.rearrange("j i -> (j i)")
                sp.dma_start(flat, src.partition_broadcast(P)).then_inc(w_in, 16)

        @block.tensor
        def _(pe):
            pe.wait_ge(w_in, 64)
            for t in range(TILES):
                for h in range(2):
                    last = pe.matmul(ps_l[:, t, :], featT[:, h, t * P:(t + 1) * P], w[:, h, :], start=h == 0, stop=h == 1)
            last.then_inc(mm, 1)
            pe.wait_ge(comb, 1)
            for q in range(QUADS):
                if q >= 4:
                    pe.wait_ge(copied, q - 3)
                for t in range(4 * q, min(4 * q + 4, TILES)):
                    last = pe.transpose(ps_c[q % 4][:, (t % 4) * P:(t % 4 + 1) * P], rank[:, t, :], ident[:])
                last.then_inc(turned, 1)

        @block.gpsimd
        def _(pool):
            pool.memset(combT[:], 1.0).then_inc(ones_set, 1)

        @block.scalar
        def _(act):
            act.wait_ge(centered, 1)
            act.activation(prob[:], logit[:], ACT.Exp).then_inc(exped, 1)
            act.wait_ge(ones_set, 1)
            for q in range(QUADS):
                act.wait_ge(turned, q + 1)
                n = min(4, TILES - 4 * q) * P
                act.activation(combT[0:E, 4 * q * P:4 * q * P + n], ps_c[q % 4][:, 0:n], ACT.Copy).then_inc(copied, 1)

        @block.vector
        def _(dve):
            n = [0]

            def linked(ins):
                n[0] += 1
                ins.then_inc(link, 1)
                dve.wait_ge(link, n[0])

            def over(t, k):
                return t[:].unsqueeze(2).to_broadcast([P, TILES, k])

            def ranks(out, x, k, mask):
                a = x.unsqueeze(2).to_broadcast([P, TILES, k, k])
                o = x.unsqueeze(3).to_broadcast([P, TILES, k, k])
                win = wins[:, :, 0:k * k].rearrange("p t (j i) -> p t j i", i=k)
                tie = ties[:, :, 0:k * k].rearrange("p t (j i) -> p t j i", i=k)
                linked(dve.tensor_tensor(win, a, o, ALU.is_gt))
                linked(dve.tensor_tensor(tie, a, o, ALU.is_equal))
                linked(dve.tensor_tensor(tie, tie, mask[:].unsqueeze(1).to_broadcast([P, TILES, k, k]), ALU.mult))
                linked(dve.tensor_tensor(win, win, tie, ALU.add))
                linked(dve.tensor_reduce(out, win, AX_X, ALU.add))

            dve.wait_ge(w_in, 64)
            dve.wait_ge(mm, 1)
            linked(dve.tensor_reduce(top[:], ps_l[:], AX_X, ALU.max))
            dve.tensor_tensor(logit[:], ps_l[:], over(top, E), ALU.subtract).then_inc(centered, 1)
            dve.wait_ge(exped, 1)
            linked(dve.tensor_reduce(den[:], prob[:], AX_X, ALU.add))
            linked(dve.reciprocal(rden[:], den[:]))
            linked(dve.tensor_tensor(prob[:], prob[:], over(rden, E), ALU.mult))
            linked(dve.tensor_tensor(biased[:], prob[:], b[:].unsqueeze(1).to_broadcast([P, TILES, E]), ALU.add))
            pairs = biased[:].rearrange("p t (g e) -> p t g e", e=E // G)
            linked(dve.tensor_tensor(grp[:], pairs[:, :, :, 0], pairs[:, :, :, 1], ALU.add))
            ranks(grank[:], grp[:], G, before_g)
            linked(dve.tensor_scalar(grank[:], grank[:], float(TOPK_GROUPS), None, ALU.is_lt))
            keep = grank[:].unsqueeze(3).to_broadcast([P, TILES, G, E // G])
            linked(dve.tensor_tensor(pairs, pairs, keep, ALU.mult))
            linked(dve.tensor_scalar(grank[:], grank[:], 1.0, OUT_OF, ALU.subtract, ALU.mult))
            linked(dve.tensor_tensor(pairs, pairs, keep, ALU.add))
            ranks(rank[:], biased[:], E, before)
            linked(dve.tensor_scalar(rank[:], rank[:], float(TOPK), None, ALU.is_lt))
            dve.tensor_tensor(rank[:], rank[:], prob[:], ALU.mult).then_inc(comb, 1)


def run_experts(nc, A, featT, combT, R):
    with ExitStack() as ctx:
        m = Mem(nc, ctx, "exp")
        NQ = QT + 1
        w13 = m.sb("w13", [DH, 2, QT, 4, P])
        ws13 = m.sb("ws13", [DH, 2, 4, INTER])
        b13 = m.sb("b13", [P, NQ, 4])
        w2 = m.sb("w2", [P, QT, D])
        ws2 = m.sb("ws2", [INTER, D])
        b2 = m.sb("b2", [EXPERTS + 1, D])
        owner = m.sb("owner", [EXPERTS, QT, P])
        comb = [m.sb(f"comb{u}", [EXPERTS + 1, EP]) for u in range(2)]
        h1 = [m.sb(f"h1_{u}", [P, 2, EP]) for u in range(2)]
        hh = [m.sb(f"hh{u}", [P, 2, EP]) for u in range(2)]
        sg = [m.sb(f"sg{u}", [P, EP]) for u in range(2)]
        act_ = [m.sb(f"act{u}", [P, NQ, EP]) for u in range(2)]
        ps1 = [m.ps(f"ps1_{u}", [P, 2, EP]) for u in range(2)]
        ps3 = [m.ps(f"ps3_{u}", [P, 2, EP]) for u in range(2)]
        ps_w = [m.ps(f"ps_w{u}", [P, 512]) for u in range(2)]
        ps_o = [m.ps(f"ps_o{u}", [P, 512]) for u in range(2)]
        w_in, comb_in, mm, h1_done, hh_done, clipped, sg_in, sg_done, gated = (
            m.sem(n) for n in ("w_in", "comb_in", "mm", "h1_done", "hh_done", "clipped", "sg_in", "sg_done", "gated"))
        prod, lin, weighed, wmm, omm, added = (m.sem(n) for n in ("prod", "lin", "weighed", "wmm", "omm", "added"))
        block = ctx.enter_context(nc.Block())

        def rows(q):
            return P if q < QT else INTER

        def late(x, n):
            return not (isinstance(x, int) and x < n)

        def pieces(eng, piece):
            for c in range(3):
                piece(c, c % 2)
            with eng.Fori(1, (EPIECES - 1) // 2) as i:
                for u in range(2):
                    piece(2 * i + u + 1, 1 - u)

        @block.sync
        def _(sp):
            for t, n in ((w13, "e_w13"), (ws13, "e_ws13"), (b13, "e_b13"), (w2, "e_w2"), (ws2, "e_ws2"),
                         (b2, "e_b2"), (owner, "e_owner")):
                sp.dma_start(t[:], A[n]).then_inc(w_in, 16)

        @block.tensor
        def _(pe):
            def hidden(c, q, at):
                s = NQ * c + q
                u = at % 2
                if late(s, 2):
                    pe.wait_ge(h1_done, s - 1)
                    pe.wait_ge(hh_done, s - 1)
                for bank, first in ((ps1[u], 0), (ps3[u], 2)):
                    for g in range(2):
                        for h in range(2):
                            lhs = w13[:, h, q, first + g, :] if q < QT else ws13[:, h, first + g, :]
                            last = pe.matmul(bank[0:rows(q), g, :], lhs, featT[:, h, ds(c * EP, EP)],
                                             start=h == 0, stop=h == 1)
                last.then_inc(mm, 1)

            def spread(c, q, u, at):
                r = QT * c + q
                if late(r, 2):
                    pe.wait_ge(weighed, r - 1)
                pe.wait_ge(comb_in, c + 1)
                pe.matmul(ps_w[at % 2][:, 0:EP], owner[:, q, :], comb[u][0:EXPERTS, :], start=True, stop=True
                          ).then_inc(wmm, 1)

            def out(c, u):
                pe.wait_ge(weighed, QT * (c + 1))
                pe.wait_ge(gated, c + 1)
                for t in range(2):
                    if late(c, 1):
                        pe.wait_ge(added, 2 * (c - 1) + t + 1)
                    cols = slice(t * P, (t + 1) * P)
                    o = ps_o[t][:, 0:D]
                    for q in range(NQ):
                        pe.matmul(o, act_[u][0:rows(q), q, cols], w2[:, q, :] if q < QT else ws2[:], start=q == 0,
                                  stop=False)
                    pe.matmul(o, comb[u][:, cols], b2[:], start=False, stop=True).then_inc(omm, 1)

            pe.wait_ge(w_in, 16 * 7)

            def piece(c, u):
                for q in range(NQ):
                    hidden(c, q, NQ * u + q)
                    if q < QT:
                        spread(c, q, u, q)
                    if q == 2 and late(c, 1):
                        out(c - 1, 1 - u)

            pieces(pe, piece)
            out(EPIECES - 1, (EPIECES - 1) % 2)

        @block.scalar
        def _(act):
            def sigmoid(c, q, at):
                s = NQ * c + q
                u = at % 2
                act.wait_ge(clipped, s + 1)
                r = rows(q)
                act.activation(sg[u][0:r, :], hh[u][0:r, 0, :], ACT.Sigmoid, scale=ALPHA).then_inc(sg_done, 1)

            def piece(c, u):
                if late(c, 2):
                    act.wait_ge(omm, 2 * (c - 1))
                act.activation(comb[u][:], combT[:, ds(c * EP, EP)], ACT.Copy).then_inc(comb_in, 1)
                for q in range(NQ):
                    s = NQ * c + q
                    at = NQ * u + q
                    r = rows(q)
                    act.wait_ge(mm, s + 1)
                    if late(s, 2):
                        act.wait_ge(hh_done, s - 1)
                    for g in range(2):
                        last = act.activation(h1[at % 2][0:r, g, :], ps1[at % 2][0:r, g, :], ACT.Identity,
                                              bias=b13[0:r, q, g:g + 1])
                    last.then_inc(h1_done, 1)
                    if late(s, 1):
                        sigmoid(*((c, q - 1, at - 1) if q > 0 else (c - 1, NQ - 1, NQ * (1 - u) + NQ - 1)))

            act.wait_ge(w_in, 16 * 7)
            pieces(act, piece)
            sigmoid(EPIECES - 1, NQ - 1, NQ * ((EPIECES - 1) % 2) + NQ - 1)

        @block.vector
        def _(dve):
            def first(c, q, at):
                s = NQ * c + q
                u, r = at % 2, rows(q)
                dve.wait_ge(h1_done, s + 1)
                if late(s, 2):
                    dve.wait_ge(sg_done, s - 1)
                    if q == 1:
                        dve.wait_ge(gated, c)
                    else:
                        dve.wait_ge(sg_in, QT * c + max(q - 1, 0))
                for g in range(2):
                    last = dve.scalar_tensor_tensor(out=hh[u][0:r, g, :], in0=ps3[u][0:r, g, :],
                                                    scalar=b13[0:r, q, 2 + g:3 + g], in1=h1[u][0:r, g, :],
                                                    op0=ALU.add, op1=ALU.mult)
                last.then_inc(hh_done, 1)
                dve.wait_ge(hh_done, s + 1)
                dve.tensor_scalar(hh[u][0:r, 0, :], hh[u][0:r, 0, :], LIMIT, None, ALU.min).then_inc(clipped, 1)
                dve.tensor_scalar(hh[u][0:r, 1, :], hh[u][0:r, 1, :], LIMIT, -LIMIT, ALU.min, ALU.max).then_inc(lin, 1)
                dve.wait_ge(clipped, s + 1)
                dve.wait_ge(lin, s + 1)
                dve.scalar_tensor_tensor(out=hh[u][0:r, 1, :], in0=hh[u][0:r, 1, :], scalar=1.0, in1=hh[u][0:r, 0, :],
                                         op0=ALU.add, op1=ALU.mult).then_inc(prod, 1)

            def second(c, q, at, par):
                s = NQ * c + q
                u, r = at % 2, rows(q)
                dve.wait_ge(sg_done, s + 1)
                dve.wait_ge(prod, s + 1)
                if q == 0 and late(c, 2):
                    dve.wait_ge(omm, 2 * (c - 1))
                o = act_[par][0:r, q, :]
                last = dve.tensor_tensor(o, hh[u][0:r, 1, :], sg[u][0:r, :], ALU.mult)
                if q < QT:
                    last.then_inc(sg_in, 1)
                    dve.wait_ge(wmm, QT * c + q + 1)
                    dve.wait_ge(sg_in, QT * c + q + 1)
                    dve.tensor_tensor(o, o, ps_w[q % 2][:, 0:EP], ALU.mult).then_inc(weighed, 1)
                else:
                    last.then_inc(gated, 1)

            def add(c):
                for t in range(2):
                    dve.wait_ge(omm, 2 * c + t + 1)
                    r = R[:, ds(2 * c + t, 1), :].rearrange("p o c -> p (o c)")
                    dve.tensor_tensor(r, r, ps_o[t][:, 0:D], ALU.add).then_inc(added, 1)

            def piece(c, u):
                for q in range(NQ):
                    at = NQ * u + q
                    first(c, q, at)
                    if late(NQ * c + q, 1):
                        if q > 0:
                            second(c, q - 1, at - 1, u)
                        else:
                            second(c - 1, NQ - 1, NQ * (1 - u) + NQ - 1, 1 - u)
                    if q == 4 and late(c, 1):
                        add(c - 1)

            dve.wait_ge(w_in, 16 * 7)
            pieces(dve, piece)
            last_u = (EPIECES - 1) % 2
            second(EPIECES - 1, NQ - 1, NQ * last_u + NQ - 1, last_u)
            add(EPIECES - 1)


def experts(nc, A, R, ident):
    with ExitStack() as ctx:
        featT = ctx.enter_context(nc.sbuf_tensor("e_feat", [DH, 2, TOK], F32))
        combT = ctx.enter_context(nc.sbuf_tensor("e_comb", [EXPERTS + 1, TOK], F32))
        layer_norm(nc, "eln", ident, R, featT)
        gate_experts(nc, A, ident, featT, combT)
        run_experts(nc, A, featT, combT, R)



def to_tokens(nc, R, ident, featD):
    with ExitStack() as ctx:
        m = Mem(nc, ctx, "tt")
        feat = m.sb("feat", [DH, 2, TOK])
        ps_t = [m.ps(f"ps_t{u}", [P, 512]) for u in range(4)]
        loaded, ident_zero, ident_set = m.sem("loaded"), m.sem("ident_zero"), m.sem("ident_set")
        turned, copied = m.sem("turned"), m.sem("copied")
        block = ctx.enter_context(nc.Block())

        @block.sync
        def _(sp):
            for h in range(2):
                sp.dma_start(feat[:, h, :], featD[h]).then_inc(loaded, 16)

        @block.gpsimd
        def _(pool):
            pool.memset(ident[:], 0.0).then_inc(ident_zero, 1)
            pool.wait_ge(ident_zero, 1)
            pool.affine_select(out=ident[:], in_=ident[:], compare_op=ALU.not_equal, fill=1.0, base=0,
                               pattern=[[-1, P]], channel_multiplier=1).then_inc(ident_set, 1)

        @block.tensor
        def _(pe):
            pe.wait_ge(loaded, 32)
            pe.wait_ge(ident_set, 1)
            for t in range(TILES):
                if t >= 4:
                    pe.wait_ge(copied, t - 3)
                for h in range(2):
                    last = pe.transpose(ps_t[t % 4][:, h * DH:(h + 1) * DH], feat[:, h, t * P:(t + 1) * P],
                                        ident[0:DH, 0:DH])
                last.then_inc(turned, 1)

        @block.vector
        def _(dve):
            for t in range(TILES):
                dve.wait_ge(turned, t + 1)
                dve.tensor_copy(R[:, t, :], ps_t[t % 4][:, 0:D]).then_inc(copied, 1)


def store_tokens(nc, R, out):
    with ExitStack() as ctx:
        m = Mem(nc, ctx, "st")
        stored = m.sem("stored")
        block = ctx.enter_context(nc.Block())

        @block.sync
        def _(sp):
            sp.dma_start(out.rearrange("(t p) c -> p t c", p=P), R[:]).then_inc(stored, 16)
            sp.wait_ge(stored, 16)



def tower(nc, A, out):
    featD = nc.dram_tensor("feat_scratch", [2, DH, TOK], F32).ap()
    offD = nc.dram_tensor("offset_scratch", [IMGS, OFF_CH, POS], F32).ap()
    bcD = nc.dram_tensor("bc_scratch", [2, 2 * N_STATE, CT], F32).ap()
    tokenizer(nc, A, featD, offD)
    with ExitStack() as ctx:
        R = ctx.enter_context(nc.sbuf_tensor("R", [P, TILES, D], F32))
        ident = ctx.enter_context(nc.sbuf_tensor("ident", [P, P], F32))
        to_tokens(nc, R, ident, featD)
        mamba(nc, A, R, ident, bcD)
        routed_ffn(nc, A, R, ident)
        rotary_attention(nc, A, R, ident)
        experts(nc, A, R, ident)
        store_tokens(nc, R, out)



def layouts(inputs):
    a = {k: np.ascontiguousarray(np.asarray(v)) for k, v in inputs.items()}
    L = {}

    def halves(v):
        return v.reshape(2, DH).T

    L["patches"] = a["x"].reshape(IMGS, IN_CH, SIDE1, KS, SIDE1, KS).transpose(1, 3, 5, 0, 2, 4).reshape(-1, IMGS * PIX)
    L["ones"] = np.ones((1, GPIX + PT - PT_LAST), np.float32)
    L["stem_w"] = a["L0_tok_stem_w"].reshape(CH1, -1).T
    L["stem_b"] = a["L0_tok_stem_b"]
    for n in ("bn1_g", "bn1_b", "bn1_m", "bn1_v"):
        L[n] = a["L0_tok_" + n]
    L["off_w"] = a["L0_tok_off_w"].reshape(TAPS, 2, CH1, TAPS).transpose(2, 3, 1, 0).reshape(CH1, TAPS, OFF_CH)
    L["off_b"] = a["L0_tok_off_b"].reshape(TAPS, 2).T.reshape(OFF_CH, 1)
    tap, pos = np.arange(TAPS)[:, None], np.arange(POS)[None, :]
    L["grid"] = np.concatenate([KS * (pos // SIDE2) + tap // KS, KS * (pos % SIDE2) + tap % KS]).astype(np.float32)
    L["dcn_w"] = a["L0_tok_dcn_w"].reshape(D, CH1, TAPS).transpose(1, 2, 0)
    for n in ("bn2_g", "bn2_b", "bn2_m", "bn2_v", "dcn_b"):
        L[n] = halves(a["L0_tok_" + n])
    p = np.arange(PT)
    L["pix_xy"] = -np.stack([p % SIDE1] + [ROWS_K * k + p // SIDE1 for k in range(KT)], 1).astype(np.float32)

    L["norm_w"], L["norm_b"] = halves(a["L0_attn_norm_w"]), halves(a["L0_attn_norm_b"])
    L["in_w"] = a["L0_attn_in_w"].T.reshape(2, DH, 2 * D_INNER).transpose(1, 0, 2)
    L["conv_w"] = a["L0_attn_conv_w"].reshape(DT, P, KS).transpose(1, 0, 2)
    L["conv_b"], L["dt_b"], L["D"] = (a["L0_attn_" + n].reshape(DT, P).T for n in ("conv_b", "dt_b", "D"))
    L["xproj_w"] = a["L0_attn_xproj_w"].T.reshape(DT, P, XP).transpose(1, 0, 2)
    L["dt_w"] = a["L0_attn_dt_w"].T
    L["A_log"] = a["L0_attn_A_log"].reshape(DT, P, N_STATE).transpose(1, 0, 2)
    L["out_w"] = a["L0_attn_out_w"].T.reshape(DT, P, D).transpose(1, 0, 2)

    for n in ("g1", "b1", "g2", "b2"):
        L[n] = halves(a["L0_ffn_" + n])
    L["Wr"] = np.repeat(a["L0_ffn_Wr"].reshape(2, DH).T[:, :, None], DH, 2)
    L["br"] = a["L0_ffn_br"].reshape(1)

    def halves_w(w):
        return w.reshape(2, DH, -1).transpose(1, 0, 2)

    L["ffn_qkv_w"] = halves_w(np.concatenate([a["L0_ffn_W" + n] for n in "qkv"], 1))
    L["ffn_qkv_b"] = np.concatenate([halves(a["L0_ffn_b" + n]) for n in "qkv"], 1)
    f = np.arange(DH)[:, None]
    L["kmask"] = (f // HD == np.arange(HH)[None, :]).astype(np.float32)
    L["vmask"] = (np.arange(K3)[:, None] // POS == np.arange(D)[None, :] // HD % H3).astype(np.float32)
    L["ffn_om_w"] = halves_w(np.concatenate([a["L0_ffn_Wo"], a["L0_ffn_Wm"]], 1)).reshape(DH, 2, 2, D)
    L["ffn_om_b"] = np.stack([a["L0_ffn_bo"], a["L0_ffn_bm"]])[None]
    L["ffn_w1"] = halves_w(a["L0_ffn_W1"])
    L["ffn_b1"] = a["L0_ffn_bf1"].reshape(FT, P).T
    L["ffn_w2"] = a["L0_ffn_W2"].reshape(FT, P, D).transpose(1, 0, 2)
    L["ffn_b2"] = a["L0_ffn_bf2"]

    wq, wk, wv = a["L1_attn_w_qkv"].reshape(3, D, D)
    swap = np.arange(D) ^ 1
    L["rot_w"] = halves_w(np.concatenate([wq.T, wk.T, wv.T, wq[swap].T, wk[swap].T], 1))
    inv_freq = 1.0 / 10000.0 ** (np.arange(0, HD, 2, dtype=np.float32) / np.float32(HD))
    freqs = np.arange(POS, dtype=np.float32)[:, None] * inv_freq.astype(np.float32)[None, :]
    angle = np.repeat(freqs, 2, -1)[:, np.arange(DH) % HD].T
    sign = np.where(np.arange(DH) % 2 == 0, -1.0, 1.0)[:, None]
    L["rot_cs"] = np.stack([np.cos(angle), sign * np.sin(angle)], 1).astype(np.float32)
    L["proj_w"] = halves_w(a["L1_attn_w_proj"].T)
    L["proj_b"] = a["L1_attn_b_proj"]

    L["gate_w"] = halves_w(a["L1_ffn_gate_w"].T)
    L["gate_b"] = a["L1_ffn_gate_b"]
    for n, k in (("before", EXPERTS), ("before_g", GROUPS)):
        L[n] = (np.arange(k)[None, :] < np.arange(k)[:, None]).astype(np.float32)

    def tiles(w):
        n = w.shape[1]
        w = w.reshape(EXPERTS, n, INTER, 2).transpose(1, 3, 0, 2).reshape(n, 2, QT, P)
        return w.transpose(0, 2, 1, 3)

    w13 = np.concatenate([tiles(a["L1_ffn_W1"]), tiles(a["L1_ffn_W3"])], 2)
    L["e_w13"] = w13.reshape(2, DH, QT, 4, P).transpose(1, 0, 2, 3, 4)
    ws = np.stack([a["L1_ffn_Ws1"][:, 0::2], a["L1_ffn_Ws1"][:, 1::2],
                   a["L1_ffn_Ws3"][:, 0::2], a["L1_ffn_Ws3"][:, 1::2]], 1)
    L["e_ws13"] = ws.reshape(2, DH, 4, INTER).transpose(1, 0, 2, 3)
    b13 = np.zeros((P, QT + 1, 4), np.float32)
    b13[:, :QT] = np.concatenate([tiles(a["L1_ffn_B1"][:, None]), tiles(a["L1_ffn_B3"][:, None])], 2)[0].transpose(2, 0, 1)
    b13[:INTER, QT] = np.stack([a["L1_ffn_Bs1"][0::2], a["L1_ffn_Bs1"][1::2],
                                a["L1_ffn_Bs3"][0::2], a["L1_ffn_Bs3"][1::2]], 1)
    L["e_b13"] = b13
    L["e_w2"] = a["L1_ffn_W2"].reshape(QT, P, D).transpose(1, 0, 2)
    L["e_ws2"] = a["L1_ffn_Ws2"]
    L["e_b2"] = np.concatenate([a["L1_ffn_B2"], a["L1_ffn_Bs2"][None]])
    hidden = np.arange(QT * P).reshape(QT, P) // INTER
    L["e_owner"] = (np.arange(EXPERTS)[:, None, None] == hidden[None]).astype(np.float32)
    return {k: np.ascontiguousarray(v) for k, v in L.items()}


def kernel(**inputs):
    import concourse.bacc as bacc
    from concourse.bass_utils import run_bass_kernel_spmd

    nc = bacc.Bacc("TRN2", target_bir_lowering=False, num_devices=1)
    arrays, A = {}, {}
    for name, v in layouts(inputs).items():
        arrays["in_" + name] = v
        A[name] = nc.dram_tensor("in_" + name, v.shape, F32, kind="ExternalInput").ap()
    out = nc.dram_tensor("tokens_out", [TOK, D], F32, kind="ExternalOutput").ap()
    tower(nc, A, out)
    r = run_bass_kernel_spmd(nc, [arrays], core_ids=[0])
    return r.results[0]["tokens_out"].reshape(IMGS, POS, D)
```

```python
from contextlib import ExitStack

import concourse.bass as bass
from concourse import mybir
import numpy as np

F32 = mybir.dt.float32
ALU = mybir.AluOpType
ACT = mybir.ActivationFunctionType
AX_X = mybir.AxisListType.X
ds = bass.ds

IMGS = 64
IN_CH, IN_SIDE = 3, 96
KS = 4
SIDE1 = IN_SIDE // KS
PIX = SIDE1 * SIDE1
CH1 = 96
SIDE2 = SIDE1 // KS
POS = SIDE2 * SIDE2
TAPS = KS * KS
D = 192
DH = D // 2
TOK = IMGS * POS
P = 128
TILES = TOK // P
EPS = 1e-5
SLOPE = 0.01

STEM_K = IN_CH * TAPS + 1
HALF_P = P // 2
GRP = 4
GRPS = IMGS // GRP
ROWS_K = 5
PT = ROWS_K * SIDE1
KT = -(-SIDE1 // ROWS_K)
PT_LAST = (SIDE1 - (KT - 1) * ROWS_K) * SIDE1
SMP = TAPS * POS
HALF_SMP = SMP // 2
OFF_CH = 2 * TAPS
GPIX = GRP * PIX
GPOS = GRP * POS
CP_COLS = 384
CP_PIECES = GPIX // CP_COLS

N_STATE = 16
D_INNER = 2 * D
DT = D_INNER // P
DT_RANK = -(-D // 16)
XP = DT_RANK + 2 * N_STATE
CH_IMGS = 16
CHUNKS = IMGS // CH_IMGS
CT = CH_IMGS * POS
HC = CT // 2
COLS = 384
PIECES = TOK // COLS
FAR = 1e30

HEADS = 12
HD = D // HEADS
HH = HEADS // 2
H3 = 3
PAIRS = IMGS // 2
PAIR = 2 * POS
ROW_B = 64
PROWS = ROW_B + POS
K3 = H3 * POS
GS = HEADS // H3
KEEP = max(1, round(0.15 * POS))
PAD = 4
FFN = 4 * D
FT = FFN // P
RP = 8 * POS
RPIECES = TOK // RP
EXPERTS, TOPK, GROUPS, TOPK_GROUPS = 8, 2, 4, 2
INTER = 96
EG = 4
HT = EG * INTER // P
QT = EXPERTS // EG * HT
EP = 2 * P
EPIECES = TOK // EP
ALPHA, LIMIT = 1.702, 7.0
OUT_OF = 1e30



class Mem:

    def __init__(self, nc, ctx, tag):
        self.nc, self.ctx, self.tag, self.sems = nc, ctx, tag, []
        ctx.callback(self.clear)

    def clear(self):
        self.nc.clear_and_free_semaphores(self.sems)
        self.nc.all_engine_barrier()

    def sb(self, name, shape, dt=F32):
        return self.ctx.enter_context(self.nc.sbuf_tensor(f"{self.tag}_{name}", shape, dt))

    def ps(self, name, shape, dt=F32):
        return self.ctx.enter_context(self.nc.psum_tensor(f"{self.tag}_{name}", shape, dt))

    def sem(self, name):
        self.sems.append(self.nc.alloc_semaphore(name=f"{self.tag}_{name}"))
        return self.sems[-1]


class Weights:

    def __init__(self, nc, ctx, tag, tensors):
        self.loads, self.tensors = [], {}
        for name, (shape, src) in tensors.items():
            t = ctx.enter_context(nc.sbuf_tensor(f"{tag}_{name}", shape, F32))
            self.loads.append((t[:], src))
            self.tensors[name] = t

    def load(self, sp, ahead):
        for dst, src in self.loads:
            sp.dma_start(dst, src).then_inc(ahead, 16)
        sp.wait_ge(ahead, 16 * len(self.loads))


def tokenizer(nc, A, feat, offD):
    with ExitStack() as ctx:
        m = Mem(nc, ctx, "tok")
        w_stem = m.sb("w_stem", [P, CH1])
        bn_rows = m.sb("bn_rows", [P, 5, CH1])
        bn_inv = m.sb("bn_inv", [P, CH1])
        bn_tmp = m.sb("bn_tmp", [P, CH1])
        off_fold = m.sb("off_fold", [P, OFF_CH])
        off_parts = m.sb("off_parts", [P, GPOS])
        w_off = m.sb("w_off", [CH1, TAPS, OFF_CH])
        b_off = m.sb("b_off", [OFF_CH, 1])
        grid = m.sb("grid", [OFF_CH, POS])
        w_dcn = m.sb("w_dcn", [CH1, TAPS, D])
        bn2 = m.sb("bn2", [DH, 5, 2])
        bn2_inv = m.sb("bn2_inv", [DH, 2])
        bn2_tmp = m.sb("bn2_tmp", [DH, 2])
        bn2_add = m.sb("bn2_add", [DH, 2])
        pix_xy = m.sb("pix_xy", [PT, 1 + KT])
        patches = [m.sb(f"patches{u}", [P, GPIX // 2 + PT - PT_LAST]) for u in range(2)]
        cp_tmp = [m.sb(f"cp_tmp{u}", [CH1, CP_COLS]) for u in range(2)]
        stem_cp = m.sb("stem_cp", [CH1, GPIX])
        coords = m.sb("coords", [OFF_CH, GRP, POS])
        coords_b = [m.sb(f"coords_b{u}", [PT, GRP, 2, SMP]) for u in range(2)]
        hat_x = [m.sb(f"hat_x{u}", [PT, GRP, SMP]) for u in range(2)]
        hat_y = [m.sb(f"hat_y{u}", [PT, KT, SMP]) for u in range(2)]
        wts = [m.sb(f"wts{u}", [PT, KT, SMP]) for u in range(2)]
        pt_tmp = [m.sb(f"pt_tmp{u}", [PT, KT, CH1]) for u in range(2)]
        stem_pt = [m.sb(f"stem_pt{u}", [PT, KT, CH1]) for u in range(2)]
        sampled = [m.sb(f"sampled{u}", [CH1, TAPS, GRP, POS]) for u in range(2)]
        dcn_tmp = m.sb("dcn_tmp", [DH, 2, GPOS])
        ps_cp = [m.ps(f"ps_cp{u}", [CH1, 512]) for u in range(2)]
        ps_off = m.ps("ps_off", [P, 512])
        ps_pt = [m.ps(f"ps_pt{u}", [PT, 512]) for u in range(2)]
        ps_smp = [m.ps(f"ps_smp{u}", [CH1, 512]) for u in range(2)]
        ps_dcn = m.ps("ps_dcn", [DH, 512])

        bn_loaded, bn2_loaded, w_loaded, w_dcn_in = (
            m.sem(n) for n in ("bn_loaded", "bn2_loaded", "w_loaded", "w_dcn_in"))
        var_ready = m.sem("var_ready")
        std_ready = m.sem("std_ready")
        fold = m.sem("fold")
        bias_row = m.sem("bias_row")
        patches_in = [m.sem(f"patches_in{u}") for u in range(2)]
        cp_mm, cp_copied, cp_done = m.sem("cp_mm"), m.sem("cp_copied"), m.sem("cp_done")
        off_mm, off_done, off_stored = m.sem("off_mm"), m.sem("off_done"), m.sem("off_stored")
        off_copied, off_summed = m.sem("off_copied"), m.sem("off_summed")
        coords0_in = [m.sem(f"coords0_in{u}") for u in range(2)]
        coords_in = [m.sem(f"coords_in{u}") for u in range(2)]
        absx_done, hatx_done = m.sem("absx_done"), m.sem("hatx_done")
        coords_used = m.sem("coords_used")
        absy_done, haty_done, wts_done = m.sem("absy_done"), m.sem("haty_done"), m.sem("wts_done")
        pt_mm, pt_copied, pt_done = m.sem("pt_mm"), m.sem("pt_copied"), m.sem("pt_done")
        smp_mm, smp_copied = m.sem("smp_mm"), m.sem("smp_copied")
        dcn_mm, dcn_copied, dcn_done = m.sem("dcn_mm"), m.sem("dcn_copied"), m.sem("dcn_done")
        pad_set, coords_free = m.sem("pad_set"), m.sem("coords_free")
        BN_LOADS, BN2_LOADS, SMALL_LOADS = 16 * 7, 16 * 5, 16 * 7
        tops = [0, HALF_P]

        block = ctx.enter_context(nc.Block())

        @block.sync
        def _(sp):
            for k, name in enumerate(("bn1_g", "bn1_b", "bn1_m", "bn1_v", "stem_b")):
                sp.dma_start(bn_rows[:, k, :], A[name].partition_broadcast(P)).then_inc(bn_loaded, 16)
            for top in tops:
                sp.dma_start(w_stem[top:top + STEM_K - 1, :], A["stem_w"]).then_inc(bn_loaded, 16)
            for k, name in enumerate(("bn2_g", "bn2_b", "bn2_m", "bn2_v", "dcn_b")):
                sp.dma_start(bn2[:, k, :], A[name]).then_inc(bn2_loaded, 16)
            for dst, src in ((pix_xy[:], A["pix_xy"]), (w_off[:], A["off_w"]), (off_fold[:], A["off_fold"]),
                             (b_off[:], A["off_b"]), (grid[:], A["grid"])):
                sp.dma_start(dst, src).then_inc(w_loaded, 16)
            for top in tops:
                sp.dma_start(patches[0][top + STEM_K - 1:top + STEM_K, :], A["ones"][:, 0:GPIX // 2 + PT - PT_LAST]
                             ).then_inc(w_loaded, 16)
            sp.wait_ge(fold, 4)
            for top in tops:
                sp.dma_start(w_stem[top + STEM_K - 1:top + STEM_K, :], bn_tmp[0:1, :]).then_inc(bias_row, 16)
            sp.dma_start(w_dcn[:], A["dcn_w"]).then_inc(w_dcn_in, 16)

            def exchange(g, u):
                sp.wait_ge(off_done, g + 1)
                sp.dma_start(offD[ds(g * GRP, GRP)].rearrange("i c p -> c i p"), coords[:]).then_inc(off_stored, 16)
                sp.wait_ge(off_stored, 16 * (g + 1))
                sp.dma_start(coords_b[u][:, 0].rearrange("p y s -> p (y s)"),
                             offD[ds(g * GRP, 1)].rearrange("i c p -> (i c p)").partition_broadcast(PT)
                             ).then_inc(coords0_in[u], 16)
                sp.dma_start(coords_b[u][:, 1:].rearrange("p i y s -> p (i y s)"),
                             offD[ds(g * GRP + 1, GRP - 1)].rearrange("i c p -> (i c p)").partition_broadcast(PT)
                             ).then_inc(coords_in[u], 16)

            exchange(0, 0)
            exchange(1, 1)
            with sp.Fori(1, GRPS // 2) as i:
                for u in range(2):
                    sp.wait_ge(coords_used, 2 * i + u - 1)
                    sp.sem_inc(coords_free, 1)
                    exchange(2 * i + u, u)

        @block.gpsimd
        def _(pool):
            def load(g, u):
                for odd, top in enumerate(tops):
                    pool.dma_start(patches[u][top:top + STEM_K - 1, 0:GPIX // 2],
                                   A["patches"][odd, :, ds(g * (GPIX // 2), GPIX // 2)]).then_inc(patches_in[u], 16)

            for u in range(2):
                for top in tops:
                    pool.memset(patches[u][top:top + STEM_K - 1, GPIX // 2:], 0.0).then_inc(pad_set, 1)
            for top in tops:
                pool.dma_start(patches[1][top + STEM_K - 1:top + STEM_K, :], A["ones"][:, 0:GPIX // 2 + PT - PT_LAST]
                               ).then_inc(patches_in[1], 16)
            load(0, 0)
            load(1, 1)
            with pool.Fori(1, GRPS // 2) as i:
                for u in range(2):
                    pool.wait_ge(pt_mm, GRP * (2 * i + u - 1))
                    load(2 * i + u, u)

        @block.tensor
        def _(pe):
            def stem_cp_mm(g, u, i, pair):
                pe.wait_ge(patches_in[u], 32 * (i + 1 + u))
                for q in (2 * pair, 2 * pair + 1):
                    if q % 2 == 0 and (q >= 2 or not isinstance(g, int) or g > 0):
                        pe.wait_ge(cp_copied, CP_PIECES * g + q)
                    rows = slice(tops[q % 2], tops[q % 2] + STEM_K)
                    pe.matmul(ps_cp[q % 2][:, 0:CP_COLS], w_stem[rows, :],
                              patches[u][rows, q // 2 * CP_COLS:(q // 2 + 1) * CP_COLS],
                              start=True, stop=True).then_inc(cp_mm, 1)

            def off_mm_(g):
                pe.wait_ge(cp_done, CP_PIECES * (g + 1))
                if not isinstance(g, int) or g > 0:
                    pe.wait_ge(off_copied, g)
                px = stem_cp[:].rearrange("c (r ky q kx) -> c r ky q kx", ky=KS, kx=KS, q=SIDE2)
                for t in range(TAPS):
                    rows = slice(t % 4 * OFF_CH, (t % 4 + 1) * OFF_CH)
                    last = pe.matmul(ps_off[rows, 0:GPOS], w_off[:, t, :], px[:, :, t // KS, :, t % KS],
                                     start=t < 4, stop=t >= TAPS - 4)
                last.then_inc(off_mm, 1)

            def off_sum(g):
                pe.wait_ge(off_copied, g + 1)
                if not isinstance(g, int) or g > 0:
                    pe.wait_ge(off_done, g)
                pe.matmul(ps_off[0:OFF_CH, GPOS:2 * GPOS], off_fold[:], off_parts[:], start=True, stop=True
                          ).then_inc(off_summed, 1)

            def stem_pt_mm(g, u, j, i):
                n = GRP * g + j
                if not isinstance(n, int) or n > 0:
                    pe.wait_ge(pt_copied, n)
                pe.wait_ge(patches_in[u], 32 * (i + 1 + u))
                for k in range(KT):
                    for odd in range(2):
                        rows = slice(tops[odd], tops[odd] + STEM_K)
                        at = j // 2 * PIX + k * PT
                        last = pe.matmul(ps_pt[odd][:, k * CH1:(k + 1) * CH1], patches[u][rows, at:at + PT],
                                         w_stem[rows, :], start=True, stop=True)
                        if k == KT - 1:
                            last.then_inc(pt_mm, 1)

            def sample_mm(g, u, j, h):
                n = GRP * g + j
                if h == 0:
                    pe.wait_ge(pt_done, n + 1)
                    pe.wait_ge(wts_done, n + 1)
                if not isinstance(n, int) or n > 0:
                    pe.wait_ge(smp_copied, 2 * n + h - 1)
                for k in range(KT):
                    rows = PT if k < KT - 1 else PT_LAST
                    last = pe.matmul(ps_smp[h][:, 0:HALF_SMP], stem_pt[j % 2][0:rows, k, :],
                                     wts[j % 2][0:rows, k, h * HALF_SMP:(h + 1) * HALF_SMP],
                                     start=k == 0, stop=k == KT - 1)
                last.then_inc(smp_mm, 1)

            def dcn_half(g, u, h):
                if isinstance(g, int) and g == 0 and h == 0:
                    pe.wait_ge(w_dcn_in, 16)
                if h == 0:
                    pe.wait_ge(smp_copied, 2 * GRP * (g + 1))
                    pe.wait_ge(dcn_copied, g + 1)
                for t in range(TAPS):
                    last = pe.matmul(ps_dcn[:, h * GPOS:(h + 1) * GPOS], w_dcn[:, t, h * DH:(h + 1) * DH],
                                     sampled[u][:, t, :, :], start=t == 0, stop=t == TAPS - 1)
                if h == 1:
                    last.then_inc(dcn_mm, 1)

            def step(g, u, j, front, dcn, i):
                if j == 1:
                    stem_pt_mm(g, u, 2, i)
                if j == GRP - 1 and front:
                    stem_pt_mm(g + 1, 1 - u, 0, i + u)
                if j == 0 and front:
                    stem_cp_mm(g + 1, 1 - u, i + u, 0)
                if j >= GRP - 2 and dcn:
                    dcn_half(g - 1, 1 - u, j - (GRP - 2))
                sample_mm(g, u, j, 0)
                if j == 0 and front:
                    stem_cp_mm(g + 1, 1 - u, i + u, 1)
                if j == 1 and front:
                    off_mm_(g + 1)
                sample_mm(g, u, j, 1)
                if j == 1 and front:
                    off_sum(g + 1)
                if j == 0 and front:
                    stem_cp_mm(g + 1, 1 - u, i + u, 2)

            def steps(g, u, i, front=True, dcn=True):
                for j in range(GRP):
                    step(g, u, j, front, dcn, i)

            pe.sem_inc(dcn_mm, 1)
            pe.wait_ge(w_loaded, SMALL_LOADS)
            pe.wait_ge(bias_row, 32)
            pe.wait_ge(fold, 6)
            pe.wait_ge(pad_set, 4)
            for pair in range(3):
                stem_cp_mm(0, 0, 0, pair)
            stem_pt_mm(0, 0, 0, 0)
            off_mm_(0)
            off_sum(0)
            steps(0, 0, 0, dcn=False)
            steps(1, 1, 0)
            with pe.Fori(1, GRPS // 2 - 1) as i:
                steps(2 * i, 0, i)
                steps(2 * i + 1, 1, i)
            steps(GRPS - 2, 0, GRPS // 2 - 1)
            steps(GRPS - 1, 1, GRPS // 2 - 1, front=False)
            for h in range(2):
                dcn_half(GRPS - 1, 1, h)

        @block.scalar
        def _(act):
            def cp_copy(g, pair):
                for q in (2 * pair, 2 * pair + 1):
                    act.wait_ge(cp_mm, CP_PIECES * g + q + 1)
                    if q >= 2 or not isinstance(g, int) or g > 0:
                        act.wait_ge(cp_done, CP_PIECES * g + q - 1)
                    act.activation(cp_tmp[q % 2][:], ps_cp[q % 2][:, 0:CP_COLS], ACT.Copy).then_inc(cp_copied, 1)

            def pt_copy(g, j):
                n = GRP * g + j
                act.wait_ge(pt_mm, n + 1)
                if not isinstance(n, int) or n >= 2:
                    act.wait_ge(pt_done, n - 1)
                act.activation(pt_tmp[j % 2][:].rearrange("p k c -> p (k c)"), ps_pt[j % 2][:, 0:KT * CH1], ACT.Copy
                               ).then_inc(pt_copied, 1)

            def abs_x(g, u, i, part):
                imgs = slice(0, 1) if part == 0 else slice(1, GRP)
                if part == 0:
                    act.wait_ge(coords0_in[u], 16 * (i + 1))
                    if not isinstance(g, int) or g >= 2:
                        act.wait_ge(wts_done, GRP * (g - 1))
                else:
                    act.wait_ge(coords_in[u], 16 * (i + 1))
                act.activation(hat_x[u][:, imgs], coords_b[u][:, imgs, 1, :], ACT.Abs, bias=pix_xy[:, 0:1]
                               ).then_inc(absx_done, 1)

            def abs_y(g, u, j):
                n = GRP * g + j
                if not isinstance(n, int) or n >= 2:
                    act.wait_ge(wts_done, n - 1)
                for k in range(KT):
                    last = act.activation(hat_y[j % 2][:, k, :], coords_b[u][:, j, 0, :], ACT.Abs,
                                          bias=pix_xy[:, 1 + k:2 + k])
                last.then_inc(absy_done if j < GRP - 1 else coords_used, 1)

            def smp_copy(g, u, j, h):
                n = GRP * g + j
                if j == 0 and h == 0 and (not isinstance(g, int) or g >= 2):
                    act.wait_ge(dcn_mm, g)
                act.wait_ge(smp_mm, 2 * n + h + 1)
                act.activation(sampled[u][:, h * TAPS // 2:(h + 1) * TAPS // 2, j, :],
                               ps_smp[h][:, 0:HALF_SMP].rearrange("c (t q) -> c t q", q=POS), ACT.Copy
                               ).then_inc(smp_copied, 1)

            def off_copy(g):
                act.wait_ge(off_mm, g + 1)
                if not isinstance(g, int) or g > 0:
                    act.wait_ge(off_summed, g)
                act.activation(off_parts[:], ps_off[:, 0:GPOS], ACT.Copy).then_inc(off_copied, 1)

            def dcn_copy(g):
                act.wait_ge(dcn_mm, g + 2)
                act.wait_ge(dcn_done, g + 1)
                for h in range(2):
                    last = act.activation(dcn_tmp[:, h, :], ps_dcn[:, h * GPOS:(h + 1) * GPOS], ACT.Identity,
                                          scale=bn2_inv[:, h:h + 1], bias=bn2_add[:, h:h + 1])
                last.then_inc(dcn_copied, 1)

            def step(g, u, j, nxt, front, dcn, i):
                if nxt:
                    g2, u2, j2 = (g, u, j + 1) if j < GRP - 1 else (g + 1, 1 - u, 0)
                    pt_copy(g2, j2)
                if front and j == 0:
                    cp_copy(g + 1, 0)
                if nxt:
                    if j2 == 0:
                        abs_x(g2, u2, i + u, 0)
                    abs_y(g2, u2, j2)
                    if j2 == 0:
                        abs_x(g2, u2, i + u, 1)
                smp_copy(g, u, j, 0)
                if front and j == 0:
                    cp_copy(g + 1, 1)
                if front and j == 1:
                    off_copy(g + 1)
                smp_copy(g, u, j, 1)
                if front and j == 0:
                    cp_copy(g + 1, 2)
                if dcn and j == GRP - 1:
                    dcn_copy(g - 1)

            def rest(g, u, more, i, dcn=True):
                for j in range(1, GRP):
                    step(g, u, j, True, j == 1, dcn, i)
                step(g + 1, 1 - u, 0, True, more, False, i + u)

            act.sem_inc(dcn_copied, 1)
            act.wait_ge(var_ready, 2)
            act.activation(bn_inv[:], bn_tmp[:], ACT.Sqrt).then_inc(std_ready, 1)
            act.activation(bn2_inv[:], bn2_tmp[:], ACT.Sqrt).then_inc(std_ready, 1)
            act.wait_ge(fold, 7)
            act.wait_ge(w_loaded, SMALL_LOADS)
            for pair in range(3):
                cp_copy(0, pair)
            pt_copy(0, 0)
            off_copy(0)
            abs_x(0, 0, 0, 0)
            abs_y(0, 0, 0)
            abs_x(0, 0, 0, 1)
            step(0, 0, 0, True, True, False, 0)
            rest(0, 0, True, 0, False)
            rest(1, 1, True, 0)
            with act.Fori(1, GRPS // 2 - 1) as i:
                rest(2 * i, 0, True, i)
                rest(2 * i + 1, 1, True, i)
            rest(GRPS - 2, 0, False, GRPS // 2 - 1)
            for j in range(1, GRP):
                step(GRPS - 1, 1, j, j < GRP - 1, False, True, GRPS // 2 - 1)
            dcn_copy(GRPS - 1)

        @block.vector
        def _(dve):
            def leaky(out, x):
                return dve.scalar_tensor_tensor(out=out, in0=x, scalar=SLOPE, in1=x, op0=ALU.mult, op1=ALU.max)

            def cp_leaky(g, pair):
                if not isinstance(g, int) or g > 0:
                    dve.wait_ge(off_mm, g)
                for q in (2 * pair, 2 * pair + 1):
                    dve.wait_ge(cp_copied, CP_PIECES * g + q + 1)
                    at = q % 2 * (GPIX // 2) + q // 2 * CP_COLS
                    leaky(stem_cp[:, at:at + CP_COLS], cp_tmp[q % 2][:]).then_inc(cp_done, 1)

            def off_add(g):
                dve.wait_ge(off_summed, g + 1)
                if not isinstance(g, int) or g > 0:
                    dve.wait_ge(off_stored, 16 * g)
                sums = ps_off[0:OFF_CH, GPOS:2 * GPOS].rearrange("c (o i q) -> c o i q", o=2, q=POS)
                for odd in range(2):
                    last = dve.scalar_tensor_tensor(out=coords[:, odd:GRP:2, :], in0=sums[:, odd], scalar=b_off[:, 0:1],
                                                    in1=grid[:].unsqueeze(1).to_broadcast([OFF_CH, GRP // 2, POS]),
                                                    op0=ALU.add, op1=ALU.add)
                last.then_inc(off_done, 1)

            def pt_leaky(g, j):
                n = GRP * g + j
                dve.wait_ge(pt_copied, n + 1)
                if not isinstance(n, int) or n >= 2:
                    dve.wait_ge(smp_mm, 2 * (n - 1))
                leaky(stem_pt[j % 2][:], pt_tmp[j % 2][:]).then_inc(pt_done, 1)

            def hat_x_(g, u, part):
                imgs = slice(0, 1) if part == 0 else slice(1, GRP)
                dve.wait_ge(absx_done, 2 * g + part + 1)
                dve.tensor_scalar(hat_x[u][:, imgs], hat_x[u][:, imgs], 1.0, 1.0, ALU.min, ALU.subtract).then_inc(hatx_done, 1)

            def weights(g, u, j):
                n = GRP * g + j
                if j < GRP - 1:
                    dve.wait_ge(absy_done, (GRP - 1) * g + j + 1)
                else:
                    dve.wait_ge(coords_used, g + 1)
                dve.tensor_scalar(hat_y[j % 2][:], hat_y[j % 2][:], 1.0, 1.0, ALU.min, ALU.subtract).then_inc(haty_done, 1)
                dve.wait_ge(haty_done, n + 1)
                dve.wait_ge(hatx_done, 2 * g + (1 if j == 0 else 2))
                if not isinstance(n, int) or n >= 2:
                    dve.wait_ge(smp_mm, 2 * (n - 1))
                dve.tensor_tensor(wts[j % 2][:], hat_y[j % 2][:],
                                  hat_x[u][:, j, :].unsqueeze(1).to_broadcast([PT, KT, SMP]), ALU.mult).then_inc(wts_done, 1)

            def dcn_leaky(g):
                dve.wait_ge(dcn_copied, g + 2)
                leaky(feat[:, :, ds(g * GPOS, GPOS)], dcn_tmp[:]).then_inc(dcn_done, 1)

            def step(g, u, j, nxt, front, dcn, i):
                if nxt:
                    g2, u2, j2 = (g, u, j + 1) if j < GRP - 1 else (g + 1, 1 - u, 0)
                    pt_leaky(g2, j2)
                if front and j == 0:
                    cp_leaky(g + 1, 0)
                if nxt:
                    if j2 == 0:
                        hat_x_(g2, u2, 0)
                    weights(g2, u2, j2)
                    if j2 == 0:
                        hat_x_(g2, u2, 1)
                if front and j == 0:
                    cp_leaky(g + 1, 1)
                    cp_leaky(g + 1, 2)
                if front and j == 1:
                    off_add(g + 1)
                if dcn and j == GRP - 1:
                    dcn_leaky(g - 1)

            def rest(g, u, more, i, dcn=True):
                for j in range(1, GRP):
                    step(g, u, j, True, j == 1, dcn, i)
                step(g + 1, 1 - u, 0, True, more, False, i + u)

            dve.sem_inc(dcn_done, 1)
            dve.wait_ge(bn_loaded, BN_LOADS)
            dve.tensor_scalar(bn_tmp[:], bn_rows[:, 3, :], EPS, None, ALU.add).then_inc(var_ready, 1)
            dve.wait_ge(bn2_loaded, BN2_LOADS)
            dve.tensor_scalar(bn2_tmp[:], bn2[:, 3, :], EPS, None, ALU.add).then_inc(var_ready, 1)
            dve.wait_ge(std_ready, 2)
            dve.reciprocal(bn_tmp[:], bn_inv[:]).then_inc(fold, 1)
            dve.wait_ge(fold, 1)
            dve.tensor_tensor(bn_inv[:], bn_tmp[:], bn_rows[:, 0, :], ALU.mult).then_inc(fold, 1)
            dve.wait_ge(fold, 2)
            dve.tensor_tensor(bn_tmp[:], bn_rows[:, 4, :], bn_rows[:, 2, :], ALU.subtract).then_inc(var_ready, 1)
            dve.wait_ge(var_ready, 3)
            dve.tensor_tensor(bn_tmp[:], bn_tmp[:], bn_inv[:], ALU.mult).then_inc(fold, 1)
            dve.wait_ge(fold, 3)
            dve.tensor_tensor(bn_tmp[:], bn_tmp[:], bn_rows[:, 1, :], ALU.add).then_inc(fold, 1)
            for top in tops:
                rows = slice(top, top + STEM_K - 1)
                last = dve.tensor_tensor(w_stem[rows, :], w_stem[rows, :], bn_inv[rows, :], ALU.mult)
            last.then_inc(fold, 1)
            dve.reciprocal(bn2_tmp[:], bn2_inv[:]).then_inc(var_ready, 1)
            dve.wait_ge(var_ready, 4)
            dve.tensor_tensor(bn2_inv[:], bn2_tmp[:], bn2[:, 0, :], ALU.mult).then_inc(fold, 1)
            dve.tensor_tensor(bn2_add[:], bn2[:, 4, :], bn2[:, 2, :], ALU.subtract).then_inc(var_ready, 1)
            dve.wait_ge(fold, 6)
            dve.wait_ge(var_ready, 5)
            dve.tensor_tensor(bn2_add[:], bn2_add[:], bn2_inv[:], ALU.mult).then_inc(var_ready, 1)
            dve.wait_ge(var_ready, 6)
            dve.tensor_tensor(bn2_add[:], bn2_add[:], bn2[:, 1, :], ALU.add).then_inc(fold, 1)
            dve.wait_ge(w_loaded, SMALL_LOADS)
            for pair in range(3):
                cp_leaky(0, pair)
            pt_leaky(0, 0)
            off_add(0)
            hat_x_(0, 0, 0)
            weights(0, 0, 0)
            hat_x_(0, 0, 1)
            step(0, 0, 0, True, True, False, 0)
            rest(0, 0, True, 0, False)
            rest(1, 1, True, 0)
            with dve.Fori(1, GRPS // 2 - 1) as i:
                rest(2 * i, 0, True, i)
                rest(2 * i + 1, 1, True, i)
            rest(GRPS - 2, 0, False, GRPS // 2 - 1)
            for j in range(1, GRP):
                step(GRPS - 1, 1, j, j < GRP - 1, False, True, GRPS // 2 - 1)
            dcn_leaky(GRPS - 1)



def layer_norm(nc, tag, ident, src, featT, x1=None, add_to=None, affine=None, twice=False, following=None):
    with ExitStack() as ctx:
        m = Mem(nc, ctx, tag)
        stats = m.sb("stats", [P, TILES, 6])
        mv = m.sb("mv", [P, TILES, 2])
        ve, sd, r1 = (m.sb(n, [P, TILES]) for n in ("ve", "sd", "r1"))
        v2, sd2, r2 = (m.sb(n, [P, TILES]) for n in ("v2", "sd2", "r2"))
        x1 = x1 if x1 is not None else m.sb("x1", [P, TILES, D])
        x2 = m.sb("x2", [P, TILES, D]) if twice else x1
        mr = m.sb("mr", [P, TILES])
        gb = m.sb("gb", [DH, 2, 2])
        QUADS = -(-TILES // 4)
        ps_t = [m.ps(f"ps_t{u}", [DH, 512]) for u in range(4)]
        stat, link, var_in, sd_out = m.sem("stat"), m.sem("link"), m.sem("var_in"), m.sem("sd_out")
        gb_in, normed, turned = m.sem("gb_in"), m.sem("normed"), m.sem("turned")
        copied = [m.sem(f"copied{h}") for h in range(2)]
        x1_done, added, mr_done = m.sem("x1_done"), m.sem("added"), m.sem("mr_done")
        ahead = m.sem("ahead")
        block = ctx.enter_context(nc.Block())

        @block.sync
        def _(sp):
            if affine:
                for k in range(2):
                    sp.dma_start(gb[:, k, :], affine[k]).then_inc(gb_in, 16)
                sp.wait_ge(gb_in, 32)
            if following:
                following.load(sp, ahead)

        @block.gpsimd
        def _(pool):
            if add_to is not None:
                if twice:
                    pool.wait_ge(x1_done, TILES)
                pool.wait_ge(normed, TILES)
                pool.tensor_tensor(add_to[:], add_to[:], x1[:], ALU.add).then_inc(added, 1)

        @block.scalar
        def _(act):
            act.wait_ge(var_in, 1)
            act.activation(sd[:], ve[:], ACT.Sqrt).then_inc(sd_out, 1)
            if twice:
                act.wait_ge(var_in, 2)
                act.activation(sd2[:], v2[:], ACT.Sqrt).then_inc(sd_out, 1)
            act.wait_ge(mr_done, 1)
            for t in range(0 if twice else 1, TILES, 1 if twice else 2):
                act.activation(x1[:, t, :], src[:, t, :], ACT.Identity, scale=r1[:, t:t + 1], bias=mr[:, t:t + 1]
                               ).then_inc(x1_done, 1)
            if affine:
                act.wait_ge(gb_in, 32)
            for q in range(QUADS):
                w = min(4, TILES - 4 * q) * P
                act.wait_ge(turned, 2 * q + 1)
                o, i = featT[:, 0, 4 * q * P:4 * q * P + w], ps_t[(2 * q) % 4][:, 0:w]
                if affine:
                    act.activation(o, i, ACT.Identity, scale=gb[:, 0, 0:1], bias=gb[:, 1, 0:1]).then_inc(copied[0], 1)
                else:
                    act.activation(o, i, ACT.Copy).then_inc(copied[0], 1)

        @block.tensor
        def _(pe):
            for q in range(QUADS):
                n = min(4, TILES - 4 * q)
                if twice:
                    pe.wait_ge(normed, 4 * q + n)
                else:
                    pe.wait_ge(normed, (4 * q + n) // 2)
                    pe.wait_ge(x1_done, (4 * q + n) // 2)
                for h in range(2):
                    if q >= 2:
                        pe.wait_ge(copied[h], q - 1)
                    for k in range(n):
                        last = pe.transpose(ps_t[(2 * q + h) % 4][:, k * P:(k + 1) * P],
                                            x2[:, 4 * q + k, h * DH:(h + 1) * DH], ident[:])
                    last.then_inc(turned, 1)

        @block.vector
        def _(dve):
            n_link = [0]

            def linked(ins):
                n_link[0] += 1
                ins.then_inc(link, 1)
                dve.wait_ge(link, n_link[0])

            for t in range(TILES):
                dve.bn_stats(stats[:, t, :], src[:, t, :]).then_inc(stat, 1)
            for t in range(TILES):
                dve.wait_ge(stat, t + 1)
                dve.bn_aggr(mv[:, t, :], stats[:, t, :]).then_inc(stat, 1)
            dve.wait_ge(stat, 2 * TILES)
            dve.tensor_scalar(ve[:], mv[:, :, 1], EPS, None, ALU.add).then_inc(var_in, 1)
            dve.wait_ge(sd_out, 1)
            linked(dve.reciprocal(r1[:], sd[:]))
            dve.scalar_tensor_tensor(out=mr[:], in0=mv[:, :, 0], scalar=-1.0, in1=r1[:], op0=ALU.mult, op1=ALU.mult
                                     ).then_inc(mr_done, 1)
            if twice:
                linked(dve.reciprocal(v2[:], ve[:]))
                linked(dve.tensor_tensor(v2[:], v2[:], mv[:, :, 1], ALU.mult))
                n_link[0] += 1
                dve.tensor_scalar(sd2[:], v2[:], EPS, None, ALU.add).then_inc(link, 1)
                dve.wait_ge(link, n_link[0])
                dve.tensor_copy(v2[:], sd2[:]).then_inc(var_in, 1)
                dve.wait_ge(sd_out, 2)
                linked(dve.reciprocal(r2[:], sd2[:]))
                linked(dve.tensor_tensor(r2[:], r2[:], r1[:], ALU.mult))
            for t in range(0, TILES, 1 if twice else 2):
                dve.tensor_scalar(x2[:, t, :], src[:, t, :], mv[:, t, 0:1], (r2 if twice else r1)[:, t:t + 1],
                                  ALU.subtract, ALU.mult).then_inc(normed, 1)
            if affine:
                dve.wait_ge(gb_in, 32)
            for q in range(QUADS):
                w = min(4, TILES - 4 * q) * P
                dve.wait_ge(turned, 2 * q + 2)
                o, i = featT[:, 1, 4 * q * P:4 * q * P + w], ps_t[(2 * q + 1) % 4][:, 0:w]
                if affine:
                    dve.tensor_scalar(o, i, gb[:, 0, 1:2], gb[:, 1, 1:2], ALU.mult, ALU.add).then_inc(copied[1], 1)
                else:
                    dve.tensor_copy(o, i).then_inc(copied[1], 1)


def in_projection(nc, W, featT, u_pre, z_gate, following):
    with ExitStack() as ctx:
        m = Mem(nc, ctx, "inp")
        w = W.tensors["w"]
        ps = [m.ps(f"ps{k}", [P, 512]) for k in range(2 * DT)]
        mm = m.sem("mm")
        u_copied, z_copied, ahead = m.sem("u_copied"), m.sem("z_copied"), m.sem("ahead")
        block = ctx.enter_context(nc.Block())

        @block.sync
        def _(sp):
            following.load(sp, ahead)

        @block.tensor
        def _(pe):
            with pe.Fori(0, PIECES) as c:
                for k in range(2 * DT):
                    pe.wait_ge(u_copied if k < DT else z_copied, DT * c + k % DT + 1)
                    for h in range(2):
                        last = pe.matmul(ps[k][:, 0:COLS], w[:, h, k * P:(k + 1) * P], featT[:, h, ds(c * COLS, COLS)],
                                         start=h == 0, stop=h == 1)
                    last.then_inc(mm, 1)

        @block.scalar
        def _(act):
            act.sem_inc(z_copied, DT)
            with act.Fori(0, PIECES) as c:
                for k in range(DT):
                    act.wait_ge(mm, 2 * DT * c + DT + k + 1)
                    act.activation(z_gate[:, k, ds(c * COLS, COLS)], ps[DT + k][:, 0:COLS], ACT.Silu).then_inc(z_copied, 1)

        @block.vector
        def _(dve):
            dve.sem_inc(u_copied, DT)
            with dve.Fori(0, PIECES) as c:
                for k in range(DT):
                    dve.wait_ge(mm, 2 * DT * c + k + 1)
                    dve.tensor_copy(u_pre[:, k, ds(c * COLS, COLS)], ps[k][:, 0:COLS]).then_inc(u_copied, 1)


def scan(nc, W, bcD, u_pre, z_gate, following):
    with ExitStack() as ctx:
        m = Mem(nc, ctx, "scn")
        taps, conv_b, w_x, w_dt, b_dt, a_log, skip = (
            W.tensors[n] for n in ("taps", "conv_b", "w_x", "w_dt", "b_dt", "a_log", "skip"))
        diag = m.sb("diag", [P, DT, KS, P])
        eye = m.sb("eye", [P, P])
        a_neg = m.sb("a_neg", [P, DT, N_STATE])
        u = [m.sb(f"u{v}", [P, DT, CT]) for v in range(2)]
        delta = [m.sb(f"delta{v}", [P, DT, CT]) for v in range(2)]
        du = [m.sb(f"du{v}", [P, DT, CT]) for v in range(2)]
        far = m.sb("far", [P, CH_IMGS])
        dbl = m.sb("dbl", [XP, CT])
        RING = 4
        decay = [m.sb(f"decay{v}", [P, DT, CT]) for v in range(RING)]
        state = [m.sb(f"state{v}", [P, DT, CT]) for v in range(RING)]
        prod = [m.sb(f"prod{v}", [P, DT, CT]) for v in range(2)]
        b_row = [m.sb(f"b_row{v}", [P, CT]) for v in range(RING)]
        c_row = [m.sb(f"c_row{v}", [P, CT]) for v in range(RING)]
        YCOLS = DT * CT
        ps_y = m.ps("ps_y", [P, -(-YCOLS // 512) * 512])
        ps_p = [m.ps(f"ps_p{v}", [P, 2, 512]) for v in range(2)]

        eye_set, diag_set, a_exp, a_done = (m.sem(n) for n in ("eye_set", "diag_set", "a_exp", "a_done"))
        conv_mm, silu_done, x_mm, x_copied, bc_stored = (
            m.sem(n) for n in ("conv_mm", "silu_done", "x_mm", "x_copied", "bc_stored"))
        dt_mm, dt_read, soft_done, delta_sum, delta_done, du_done = (
            m.sem(n) for n in ("dt_mm", "dt_read", "soft_done", "delta_sum", "delta_done", "du_done"))
        soft_link = m.sem("soft_link")
        b_in = [m.sem(f"b_in{v}") for v in range(RING)]
        c_in = [m.sem(f"c_in{v}") for v in range(RING)]
        decay_done, bu_done, scan_done, c_done, sum_done = (
            m.sem(n) for n in ("decay_done", "bu_done", "scan_done", "c_done", "sum_done"))
        rows_ready, far_set, ahead = m.sem("rows_ready"), m.sem("far_set"), m.sem("ahead")
        y_out, joined, y_gated = m.sem("y_out"), m.sem("joined"), m.sem("y_gated")
        S = N_STATE
        EXP_LN = "natural_log_exp_and_others"
        block = ctx.enter_context(nc.Block())

        def run(eng, prep_all, units):
            prep_all(0)
            units(0, 0, True)
            with eng.Fori(0, CHUNKS - 1) as c:
                units(c, 1, True)
                units(c + 1, 0, True)
            units(CHUNKS - 1, 1, False)

        def after(c, d):
            return (c, 1) if d == 0 else (c + 1, 0)

        def flat(t):
            return t[:].rearrange("p d t -> p (d t)")

        def two(t, k):
            return t[:, k, :].rearrange("p (h t) -> p h t", h=2)

        @block.sync
        def _(sp):
            def load_b(d, s):
                sp.dma_start(b_row[s % RING][:], bcD[d, s].partition_broadcast(P)).then_inc(b_in[s % RING], 16)

            def load_c(d, s):
                sp.dma_start(c_row[s % RING][:], bcD[d, S + s].partition_broadcast(P)).then_inc(c_in[s % RING], 16)

            def store(c, d):
                sp.wait_ge(x_copied, 2 * c + d + 1)
                sp.dma_start(bcD[d], dbl[DT_RANK:XP, :]).then_inc(bc_stored, 16)

            def prep_all(_):
                store(0, 0)
                sp.wait_ge(bc_stored, 16)
                for s in range(3):
                    load_b(0, s)
                load_c(0, 0)

            def units(c, d, more):
                for s in range(S):
                    n = (2 * c + d) * S + s
                    if s == 10 and more:
                        store(*after(c, d))
                        sp.wait_ge(bc_stored, 16 * (2 * c + d + 2))
                        sp.sem_inc(rows_ready, 1)
                    if s + 3 < S or more:
                        if not (isinstance(n, int) and n == 0):
                            sp.wait_ge(bu_done, n)
                        load_b(d if s + 3 < S else 1 - d, (s + 3) % S)
                    if s + 1 < S or more:
                        if not (isinstance(n, int) and n < 3):
                            sp.wait_ge(c_done, n - 2)
                        load_c(d if s + 1 < S else 1 - d, (s + 1) % S)

            run(sp, prep_all, units)
            following.load(sp, ahead)

        @block.tensor
        def _(pe):
            def conv(c, d, k):
                b = 2 * c + d
                if k == 2:
                    pe.wait_ge(silu_done, DT * b + 1)
                elif not (isinstance(b, int) and b == 0):
                    pe.wait_ge(dt_read, DT * b - 1 + k)
                bank = ps_p[(d + k) % 2]
                for h in range(2):
                    for j in range(KS):
                        sh, tap = j, KS - 1 - j
                        o = bank[:, h, 0:HC].rearrange("p (i t) -> p i t", t=POS)
                        x = u_pre[:, k, ds(c * CT + h * HC, HC)].rearrange("p (i t) -> p i t", t=POS)
                        if d == 0:
                            o, x = o[:, :, sh:POS], x[:, :, 0:POS - sh]
                        else:
                            o, x = o[:, :, 0:POS - sh], x[:, :, sh:POS]
                        last = pe.matmul(o, diag[:, k, tap, :], x, start=j == 0, stop=j == KS - 1)
                last.then_inc(conv_mm, 1)

            def xproj(c, d):
                pe.wait_ge(silu_done, DT * (2 * c + d) + DT)
                for h in range(2):
                    for k in range(DT):
                        last = pe.matmul(ps_p[(d + 3) % 2][0:XP, h, 0:HC], w_x[:, k, :], u[d][:, k, h * HC:(h + 1) * HC],
                                         start=k == 0, stop=k == DT - 1)
                last.then_inc(x_mm, 1)

            def dt_(c, d, k):
                pe.wait_ge(x_copied, 2 * c + d + 1)
                if k == 2:
                    pe.wait_ge(dt_read, DT * (2 * c + d) + 1)
                for h in range(2):
                    last = pe.matmul(ps_p[(d + k) % 2][:, h, 0:HC], w_dt[:, k * P:(k + 1) * P], dbl[0:DT_RANK, h * HC:(h + 1) * HC],
                                     start=True, stop=True)
                last.then_inc(dt_mm, 1)

            def prep_all(_):
                pe.wait_ge(diag_set, 1)
                for k in range(DT):
                    conv(0, 0, k)
                xproj(0, 0)
                for k in range(DT):
                    dt_(0, 0, k)

            def units(c, d, more):
                b2 = after(c, d)
                for s in range(S):
                    n = (2 * c + d) * S + s
                    if more:
                        if s in (0, 1, 3):
                            conv(*b2, (s + 1) // 2 if s < 3 else 2)
                        if s == 5:
                            xproj(*b2)
                        if s in (8, 9, 10):
                            dt_(*b2, s - 8)
                    pe.wait_ge(c_done, n + 1)
                    if s == 0 and not (isinstance(n, int) and n == 0):
                        pe.wait_ge(y_out, 2 * c + d)
                    for at in range(0, YCOLS, 512):
                        cols = slice(at, min(at + 512, YCOLS))
                        last = pe.matmul(ps_y[:, cols], eye[:], flat(prod[s % 2])[:, cols], start=s == 0, stop=s == S - 1)
                    last.then_inc(sum_done, 1)

            run(pe, prep_all, units)

        @block.scalar
        def _(act):
            def silu(c, d, k):
                act.wait_ge(conv_mm, DT * (2 * c + d) + k + 1)
                if k == 0 and not (isinstance(c, int) and c == 0):
                    if d == 0:
                        act.wait_ge(y_out, 2 * c - 1)
                    else:
                        act.wait_ge(joined, c)
                act.activation(two(u[d], k), ps_p[(d + k) % 2][:, :, 0:HC], ACT.Silu, bias=conv_b[:, k:k + 1]).then_inc(silu_done, 1)
                act.preload_act_table_set(EXP_LN)

            def x_copy(c, d):
                act.wait_ge(x_mm, 2 * c + d + 1)
                if not (isinstance(c, int) and c == 0 and d == 0):
                    act.wait_ge(bc_stored, 16 * (2 * c + d))
                    act.wait_ge(dt_mm, DT * (2 * c + d))
                act.activation(dbl[:].rearrange("p (h t) -> p h t", h=2), ps_p[(d + 3) % 2][0:XP, :, 0:HC], ACT.Copy
                               ).then_inc(x_copied, 1)

            def softplus(c, d, k):
                r = DT * (2 * c + d) + k
                act.wait_ge(dt_mm, r + 1)
                if not (isinstance(c, int) and c == 0) and k == 0:
                    act.wait_ge(decay_done, (2 * c + d - 1) * S)
                    act.wait_ge(bu_done, (2 * c + d - 1) * S)
                x = ps_p[(d + k) % 2][:, :, 0:HC]
                act.activation(two(du[d], k), x, ACT.Relu, bias=b_dt[:, k:k + 1])
                act.activation(two(delta[d], k), x, ACT.Abs, bias=b_dt[:, k:k + 1]).then_inc(dt_read, 1)
                act.wait_ge(dt_read, r + 1)
                act.activation(delta[d][:, k, :], delta[d][:, k, :], ACT.Exp, scale=-1.0).then_inc(soft_link, 1)
                act.wait_ge(soft_link, r + 1)
                act.activation(delta[d][:, k, :], delta[d][:, k, :], ACT.Ln, bias=1.0).then_inc(soft_done, 1)

            def prep_all(_):
                act.preload_act_table_set(EXP_LN)
                act.activation(a_log[:], a_log[:], ACT.Exp).then_inc(a_exp, 1)
                for k in range(DT):
                    silu(0, 0, k)
                x_copy(0, 0)
                for k in range(DT):
                    softplus(0, 0, k)
                act.wait_ge(a_done, 1)

            def units(c, d, more):
                b2 = after(c, d)
                for s in range(S):
                    n = (2 * c + d) * S + s
                    if s == 0:
                        act.wait_ge(delta_done, DT * (2 * c + d + 1))
                    if not (isinstance(n, int) and n < RING):
                        act.wait_ge(scan_done, n - RING + 1)
                    for k in range(DT):
                        last = act.activation(decay[s % RING][:, k, :], delta[d][:, k, :], ACT.Exp, scale=a_neg[:, k, s:s + 1])
                    last.then_inc(decay_done, 1)
                    if more:
                        if s in (4, 5, 6):
                            silu(*b2, s - 4)
                        if s == 8:
                            x_copy(*b2)
                        if s in (11, 12, 13):
                            softplus(*b2, s - 11)

            run(act, prep_all, units)

        @block.gpsimd
        def _(pool):
            def delta_(c, d, k):
                r = DT * (2 * c + d) + k
                pool.wait_ge(soft_done, r + 1)
                pool.tensor_tensor(delta[d][:, k, :], delta[d][:, k, :], du[d][:, k, :], ALU.add).then_inc(delta_sum, 1)

            def prep_all(_):
                pool.memset(eye[:], 0.0).then_inc(eye_set, 1)
                pool.wait_ge(eye_set, 1)
                pool.affine_select(out=eye[:], in_=eye[:], compare_op=ALU.not_equal, fill=1.0, base=0,
                                   pattern=[[-1, P]], channel_multiplier=1).then_inc(eye_set, 1)
                pool.memset(far[:], FAR).then_inc(far_set, 1)
                for k in range(DT):
                    delta_(0, 0, k)

            def join(c):
                pool.wait_ge(y_out, 2 * c + 2)
                at = ds(c * CT, CT)
                pool.tensor_tensor(u_pre[:, :, at], u_pre[:, :, at], u[1][:], ALU.add).then_inc(joined, 1)

            def units(c, d, more):
                b2 = after(c, d)
                for s in range(S):
                    n = (2 * c + d) * S + s
                    uses = S // RING * (2 * c + d) + s // RING
                    pool.wait_ge(b_in[s % RING], 16 * (uses + 1))
                    if s == 0:
                        pool.wait_ge(du_done, DT * (2 * c + d + 1))
                    if not (isinstance(n, int) and n < RING):
                        pool.wait_ge(c_done, n - RING + 1)
                    pool.tensor_tensor(state[s % RING][:], du[d][:], b_row[s % RING][:].unsqueeze(1).to_broadcast([P, DT, CT]),
                                       ALU.mult).then_inc(bu_done, 1)
                    if more and s in (11, 12, 13):
                        delta_(*b2, s - 11)
                    if d == 0 and s == 3 and not (isinstance(c, int) and c == 0):
                        join(c - 1)

            run(pool, prep_all, units)
            join(CHUNKS - 1)

        @block.vector
        def _(dve):
            def c_mul(blk, s):
                n = blk * S + s
                dve.wait_ge(scan_done, n + 1)
                dve.wait_ge(c_in[s % RING], 16 * (S // RING * blk + s // RING + 1))
                if not (isinstance(n, int) and n < 2):
                    dve.wait_ge(sum_done, n - 1)
                dve.tensor_tensor(prod[s % 2][:], state[s % RING][:],
                                  c_row[s % RING][:].unsqueeze(1).to_broadcast([P, DT, CT]), ALU.mult).then_inc(c_done, 1)

            def read_y(c, d):
                dve.wait_ge(sum_done, S * (2 * c + d + 1))
                if d == 0:
                    dve.wait_ge(conv_mm, DT * (2 * c + 2))
                for k in range(DT):
                    o = u_pre[:, k, ds(c * CT, CT)] if d == 0 else u[1][:, k, :]
                    last = dve.scalar_tensor_tensor(out=o, in0=u[d][:, k, :], scalar=skip[:, k:k + 1],
                                                    in1=ps_y[:, k * CT:(k + 1) * CT], op0=ALU.mult, op1=ALU.add)
                last.then_inc(y_out, 1)

            def gate(c):
                dve.wait_ge(joined, c + 1)
                at = ds(c * CT, CT)
                dve.tensor_tensor(u_pre[:, :, at], u_pre[:, :, at], z_gate[:, :, at], ALU.mult).then_inc(y_gated, 1)

            def du_(c, d, k):
                r = DT * (2 * c + d) + k
                dve.wait_ge(delta_sum, r + 1)
                dve.tensor_tensor(du[d][:, k, :], delta[d][:, k, :], u[d][:, k, :], ALU.mult).then_inc(du_done, 1)
                dve.wait_ge(du_done, r + 1)
                first = (0 if d == 0 else POS - 1)
                starts = delta[d][:, k, first:CT:POS]
                dve.tensor_tensor(starts, starts, far[:], ALU.add).then_inc(delta_done, 1)

            def prep_all(_):
                dve.wait_ge(a_exp, 1)
                dve.tensor_scalar(a_neg[:], a_log[:], -1.0, None, ALU.mult).then_inc(a_done, 1)
                dve.wait_ge(eye_set, 2)
                dve.wait_ge(far_set, 1)
                for k in range(DT):
                    for j in range(KS):
                        last = dve.tensor_scalar(diag[:, k, j, :], eye[:], taps[:, k, j:j + 1], None, ALU.mult)
                last.then_inc(diag_set, 1)
                for k in range(DT):
                    du_(0, 0, k)

            def one(c, d, s, first=False):
                n = (2 * c + d) * S + s
                dve.wait_ge(decay_done, n + 1)
                dve.wait_ge(bu_done, n + 1)
                x, a = flat(state[s % RING]), flat(decay[s % RING])
                if d == 1:
                    x, a = x[:, ::-1], a[:, ::-1]
                dve.tensor_tensor_scan(x, a, x, 0.0, ALU.mult, ALU.add).then_inc(scan_done, 1)
                if not first:
                    c_mul(2 * c + d - (s == 0), (s - 1) % S)

            def units(c, d, first=False, more=True):
                for s in range(S):
                    one(c, d, s, first and s == 0)
                    if more and s in (11, 12, 13):
                        du_(*after(c, d), s - 11)
                    if d == 0 and s == 6 and not (isinstance(c, int) and c == 0):
                        gate(c - 1)
                    if s == 1 and not first:
                        read_y(*((c - 1, 1) if d == 0 else (c, 0)))

            prep_all(0)
            units(0, 0, True)
            with dve.Fori(0, CHUNKS - 1) as c:
                units(c, 1)
                units(c + 1, 0)
            units(CHUNKS - 1, 1, more=False)
            c_mul(2 * CHUNKS - 1, S - 1)
            read_y(CHUNKS - 1, 1)
            gate(CHUNKS - 1)


def out_projection(nc, W, y, R):
    with ExitStack() as ctx:
        m = Mem(nc, ctx, "outp")
        w = W.tensors["w"]
        ps = [m.ps(f"ps{v}", [P, 512]) for v in range(4)]
        mm, added = m.sem("mm"), m.sem("added")
        block = ctx.enter_context(nc.Block())

        @block.tensor
        def _(pe):
            for t in range(TILES):
                if t >= 4:
                    pe.wait_ge(added, t - 3)
                for k in range(DT):
                    last = pe.matmul(ps[t % 4][:, 0:D], y[:, k, t * P:(t + 1) * P], w[:, k, :],
                                     start=k == 0, stop=k == DT - 1)
                last.then_inc(mm, 1)

        @block.vector
        def _(dve):
            for t in range(TILES):
                dve.wait_ge(mm, t + 1)
                dve.scalar_tensor_tensor(out=R[:, t, :], in0=ps[t % 4][:, 0:D], scalar=0.5, in1=R[:, t, :],
                                         op0=ALU.mult, op1=ALU.add).then_inc(added, 1)


def mamba(nc, A, R, ident, bcD):
    with ExitStack() as ctx:
        u_pre = ctx.enter_context(nc.sbuf_tensor("u_pre", [P, DT, TOK], F32))
        z_gate = ctx.enter_context(nc.sbuf_tensor("z_gate", [P, DT, TOK], F32))
        w_scan = Weights(nc, ctx, "scn", {
            "taps": ([P, DT, KS], A["conv_w"]), "conv_b": ([P, DT], A["conv_b"]), "w_x": ([P, DT, XP], A["xproj_w"]),
            "w_dt": ([DT_RANK, D_INNER], A["dt_w"]), "b_dt": ([P, DT], A["dt_b"]),
            "a_log": ([P, DT, N_STATE], A["A_log"]), "skip": ([P, DT], A["D"])})
        with ExitStack() as inner:
            featT = inner.enter_context(nc.sbuf_tensor("m_feat", [DH, 2, TOK], F32))
            W = Weights(nc, inner, "inp", {"w": ([DH, 2, 2 * D_INNER], A["in_w"])})
            layer_norm(nc, "mln", ident, R, featT, add_to=R, affine=(A["norm_w"], A["norm_b"]), twice=True, following=W)
            in_projection(nc, W, featT, u_pre, z_gate, following=w_scan)
        W = Weights(nc, ctx, "outp", {"w": ([P, DT, D], A["out_w"])})
        scan(nc, w_scan, bcD, u_pre, z_gate, following=W)
        out_projection(nc, W, u_pre, R)



def scores_and_mixer(nc, W, ident, normT, mixT, mask, scD, maskD, following):
    with ExitStack() as ctx:
        m = Mem(nc, ctx, "sc")
        wr, br = W.tensors["wr"], W.tensors["br"]
        score = m.sb("score", [DH, TOK])
        prod = m.sb("prod", [DH, 2, TOK])
        pooled = m.sb("pooled", [DH, 2, IMGS])
        total = m.sb("total", [DH, IMGS])
        inv = m.sb("inv", [DH, IMGS])
        ranks = m.sb("ranks", [IMGS, POS + PAD])
        neg = m.sb("neg", [IMGS, POS + PAD])
        low = m.sb("low", [IMGS, 8])
        marked = m.sb("marked", [IMGS, POS + PAD])
        mask_rows = m.sb("mask_rows", [TILES, P])
        ps = [m.ps(f"ps{v}", [DH, 512]) for v in range(PIECES)]
        ps_m = m.ps("ps_m", [P, 512])
        mask_turned = m.sem("mask_turned")
        ahead, mm, sig, sc_out, sc_in = (m.sem(n) for n in ("ahead", "mm", "sig", "sc_out", "sc_in"))
        link, mask_done, mask_out, mask_in = (m.sem(n) for n in ("link", "mask_done", "mask_out", "mask_in"))
        weighed, summed, pool_link, inv_done, mixed = (
            m.sem(n) for n in ("weighed", "summed", "pool_link", "inv_done", "mixed"))
        block = ctx.enter_context(nc.Block())

        def imgs(t):
            return t.rearrange("c (i q) -> c i q", q=POS)

        @block.sync
        def _(sp):
            following.load(sp, ahead)
            sp.wait_ge(sig, PIECES)
            sp.dma_start(scD, score[0:1, :]).then_inc(sc_out, 16)
            sp.wait_ge(sc_out, 16)
            sp.dma_start(ranks[:, 0:POS], scD.rearrange("o (i q) -> (o i) q", q=POS)).then_inc(sc_in, 16)
            sp.wait_ge(mask_done, 1)
            sp.dma_start(maskD.rearrange("o (i q) -> (o i) q", q=POS), marked[:, 0:POS]).then_inc(mask_out, 16)
            sp.wait_ge(mask_out, 16)
            sp.dma_start(mask_rows[:], maskD.rearrange("o (t p) -> (o t) p", p=P)).then_inc(mask_in, 16)

        @block.tensor
        def _(pe):
            for c in range(PIECES):
                for h in range(2):
                    last = pe.matmul(ps[c][:, 0:COLS], wr[:, h, :], normT[:, h, c * COLS:(c + 1) * COLS],
                                     start=h == 0, stop=h == 1)
                last.then_inc(mm, 1)
            pe.wait_ge(mask_in, 16)
            pe.transpose(ps_m[:, 0:TILES], mask_rows[:], ident[0:TILES, 0:TILES]).then_inc(mask_turned, 1)

        @block.scalar
        def _(act):
            for c in range(PIECES):
                act.wait_ge(mm, c + 1)
                act.activation(score[:, c * COLS:(c + 1) * COLS], ps[c][:, 0:COLS], ACT.Sigmoid, bias=br[:, 0:1]
                               ).then_inc(sig, 1)

        @block.gpsimd
        def _(pool):
            pool.wait_ge(sig, PIECES)
            pool.tensor_tensor(prod[:, 1, :], normT[:, 1, :], score[:], ALU.mult).then_inc(weighed, 1)
            pool.wait_ge(pool_link, 2)
            pool.tensor_tensor(imgs(prod[:, 1, :]), imgs(score[:]), pooled[:, 1, :].unsqueeze(2).to_broadcast([DH, IMGS, POS]),
                               ALU.mult).then_inc(weighed, 1)
            pool.wait_ge(weighed, 2)
            pool.tensor_tensor(mixT[:, 1, :], prod[:, 1, :], normT[:, 1, :], ALU.add).then_inc(mixed, 1)

        @block.vector
        def _(dve):
            n = [0]

            def linked(ins):
                n[0] += 1
                ins.then_inc(link, 1)
                dve.wait_ge(link, n[0])

            dve.memset(neg[:], -2.0).then_inc(link, 1)
            n[0] += 1
            dve.wait_ge(sig, PIECES)
            linked(dve.tensor_tensor(prod[:, 0, :], normT[:, 0, :], score[:], ALU.mult))
            dve.tensor_reduce(pooled[:, 0, :], imgs(prod[:, 0, :]), AX_X, ALU.add).then_inc(summed, 1)
            dve.tensor_reduce(total[:], imgs(score[:]), AX_X, ALU.add).then_inc(summed, 1)
            dve.wait_ge(weighed, 1)
            dve.tensor_reduce(pooled[:, 1, :], imgs(prod[:, 1, :]), AX_X, ALU.add).then_inc(summed, 1)
            dve.wait_ge(summed, 3)
            linked(dve.tensor_scalar(total[:], total[:], 1e-6, None, ALU.add))
            linked(dve.reciprocal(inv[:], total[:]))
            for h in range(2):
                dve.tensor_tensor(pooled[:, h, :], pooled[:, h, :], inv[:], ALU.mult).then_inc(pool_link, 1)
            dve.wait_ge(pool_link, 2)
            linked(dve.tensor_tensor(imgs(prod[:, 0, :]), imgs(score[:]),
                                     pooled[:, 0, :].unsqueeze(2).to_broadcast([DH, IMGS, POS]), ALU.mult))
            dve.tensor_tensor(mixT[:, 0, :], prod[:, 0, :], normT[:, 0, :], ALU.add).then_inc(mixed, 1)
            dve.wait_ge(sc_in, 16)
            linked(dve.tensor_scalar(neg[:, 0:POS], ranks[:, 0:POS], -1.0, None, ALU.mult))
            linked(dve.max(low[:], neg[:]))
            linked(dve.memset(low[:, KEEP:8], -2.0))
            linked(dve.match_replace(out=marked[:], in_to_replace=low[:], in_values=neg[:], imm_value=5.0))
            dve.tensor_scalar(marked[:], marked[:], 1.0, None, ALU.is_ge).then_inc(mask_done, 1)
            dve.wait_ge(mask_turned, 1)
            dve.tensor_copy(mask[:, 0, :], ps_m[:, 0:TILES]).then_inc(mask_done, 1)
            dve.tensor_scalar(mask[:, 1, :], ps_m[:, 0:TILES], -1.0, 1.0, ALU.mult, ALU.add).then_inc(mask_done, 1)


def qkv_projection(nc, W, featT, q, k, v):
    outs = [(t, h) for t in (q, k, v) for h in range(2)]
    with ExitStack() as ctx:
        m = Mem(nc, ctx, "qkv")
        w, b = W.tensors["w"], W.tensors["b"]
        ps = [m.ps(f"ps{n}", [DH, 512]) for n in range(6)]
        mm = m.sem("mm")
        copied = [m.sem(f"copied{e}") for e in range(2)]
        block = ctx.enter_context(nc.Block())

        @block.tensor
        def _(pe):
            with pe.Fori(0, PIECES) as c:
                for n in range(6):
                    pe.wait_ge(copied[n % 2], 3 * c + n // 2 + 1)
                    for h in range(2):
                        last = pe.matmul(ps[n][:, 0:COLS], w[:, h, n * DH:(n + 1) * DH], featT[:, h, ds(c * COLS, COLS)],
                                         start=h == 0, stop=h == 1)
                    last.then_inc(mm, 1)

        @block.scalar
        def _(act):
            act.sem_inc(copied[0], 3)
            with act.Fori(0, PIECES) as c:
                for n in range(0, 6, 2):
                    t, h = outs[n]
                    act.wait_ge(mm, 6 * c + n + 1)
                    act.activation(t[:, h, ds(c * COLS, COLS)], ps[n][:, 0:COLS], ACT.Identity, bias=b[:, n:n + 1]
                                   ).then_inc(copied[0], 1)

        @block.vector
        def _(dve):
            dve.sem_inc(copied[1], 3)
            with dve.Fori(0, PIECES) as c:
                for n in range(1, 6, 2):
                    t, h = outs[n]
                    dve.wait_ge(mm, 6 * c + n + 1)
                    dve.tensor_scalar(t[:, h, ds(c * COLS, COLS)], ps[n][:, 0:COLS], b[:, n:n + 1], None, ALU.add
                                      ).then_inc(copied[1], 1)


def attention(nc, A, tag, ident, q, k, v, ctxT, following):
    with ExitStack() as ctx:
        m = Mem(nc, ctx, tag)
        kmask = m.sb("kmask", [DH, HH])
        vmask = m.sb("vmask", [K3, D])
        qs = [m.sb(f"qs{u}", [DH, 2, PAIR]) for u in range(2)]
        vs = [m.sb(f"vs{u}", [DH, 2, 2, H3, POS]) for u in range(2)]
        kb = [m.sb(f"kb{u}", [DH, 2, 2, HH, POS]) for u in range(2)]
        prob = [m.sb(f"prob{u}", [PROWS, HEADS, POS]) for u in range(2)]
        top = [m.sb(f"top{u}", [PROWS, HEADS]) for u in range(2)]
        den = [m.sb(f"den{u}", [PROWS, HEADS]) for u in range(2)]
        rden = [m.sb(f"rden{u}", [PROWS, HEADS]) for u in range(2)]
        probT = [m.sb(f"probT{u}", [K3, GS, PROWS]) for u in range(2)]
        vb = [m.sb(f"vb{u}", [K3, 2, D]) for u in range(2)]
        cx = [m.sb(f"cx{u}", [PROWS, D]) for u in range(2)]
        ps_s = [m.ps(f"ps_s{u}", [PROWS, 512]) for u in range(2)]
        ps_p = [m.ps(f"ps_p{u}", [K3, 512]) for u in range(2)]
        ps_v = m.ps("ps_v", [K3, 512])
        ps_c = m.ps("ps_c", [PROWS, 512])
        ps_t = m.ps("ps_t", [DH, 512])
        masks_in, ahead = m.sem("masks_in"), m.sem("ahead")
        qk_ready, v_ready, qk_mm, sub_done, exp_done = (
            m.sem(n) for n in ("qk_ready", "v_ready", "qk_mm", "sub_done", "exp_done"))
        p_turned, p_copied, v_turned, vb_done, pv_mm, cx_done, c_turned, c_copied = (
            m.sem(n) for n in ("p_turned", "p_copied", "v_turned", "vb_done", "pv_mm", "cx_done", "c_turned", "c_copied"))
        top_done, den_done, rden_done = m.sem("top_done"), m.sem("den_done"), m.sem("rden_done")
        block = ctx.enter_context(nc.Block())

        def skewed(eng, stages):
            depth = len(stages)

            def step(p, parity):
                for lag, stage in enumerate(stages):
                    if stage and not (isinstance(p, int) and not 0 <= p - lag < PAIRS):
                        stage(p - lag, (parity + lag) % 2)
            for p in range(4):
                step(p, p % 2)
            with eng.Fori(2, PAIRS // 2) as i:
                for u in range(2):
                    step(2 * i + u, u)
            for p in range(PAIRS, PAIRS + depth - 1):
                step(p, p % 2)

        def late(p, n):
            return not (isinstance(p, int) and p < n)

        @block.sync
        def _(sp):
            sp.dma_start(kmask[:], A["kmask"]).then_inc(masks_in, 16)
            sp.dma_start(vmask[:], A["vmask"]).then_inc(masks_in, 16)
            following.load(sp, ahead)

        @block.gpsimd
        def _(pool):
            def stage(p, u):
                if late(p, 2):
                    pool.wait_ge(qk_mm, p - 1)
                at = ds(p * PAIR, PAIR)
                pool.tensor_copy(qs[u][:], q[:, :, at])
                for h in range(2):
                    last = pool.tensor_tensor(
                        kb[u][:, h],
                        k[:, h, at].rearrange("c (i t) -> c i t", i=2).unsqueeze(2).to_broadcast([DH, 2, HH, POS]),
                        kmask[:].unsqueeze(1).unsqueeze(3).to_broadcast([DH, 2, HH, POS]), ALU.mult)
                last.then_inc(qk_ready, 1)

            pool.wait_ge(masks_in, 32)
            skewed(pool, [stage])

        @block.tensor
        def _(pe):
            def scores(p, u):
                pe.wait_ge(qk_ready, p + 1)
                if late(p, 2):
                    pe.wait_ge(sub_done, p - 1)
                for h in range(2):
                    cols = slice(h * HH * POS, (h + 1) * HH * POS)
                    pe.matmul(ps_s[u][0:ROW_B, cols], qs[u][:, h, 0:ROW_B], kb[u][:, h, 0], start=True, stop=True)
                    last = pe.matmul(ps_s[u][ROW_B:PROWS, cols], qs[u][:, h, POS:PAIR], kb[u][:, h, 1],
                                     start=True, stop=True)
                last.then_inc(qk_mm, 1)

            def turn(p, u):
                pe.wait_ge(exp_done, p + 1)
                if late(p, 2):
                    pe.wait_ge(p_copied, p - 1)
                for g in range(GS):
                    last = pe.transpose(ps_p[u][:, g * PROWS:(g + 1) * PROWS], prob[u][:, g * H3:(g + 1) * H3, :],
                                        ident[0:PROWS, 0:PROWS])
                last.then_inc(p_turned, 1)
                pe.wait_ge(v_ready, p + 1)
                if late(p, 1):
                    pe.wait_ge(vb_done, p)
                for i in range(2):
                    for h in range(2):
                        last = pe.transpose(ps_v[:, i * D + h * DH:i * D + (h + 1) * DH],
                                            vs[u][:, h, i].rearrange("c r t -> c (r t)"),
                                            ident[0:DH, 0:DH])
                last.then_inc(v_turned, 1)

            def values(p, u):
                pe.wait_ge(p_copied, p + 1)
                pe.wait_ge(vb_done, p + 1)
                if late(p, 1):
                    pe.wait_ge(cx_done, p)
                W3 = H3 * HD
                for g in range(GS):
                    cols = slice(g * W3, (g + 1) * W3)
                    pe.matmul(ps_c[0:ROW_B, cols], probT[u][:, g, 0:ROW_B], vb[u][:, 0, cols], start=True, stop=True)
                    last = pe.matmul(ps_c[ROW_B:PROWS, cols], probT[u][:, g, ROW_B:PROWS], vb[u][:, 1, cols],
                                     start=True, stop=True)
                last.then_inc(pv_mm, 1)

            def turn_back(p, u):
                pe.wait_ge(cx_done, p + 1)
                if late(p, 1):
                    pe.wait_ge(c_copied, p)
                for h in range(2):
                    last = pe.transpose(ps_t[:, h * PROWS:(h + 1) * PROWS], cx[u][:, h * DH:(h + 1) * DH],
                                        ident[0:PROWS, 0:PROWS])
                last.then_inc(c_turned, 1)

            skewed(pe, [scores, turn, values, turn_back])

        @block.scalar
        def _(act):
            def exps(p, u):
                act.wait_ge(sub_done, p + 1)
                act.activation(prob[u][:], prob[u][:], ACT.Exp, scale=float(HD) ** -0.5).then_inc(exp_done, 1)

            def copy_p(p, u):
                act.wait_ge(p_turned, p + 1)
                if late(p, 2):
                    act.wait_ge(pv_mm, p - 1)
                act.activation(probT[u][:].rearrange("c g t -> c (g t)"), ps_p[u][:, 0:GS * PROWS], ACT.Copy
                               ).then_inc(p_copied, 1)

            def copy_c(p, u):
                act.wait_ge(c_turned, p + 1)
                for h in range(2):
                    src = ps_t[:, h * PROWS:(h + 1) * PROWS]
                    src = bass.AP(tensor=src.tensor, offset=src.offset, ap=[src.ap[0], [ROW_B, 2], [1, POS]])
                    last = act.activation(ctxT[:, h, ds(p * PAIR, PAIR)].rearrange("c (i t) -> c i t", i=2), src, ACT.Copy)
                last.then_inc(c_copied, 1)

            def stage_v(p, u):
                if late(p, 2):
                    act.wait_ge(v_turned, p - 1)
                for h in range(2):
                    src = v[:, h, ds(p * PAIR, PAIR)].rearrange("c (i t) -> c i t", i=2)
                    last = act.activation(vs[u][:, h], src.unsqueeze(2).to_broadcast([DH, 2, H3, POS]), ACT.Copy)
                last.then_inc(v_ready, 1)

            def values_and_exps(p, u):
                stage_v(p, u)
                exps(p, u)

            skewed(act, [values_and_exps, copy_p, None, copy_c])

        @block.vector
        def _(dve):
            def center(p, u):
                dve.wait_ge(qk_mm, p + 1)
                s = ps_s[u][:, 0:HEADS * POS].rearrange("q (h t) -> q h t", t=POS)
                dve.tensor_reduce(top[u][:], s, AX_X, ALU.max).then_inc(top_done, 1)
                dve.wait_ge(top_done, p + 1)
                if late(p, 2):
                    dve.wait_ge(p_turned, p - 1)
                    dve.wait_ge(den_done, p - 1)
                dve.tensor_tensor(prob[u][:], s, top[u][:].unsqueeze(2).to_broadcast([PROWS, HEADS, POS]), ALU.subtract
                                  ).then_inc(sub_done, 1)

            def sums_and_values(p, u):
                dve.wait_ge(exp_done, p + 1)
                dve.tensor_reduce(den[u][:], prob[u][:], AX_X, ALU.add).then_inc(den_done, 1)
                dve.wait_ge(v_turned, p + 1)
                if late(p, 2):
                    dve.wait_ge(pv_mm, p - 1)
                dve.tensor_tensor(vb[u][:], ps_v[:, 0:2 * D].rearrange("c (i f) -> c i f", i=2),
                                  vmask[:].unsqueeze(1).to_broadcast([K3, 2, D]), ALU.mult).then_inc(vb_done, 1)
                dve.wait_ge(den_done, p + 1)
                if late(p, 2):
                    dve.wait_ge(cx_done, p - 1)
                dve.reciprocal(rden[u][:], den[u][:]).then_inc(rden_done, 1)

            def normalise(p, u):
                dve.wait_ge(pv_mm, p + 1)
                dve.wait_ge(rden_done, p + 1)
                if late(p, 2):
                    dve.wait_ge(c_turned, p - 1)
                dve.tensor_tensor(cx[u][:].rearrange("q (h f) -> q h f", f=HD),
                                  ps_c[:, 0:D].rearrange("q (h f) -> q h f", f=HD),
                                  rden[u][:].unsqueeze(2).to_broadcast([PROWS, HEADS, HD]), ALU.mult).then_inc(cx_done, 1)

            skewed(dve, [center, sums_and_values, normalise])


def merge(nc, W, ctxT, mixT, mask, h):
    with ExitStack() as ctx:
        m = Mem(nc, ctx, "mrg")
        w = W.tensors["w"]
        ps = [[m.ps(f"ps{v}_{u}", [P, 512]) for u in range(4)] for v in range(2)]
        mm, half_done, done = (m.sem(n) for n in ("mm", "half_done", "done"))
        block = ctx.enter_context(nc.Block())

        @block.tensor
        def _(pe):
            for t in range(TILES):
                if t >= 4:
                    pe.wait_ge(done, t - 3)
                for v, src in enumerate((ctxT, mixT)):
                    o = ps[v][t % 4][:, 0:D]
                    for hh in range(2):
                        rows = DH + 1 - hh
                        last = pe.matmul(o, src[0:rows, hh, t * P:(t + 1) * P], w[0:rows, hh, v, :],
                                         start=hh == 0, stop=hh == 1)
                last.then_inc(mm, 1)

        @block.vector
        def _(dve):
            for t in range(TILES):
                dve.wait_ge(mm, t + 1)
                dve.scalar_tensor_tensor(out=h[:, t, :], in0=ps[0][t % 4][:, 0:D], scalar=mask[:, 0, t:t + 1],
                                         in1=h[:, t, :], op0=ALU.mult, op1=ALU.add).then_inc(half_done, 1)
                dve.wait_ge(half_done, t + 1)
                dve.scalar_tensor_tensor(out=h[:, t, :], in0=ps[1][t % 4][:, 0:D], scalar=mask[:, 1, t:t + 1],
                                         in1=h[:, t, :], op0=ALU.mult, op1=ALU.add).then_inc(done, 1)


def mlp(nc, W, featT, h, R):
    with ExitStack() as ctx:
        m = Mem(nc, ctx, "mlp")
        w1, b1, w2, b2 = (W.tensors[n] for n in ("w1", "b1", "w2", "b2"))
        hid = [m.sb(f"hid{u}", [P, FT, COLS]) for u in range(2)]
        ps1 = [m.ps(f"ps1_{u}", [P, 512]) for u in range(4)]
        ps2 = [m.ps(f"ps2_{u}", [P, 512]) for u in range(4)]
        mm1, act_done, mm2, added, base = (m.sem(n) for n in ("mm1", "act_done", "mm2", "added", "base"))
        PT_ = COLS // P
        block = ctx.enter_context(nc.Block())

        @block.gpsimd
        def _(pool):
            pool.tensor_tensor(h[:], h[:], b2[:].unsqueeze(1).to_broadcast([P, TILES, D]), ALU.add).then_inc(base, 1)
            pool.wait_ge(base, 1)
            pool.tensor_tensor(R[:], R[:], h[:], ALU.add).then_inc(base, 1)

        @block.tensor
        def _(pe):
            def first(c):
                for k in range(FT):
                    n = c * FT + k
                    if n >= 4:
                        pe.wait_ge(act_done, n - 3)
                    for hh in range(2):
                        last = pe.matmul(ps1[n % 4][:, 0:COLS], w1[:, hh, k * P:(k + 1) * P],
                                         featT[:, hh, c * COLS:(c + 1) * COLS], start=hh == 0, stop=hh == 1)
                    last.then_inc(mm1, 1)

            def second(c):
                pe.wait_ge(act_done, FT * (c + 1))
                for t in range(PT_):
                    n = c * PT_ + t
                    if n >= 4:
                        pe.wait_ge(added, n - 3)
                    for k in range(FT):
                        last = pe.matmul(ps2[n % 4][:, 0:D], hid[c % 2][:, k, t * P:(t + 1) * P], w2[:, k, :],
                                         start=k == 0, stop=k == FT - 1)
                    last.then_inc(mm2, 1)

            first(0)
            for c in range(1, PIECES):
                first(c)
                second(c - 1)
            second(PIECES - 1)

        @block.scalar
        def _(act):
            for c in range(PIECES):
                if c >= 2:
                    act.wait_ge(mm2, PT_ * (c - 1))
                for k in range(FT):
                    act.wait_ge(mm1, c * FT + k + 1)
                    act.activation(hid[c % 2][:, k, :], ps1[(c * FT + k) % 4][:, 0:COLS], ACT.Gelu, bias=b1[:, k:k + 1]
                                   ).then_inc(act_done, 1)

        @block.vector
        def _(dve):
            dve.wait_ge(base, 2)
            for t in range(TILES):
                dve.wait_ge(mm2, t + 1)
                dve.tensor_tensor(R[:, t, :], R[:, t, :], ps2[t % 4][:, 0:D], ALU.add).then_inc(added, 1)


def routed_ffn(nc, A, R, ident):
    scD = nc.dram_tensor("score_scratch", [1, TOK], F32).ap()
    maskD = nc.dram_tensor("mask_scratch", [1, TOK], F32).ap()
    with ExitStack() as ctx:
        h = ctx.enter_context(nc.sbuf_tensor("f_h", [P, TILES, D], F32))
        mask = ctx.enter_context(nc.sbuf_tensor("f_mask", [P, 2, TILES], F32))
        with ExitStack() as inner:
            def feat(name, rows=DH):
                return inner.enter_context(nc.sbuf_tensor(name, [rows, 2, TOK], F32))

            def weights(tag, **tensors):
                return Weights(nc, inner, tag, tensors)

            normT, mixT = feat("f_norm"), feat("f_mix", DH + 1)
            w_score = weights("sc", wr=([DH, 2, DH], A["Wr"]), br=([DH, 1], A["br"].partition_broadcast(DH)))
            layer_norm(nc, "fln", ident, R, normT, x1=h, affine=(A["g1"], A["b1"]), twice=True, following=w_score)
            w_qkv = weights("qkv", w=([DH, 2, 3 * D], A["ffn_qkv_w"]), b=([DH, 6], A["ffn_qkv_b"]))
            scores_and_mixer(nc, w_score, ident, normT, mixT[0:DH], mask, scD, maskD, following=w_qkv)
            q, k, v, ctxT = feat("f_q"), feat("f_k"), feat("f_v"), feat("f_ctx", DH + 1)
            qkv_projection(nc, w_qkv, normT, q, k, v)
            w_out = weights("mrg", w=([DH + 1, 2, 2, D], None))
            w_out.loads = [(w_out.tensors["w"][0:DH], A["ffn_om_w"]), (w_out.tensors["w"][DH:DH + 1, 0], A["ffn_om_b"])]
            w_out.loads += [(t[DH:DH + 1, 0, :], A["ones"][:, 0:TOK]) for t in (ctxT, mixT)]
            attention(nc, A, "fat", ident, q, k, v, ctxT[0:DH], following=w_out)
            merge(nc, w_out, ctxT, mixT, mask, h)
        with ExitStack() as inner:
            n2T = inner.enter_context(nc.sbuf_tensor("f_norm2", [DH, 2, TOK], F32))
            w_mlp = Weights(nc, inner, "mlp", {
                "w1": ([DH, 2, FFN], A["ffn_w1"]), "b1": ([P, FT], A["ffn_b1"]), "w2": ([P, FT, D], A["ffn_w2"]),
                "b2": ([P, D], A["ffn_b2"].partition_broadcast(P))})
            layer_norm(nc, "fln2", ident, h, n2T, affine=(A["g2"], A["b2"]), following=w_mlp)
            mlp(nc, w_mlp, n2T, h, R)



def rotary_projection(nc, W, featT, q, k, v):
    with ExitStack() as ctx:
        m = Mem(nc, ctx, "rot")
        w, cs, swap = (W.tensors[n] for n in ("w", "cs", "swap"))
        straight = [m.sb(f"straight{n}", [DH, RP]) for n in range(4)]
        swapped = [m.sb(f"swapped{u}", [DH, RP]) for u in range(2)]
        plain = [m.sb(f"plain{u}", [DH, RP]) for u in range(2)]
        ps = [m.ps(f"ps{n}", [DH, 512]) for n in range(8)]
        mm, copied, cosd, sind, turned, v_copied = (
            m.sem(n) for n in ("mm", "copied", "cosd", "sind", "turned", "v_copied"))
        block = ctx.enter_context(nc.Block())
        dst = [(t, h) for t in (q, k) for h in range(2)]

        def imgs(t):
            return t.rearrange("c (i q) -> c i q", q=POS)

        @block.tensor
        def _(pe):
            def product(bank, col, c):
                for h in range(2):
                    last = pe.matmul(ps[bank][:, 0:RP], w[:, h, col:col + DH], featT[:, h, ds(c * RP, RP)],
                                     start=h == 0, stop=h == 1)
                last.then_inc(mm, 1)

            with pe.Fori(0, RPIECES) as c:
                for n in range(4):
                    if n == 0:
                        pe.wait_ge(v_copied, 2 * c + 2)
                    else:
                        pe.wait_ge(sind, 4 * c + n + 1)
                    product(2 * n, n * DH, c)
                for n in range(4):
                    pe.wait_ge(copied, 4 * c + n + 1)
                    pe.matmul(ps[2 * n + 1][:, 0:RP], swap[:], straight[n][:], start=True, stop=True).then_inc(mm, 1)
                for h in range(2):
                    pe.wait_ge(sind, 4 * c + 5)
                    product(h, (4 + h) * DH, c)

        @block.scalar
        def _(act):
            act.sem_inc(v_copied, 2)
            with act.Fori(0, RPIECES) as c:
                for n in range(4):
                    act.wait_ge(mm, 10 * c + n + 1)
                    act.activation(straight[n][:], ps[2 * n][:, 0:RP], ACT.Copy).then_inc(copied, 1)
                for h in range(2):
                    act.wait_ge(mm, 10 * c + 9 + h)
                    act.activation(v[:, h, ds(c * RP, RP)], ps[h][:, 0:RP], ACT.Copy).then_inc(v_copied, 1)

        @block.vector
        def _(dve):
            dve.sem_inc(sind, 4)
            with dve.Fori(0, RPIECES) as c:
                for n in range(4):
                    dve.wait_ge(mm, 10 * c + n + 5)
                    dve.wait_ge(turned, 4 * c + n + 1)
                    dve.tensor_tensor(imgs(plain[n % 2][:]), imgs(ps[2 * n][:, 0:RP]),
                                      cs[:, 0, :].unsqueeze(1).to_broadcast([DH, RP // POS, POS]), ALU.mult
                                      ).then_inc(cosd, 1)
                    dve.tensor_tensor(imgs(swapped[n % 2][:]), imgs(ps[2 * n + 1][:, 0:RP]),
                                      cs[:, 1, :].unsqueeze(1).to_broadcast([DH, RP // POS, POS]), ALU.mult
                                      ).then_inc(sind, 1)

        @block.gpsimd
        def _(pool):
            pool.sem_inc(turned, 2)
            with pool.Fori(0, RPIECES) as c:
                for n in range(4):
                    t, h = dst[n]
                    pool.wait_ge(cosd, 4 * c + n + 1)
                    pool.wait_ge(sind, 4 * c + n + 5)
                    pool.tensor_tensor(t[:, h, ds(c * RP, RP)], plain[n % 2][:], swapped[n % 2][:], ALU.add
                                       ).then_inc(turned, 1)


def project_out(nc, W, ctxT, R):
    with ExitStack() as ctx:
        m = Mem(nc, ctx, "prj")
        w, b = W.tensors["w"], W.tensors["b"]
        ps = [m.ps(f"ps{u}", [P, 512]) for u in range(4)]
        mm, base, done = (m.sem(n) for n in ("mm", "base", "done"))
        block = ctx.enter_context(nc.Block())

        @block.gpsimd
        def _(pool):
            for t in range(TILES):
                pool.tensor_tensor(R[:, t, :], R[:, t, :], b[:], ALU.add).then_inc(base, 1)

        @block.tensor
        def _(pe):
            for t in range(TILES):
                if t >= 4:
                    pe.wait_ge(done, t - 3)
                for h in range(2):
                    last = pe.matmul(ps[t % 4][:, 0:D], ctxT[:, h, t * P:(t + 1) * P], w[:, h, :],
                                     start=h == 0, stop=h == 1)
                last.then_inc(mm, 1)

        @block.vector
        def _(dve):
            for t in range(TILES):
                dve.wait_ge(mm, t + 1)
                dve.wait_ge(base, t + 1)
                dve.tensor_tensor(R[:, t, :], R[:, t, :], ps[t % 4][:, 0:D], ALU.add).then_inc(done, 1)


def rotary_attention(nc, A, R, ident):
    with ExitStack() as ctx:
        def feat(name):
            return ctx.enter_context(nc.sbuf_tensor(name, [DH, 2, TOK], F32))

        normT, q, k, v, ctxT = (feat("a_" + n) for n in ("norm", "q", "k", "v", "ctx"))
        w_rot = Weights(nc, ctx, "rot", {"w": ([DH, 2, 3 * D], A["rot_w"]), "cs": ([DH, 2, POS], A["rot_cs"]),
                                             "swap": ([DH, DH], A["rot_swap"])})
        layer_norm(nc, "aln", ident, R, normT, following=w_rot)
        rotary_projection(nc, w_rot, normT, q, k, v)
        w_proj = Weights(nc, ctx, "prj", {"w": ([DH, 2, D], A["proj_w"]),
                                             "b": ([P, D], A["proj_b"].partition_broadcast(P))})
        attention(nc, A, "aat", ident, q, k, v, ctxT, following=w_proj)
        project_out(nc, w_proj, ctxT, R)



def gate_experts(nc, W, ident, featT, combT, following):
    with ExitStack() as ctx:
        m = Mem(nc, ctx, "gat")
        E, G = EXPERTS, GROUPS
        w, b, before, before_g = (W.tensors[n] for n in ("w", "b", "before", "before_g"))
        logit, prob, biased = (m.sb(n, [P, TILES, E]) for n in ("logit", "prob", "biased"))
        top, den, rden = (m.sb(n, [P, TILES]) for n in ("top", "den", "rden"))
        grp, grank = m.sb("grp", [P, TILES, G]), m.sb("grank", [P, TILES, G])
        rank = m.sb("rank", [P, TILES, E])
        wins, ties = m.sb("wins", [P, TILES, E * E]), m.sb("ties", [P, TILES, E * E])
        ps_l = m.ps("ps_l", [P, TILES, E])
        ps_c = [m.ps(f"ps_c{u}", [E, 512]) for u in range(4)]
        ahead, mm, link, centered, exped, comb, turned, copied, ones_set = (
            m.sem(n) for n in ("ahead", "mm", "link", "centered", "exped", "comb", "turned", "copied", "ones_set"))
        QUADS = -(-TILES // 4)
        block = ctx.enter_context(nc.Block())

        @block.sync
        def _(sp):
            following.load(sp, ahead)

        @block.tensor
        def _(pe):
            for t in range(TILES):
                for h in range(2):
                    last = pe.matmul(ps_l[:, t, :], featT[:, h, t * P:(t + 1) * P], w[:, h, :], start=h == 0, stop=h == 1)
            last.then_inc(mm, 1)
            pe.wait_ge(comb, 1)
            for q in range(QUADS):
                if q >= 4:
                    pe.wait_ge(copied, q - 3)
                for t in range(4 * q, min(4 * q + 4, TILES)):
                    last = pe.transpose(ps_c[q % 4][:, (t % 4) * P:(t % 4 + 1) * P], rank[:, t, :], ident[:])
                last.then_inc(turned, 1)

        @block.gpsimd
        def _(pool):
            pool.memset(combT[:], 1.0).then_inc(ones_set, 1)

        @block.scalar
        def _(act):
            act.wait_ge(centered, 1)
            act.activation(prob[:], logit[:], ACT.Exp).then_inc(exped, 1)
            act.wait_ge(ones_set, 1)
            for q in range(QUADS):
                act.wait_ge(turned, q + 1)
                n = min(4, TILES - 4 * q) * P
                act.activation(combT[0:E, 4 * q * P:4 * q * P + n], ps_c[q % 4][:, 0:n], ACT.Copy).then_inc(copied, 1)

        @block.vector
        def _(dve):
            n = [0]

            def linked(ins):
                n[0] += 1
                ins.then_inc(link, 1)
                dve.wait_ge(link, n[0])

            def over(t, k):
                return t[:].unsqueeze(2).to_broadcast([P, TILES, k])

            def ranks(out, x, k, mask):
                a = x.unsqueeze(2).to_broadcast([P, TILES, k, k])
                o = x.unsqueeze(3).to_broadcast([P, TILES, k, k])
                win = wins[:, :, 0:k * k].rearrange("p t (j i) -> p t j i", i=k)
                tie = ties[:, :, 0:k * k].rearrange("p t (j i) -> p t j i", i=k)
                linked(dve.tensor_tensor(win, a, o, ALU.is_gt))
                linked(dve.tensor_tensor(tie, a, o, ALU.is_equal))
                linked(dve.tensor_tensor(tie, tie, mask[:].unsqueeze(1).to_broadcast([P, TILES, k, k]), ALU.mult))
                linked(dve.tensor_tensor(win, win, tie, ALU.add))
                linked(dve.tensor_reduce(out, win, AX_X, ALU.add))

            dve.wait_ge(mm, 1)
            linked(dve.tensor_reduce(top[:], ps_l[:], AX_X, ALU.max))
            dve.tensor_tensor(logit[:], ps_l[:], over(top, E), ALU.subtract).then_inc(centered, 1)
            dve.wait_ge(exped, 1)
            linked(dve.tensor_reduce(den[:], prob[:], AX_X, ALU.add))
            linked(dve.reciprocal(rden[:], den[:]))
            linked(dve.tensor_tensor(prob[:], prob[:], over(rden, E), ALU.mult))
            linked(dve.tensor_tensor(biased[:], prob[:], b[:].unsqueeze(1).to_broadcast([P, TILES, E]), ALU.add))
            pairs = biased[:].rearrange("p t (g e) -> p t g e", e=E // G)
            linked(dve.tensor_tensor(grp[:], pairs[:, :, :, 0], pairs[:, :, :, 1], ALU.add))
            ranks(grank[:], grp[:], G, before_g)
            linked(dve.tensor_scalar(grank[:], grank[:], float(TOPK_GROUPS), None, ALU.is_lt))
            keep = grank[:].unsqueeze(3).to_broadcast([P, TILES, G, E // G])
            linked(dve.tensor_tensor(pairs, pairs, keep, ALU.mult))
            linked(dve.tensor_scalar(grank[:], grank[:], 1.0, OUT_OF, ALU.subtract, ALU.mult))
            linked(dve.tensor_tensor(pairs, pairs, keep, ALU.add))
            ranks(rank[:], biased[:], E, before)
            linked(dve.tensor_scalar(rank[:], rank[:], float(TOPK), None, ALU.is_lt))
            dve.tensor_tensor(rank[:], rank[:], prob[:], ALU.mult).then_inc(comb, 1)


def run_experts(nc, W, featT, combT, R, tokens):
    with ExitStack() as ctx:
        m = Mem(nc, ctx, "exp")
        NQ = QT + 1
        w13, ws13, b13, w2, ws2, b2, owner = (
            W.tensors[n] for n in ("w13", "ws13", "b13", "w2", "ws2", "b2", "owner"))
        comb = [m.sb(f"comb{u}", [EXPERTS + 1, EP]) for u in range(2)]
        h1 = [m.sb(f"h1_{u}", [P, 2, EP]) for u in range(2)]
        hh = [m.sb(f"hh{u}", [P, 2, EP]) for u in range(2)]
        sg = [m.sb(f"sg{u}", [P, EP]) for u in range(2)]
        act_ = [m.sb(f"act{u}", [P, NQ, EP]) for u in range(2)]
        ps1 = [m.ps(f"ps1_{u}", [P, 2, EP]) for u in range(2)]
        ps3 = [m.ps(f"ps3_{u}", [P, 2, EP]) for u in range(2)]
        ps_w = [m.ps(f"ps_w{u}", [P, 512]) for u in range(2)]
        ps_o = [m.ps(f"ps_o{u}", [P, 512]) for u in range(2)]
        comb_in, mm, h1_done, hh_done, clipped, sg_in, sg_done, gated = (
            m.sem(n) for n in ("comb_in", "mm", "h1_done", "hh_done", "clipped", "sg_in", "sg_done", "gated"))
        prod, lin, weighed, wmm, omm, added = (m.sem(n) for n in ("prod", "lin", "weighed", "wmm", "omm", "added"))
        block = ctx.enter_context(nc.Block())

        stored = m.sem("stored")

        @block.sync
        def _(sp):
            with sp.Fori(0, EPIECES) as c:
                sp.wait_ge(added, 2 * c + 2)
                sp.dma_start(tokens[ds(c * EP, EP)].rearrange("(t p) c -> p t c", p=P), R[:, ds(2 * c, 2), :]
                             ).then_inc(stored, 16)
            sp.wait_ge(stored, 16 * EPIECES)

        def rows(q):
            return P if q < QT else INTER

        def late(x, n):
            return not (isinstance(x, int) and x < n)

        def pieces(eng, piece):
            for c in range(3):
                piece(c, c % 2)
            with eng.Fori(1, (EPIECES - 1) // 2) as i:
                for u in range(2):
                    piece(2 * i + u + 1, 1 - u)

        @block.tensor
        def _(pe):
            def hidden(c, q, at):
                s = NQ * c + q
                u = at % 2
                if late(s, 2):
                    pe.wait_ge(h1_done, s - 1)
                    pe.wait_ge(hh_done, s - 1)
                for bank, first in ((ps1[u], 0), (ps3[u], 2)):
                    for g in range(2):
                        for h in range(2):
                            lhs = w13[:, h, q, first + g, :] if q < QT else ws13[:, h, first + g, :]
                            last = pe.matmul(bank[0:rows(q), g, :], lhs, featT[:, h, ds(c * EP, EP)],
                                             start=h == 0, stop=h == 1)
                last.then_inc(mm, 1)

            def spread(c, q, u, at):
                r = QT * c + q
                if late(r, 2):
                    pe.wait_ge(weighed, r - 1)
                pe.wait_ge(comb_in, c + 1)
                pe.matmul(ps_w[at % 2][:, 0:EP], owner[:, q, :], comb[u][0:EXPERTS, :], start=True, stop=True
                          ).then_inc(wmm, 1)

            def out(c, u):
                pe.wait_ge(weighed, QT * (c + 1))
                pe.wait_ge(gated, c + 1)
                for t in range(2):
                    if late(c, 1):
                        pe.wait_ge(added, 2 * (c - 1) + t + 1)
                    cols = slice(t * P, (t + 1) * P)
                    o = ps_o[t][:, 0:D]
                    for q in range(NQ):
                        pe.matmul(o, act_[u][0:rows(q), q, cols], w2[:, q, :] if q < QT else ws2[:], start=q == 0,
                                  stop=False)
                    pe.matmul(o, comb[u][:, cols], b2[:], start=False, stop=True).then_inc(omm, 1)

            def piece(c, u):
                for q in range(NQ):
                    hidden(c, q, NQ * u + q)
                    if q < QT:
                        spread(c, q, u, q)
                    if q == 2 and late(c, 1):
                        out(c - 1, 1 - u)

            pieces(pe, piece)
            out(EPIECES - 1, (EPIECES - 1) % 2)

        @block.scalar
        def _(act):
            def sigmoid(c, q, at):
                s = NQ * c + q
                u = at % 2
                act.wait_ge(clipped, s + 1)
                r = rows(q)
                act.activation(sg[u][0:r, :], hh[u][0:r, 0, :], ACT.Sigmoid, scale=ALPHA).then_inc(sg_done, 1)

            def piece(c, u):
                if late(c, 2):
                    act.wait_ge(omm, 2 * (c - 1))
                act.activation(comb[u][:], combT[:, ds(c * EP, EP)], ACT.Copy).then_inc(comb_in, 1)
                for q in range(NQ):
                    s = NQ * c + q
                    at = NQ * u + q
                    r = rows(q)
                    act.wait_ge(mm, s + 1)
                    if late(s, 2):
                        act.wait_ge(hh_done, s - 1)
                    for g in range(2):
                        last = act.activation(h1[at % 2][0:r, g, :], ps1[at % 2][0:r, g, :], ACT.Identity,
                                              bias=b13[0:r, q, g:g + 1])
                    last.then_inc(h1_done, 1)
                    if late(s, 1):
                        sigmoid(*((c, q - 1, at - 1) if q > 0 else (c - 1, NQ - 1, NQ * (1 - u) + NQ - 1)))

            pieces(act, piece)
            sigmoid(EPIECES - 1, NQ - 1, NQ * ((EPIECES - 1) % 2) + NQ - 1)

        @block.vector
        def _(dve):
            def first(c, q, at):
                s = NQ * c + q
                u, r = at % 2, rows(q)
                dve.wait_ge(h1_done, s + 1)
                if late(s, 2):
                    dve.wait_ge(sg_done, s - 1)
                    if q == 1:
                        dve.wait_ge(gated, c)
                    else:
                        dve.wait_ge(sg_in, QT * c + max(q - 1, 0))
                for g in range(2):
                    last = dve.scalar_tensor_tensor(out=hh[u][0:r, g, :], in0=ps3[u][0:r, g, :],
                                                    scalar=b13[0:r, q, 2 + g:3 + g], in1=h1[u][0:r, g, :],
                                                    op0=ALU.add, op1=ALU.mult)
                last.then_inc(hh_done, 1)
                dve.wait_ge(hh_done, s + 1)
                dve.tensor_scalar(hh[u][0:r, 0, :], hh[u][0:r, 0, :], LIMIT, None, ALU.min).then_inc(clipped, 1)
                dve.tensor_scalar(hh[u][0:r, 1, :], hh[u][0:r, 1, :], LIMIT, -LIMIT, ALU.min, ALU.max).then_inc(lin, 1)
                dve.wait_ge(clipped, s + 1)
                dve.wait_ge(lin, s + 1)
                dve.scalar_tensor_tensor(out=hh[u][0:r, 1, :], in0=hh[u][0:r, 1, :], scalar=1.0, in1=hh[u][0:r, 0, :],
                                         op0=ALU.add, op1=ALU.mult).then_inc(prod, 1)

            def second(c, q, at, par):
                s = NQ * c + q
                u, r = at % 2, rows(q)
                dve.wait_ge(sg_done, s + 1)
                dve.wait_ge(prod, s + 1)
                if q == 0 and late(c, 2):
                    dve.wait_ge(omm, 2 * (c - 1))
                o = act_[par][0:r, q, :]
                last = dve.tensor_tensor(o, hh[u][0:r, 1, :], sg[u][0:r, :], ALU.mult)
                if q < QT:
                    last.then_inc(sg_in, 1)
                    dve.wait_ge(wmm, QT * c + q + 1)
                    dve.wait_ge(sg_in, QT * c + q + 1)
                    dve.tensor_tensor(o, o, ps_w[q % 2][:, 0:EP], ALU.mult).then_inc(weighed, 1)
                else:
                    last.then_inc(gated, 1)

            def add(c):
                for t in range(2):
                    dve.wait_ge(omm, 2 * c + t + 1)
                    r = R[:, ds(2 * c + t, 1), :].rearrange("p o c -> p (o c)")
                    dve.tensor_tensor(r, r, ps_o[t][:, 0:D], ALU.add).then_inc(added, 1)

            def piece(c, u):
                for q in range(NQ):
                    at = NQ * u + q
                    first(c, q, at)
                    if late(NQ * c + q, 1):
                        if q > 0:
                            second(c, q - 1, at - 1, u)
                        else:
                            second(c - 1, NQ - 1, NQ * (1 - u) + NQ - 1, 1 - u)
                    if q == 4 and late(c, 1):
                        add(c - 1)

            pieces(dve, piece)
            last_u = (EPIECES - 1) % 2
            second(EPIECES - 1, NQ - 1, NQ * last_u + NQ - 1, last_u)
            add(EPIECES - 1)


def experts(nc, A, R, ident, tokens):
    with ExitStack() as ctx:
        featT = ctx.enter_context(nc.sbuf_tensor("e_feat", [DH, 2, TOK], F32))
        combT = ctx.enter_context(nc.sbuf_tensor("e_comb", [EXPERTS + 1, TOK], F32))

        w_gate = Weights(nc, ctx, "gat", {
            "w": ([DH, 2, EXPERTS], A["gate_w"]), "b": ([P, EXPERTS], A["gate_b"].partition_broadcast(P)),
            "before": ([P, EXPERTS, EXPERTS], A["before"].partition_broadcast(P)),
            "before_g": ([P, GROUPS, GROUPS], A["before_g"].partition_broadcast(P))})
        w_exp = Weights(nc, ctx, "exp", {
            "w13": ([DH, 2, QT, 4, P], A["e_w13"]), "ws13": ([DH, 2, 4, INTER], A["e_ws13"]),
            "b13": ([P, QT + 1, 4], A["e_b13"]), "w2": ([P, QT, D], A["e_w2"]), "ws2": ([INTER, D], A["e_ws2"]),
            "b2": ([EXPERTS + 1, D], A["e_b2"]), "owner": ([EXPERTS, QT, P], A["e_owner"])})
        layer_norm(nc, "eln", ident, R, featT, following=w_gate)
        gate_experts(nc, w_gate, ident, featT, combT, following=w_exp)
        run_experts(nc, w_exp, featT, combT, R, tokens)



def to_tokens(nc, R, ident, feat):
    with ExitStack() as ctx:
        m = Mem(nc, ctx, "tt")
        ps_t = [m.ps(f"ps_t{u}", [P, 512]) for u in range(4)]
        ident_zero, ident_set = m.sem("ident_zero"), m.sem("ident_set")
        turned, copied = m.sem("turned"), m.sem("copied")
        block = ctx.enter_context(nc.Block())

        @block.gpsimd
        def _(pool):
            pool.memset(ident[:], 0.0).then_inc(ident_zero, 1)
            pool.wait_ge(ident_zero, 1)
            pool.affine_select(out=ident[:], in_=ident[:], compare_op=ALU.not_equal, fill=1.0, base=0,
                               pattern=[[-1, P]], channel_multiplier=1).then_inc(ident_set, 1)

        @block.tensor
        def _(pe):
            pe.wait_ge(ident_set, 1)
            for t in range(TILES):
                if t >= 4:
                    pe.wait_ge(copied, t - 3)
                for h in range(2):
                    last = pe.transpose(ps_t[t % 4][:, h * DH:(h + 1) * DH], feat[:, h, t * P:(t + 1) * P],
                                        ident[0:DH, 0:DH])
                last.then_inc(turned, 1)

        @block.vector
        def _(dve):
            for t in range(TILES):
                dve.wait_ge(turned, t + 1)
                dve.tensor_copy(R[:, t, :], ps_t[t % 4][:, 0:D]).then_inc(copied, 1)



def tower(nc, A, out):
    offD = nc.dram_tensor("offset_scratch", [IMGS, OFF_CH, POS], F32).ap()
    bcD = nc.dram_tensor("bc_scratch", [2, 2 * N_STATE, CT], F32).ap()
    with ExitStack() as ctx:
        R = ctx.enter_context(nc.sbuf_tensor("R", [P, TILES, D], F32))
        ident = ctx.enter_context(nc.sbuf_tensor("ident", [P, P], F32))
        with nc.sbuf_tensor("tok_feat", [DH, 2, TOK], F32) as feat:
            tokenizer(nc, A, feat, offD)
            to_tokens(nc, R, ident, feat)
        mamba(nc, A, R, ident, bcD)
        routed_ffn(nc, A, R, ident)
        rotary_attention(nc, A, R, ident)
        experts(nc, A, R, ident, out)



def layouts(inputs):
    a = {k: np.ascontiguousarray(np.asarray(v)) for k, v in inputs.items()}
    L = {}

    def halves(v):
        return v.reshape(2, DH).T

    L["patches"] = a["x"].reshape(IMGS, IN_CH, SIDE1, KS, SIDE1, KS).transpose(1, 3, 5, 0, 2, 4).reshape(-1, IMGS, PIX)
    L["patches"] = L["patches"].reshape(STEM_K - 1, IMGS // 2, 2, PIX).transpose(2, 0, 1, 3).reshape(2, STEM_K - 1, -1)
    L["ones"] = np.ones((1, GPIX + PT - PT_LAST), np.float32)
    L["off_fold"] = np.tile(np.eye(OFF_CH, dtype=np.float32), (P // OFF_CH, 1))
    L["stem_w"] = a["L0_tok_stem_w"].reshape(CH1, -1).T
    L["stem_b"] = a["L0_tok_stem_b"]
    for n in ("bn1_g", "bn1_b", "bn1_m", "bn1_v"):
        L[n] = a["L0_tok_" + n]
    L["off_w"] = a["L0_tok_off_w"].reshape(TAPS, 2, CH1, TAPS).transpose(2, 3, 1, 0).reshape(CH1, TAPS, OFF_CH)
    L["off_b"] = a["L0_tok_off_b"].reshape(TAPS, 2).T.reshape(OFF_CH, 1)
    tap, pos = np.arange(TAPS)[:, None], np.arange(POS)[None, :]
    L["grid"] = np.concatenate([KS * (pos // SIDE2) + tap // KS, KS * (pos % SIDE2) + tap % KS]).astype(np.float32)
    L["dcn_w"] = a["L0_tok_dcn_w"].reshape(D, CH1, TAPS).transpose(1, 2, 0)
    for n in ("bn2_g", "bn2_b", "bn2_m", "bn2_v", "dcn_b"):
        L[n] = halves(a["L0_tok_" + n])
    p = np.arange(PT)
    L["pix_xy"] = -np.stack([p % SIDE1] + [ROWS_K * k + p // SIDE1 for k in range(KT)], 1).astype(np.float32)

    L["norm_w"], L["norm_b"] = halves(a["L0_attn_norm_w"]), halves(a["L0_attn_norm_b"])
    L["in_w"] = a["L0_attn_in_w"].T.reshape(2, DH, 2 * D_INNER).transpose(1, 0, 2)
    L["conv_w"] = a["L0_attn_conv_w"].reshape(DT, P, KS).transpose(1, 0, 2)
    L["conv_b"], L["dt_b"], L["D"] = (a["L0_attn_" + n].reshape(DT, P).T for n in ("conv_b", "dt_b", "D"))
    L["xproj_w"] = a["L0_attn_xproj_w"].T.reshape(DT, P, XP).transpose(1, 0, 2)
    L["dt_w"] = a["L0_attn_dt_w"].T
    L["A_log"] = a["L0_attn_A_log"].reshape(DT, P, N_STATE).transpose(1, 0, 2)
    L["out_w"] = a["L0_attn_out_w"].T.reshape(DT, P, D).transpose(1, 0, 2)

    for n in ("g1", "b1", "g2", "b2"):
        L[n] = halves(a["L0_ffn_" + n])
    L["Wr"] = np.repeat(a["L0_ffn_Wr"].reshape(2, DH).T[:, :, None], DH, 2)
    L["br"] = a["L0_ffn_br"].reshape(1)

    def halves_w(w):
        return w.reshape(2, DH, -1).transpose(1, 0, 2)

    L["ffn_qkv_w"] = halves_w(np.concatenate([a["L0_ffn_W" + n] for n in "qkv"], 1))
    L["ffn_qkv_b"] = np.concatenate([halves(a["L0_ffn_b" + n]) for n in "qkv"], 1)
    f = np.arange(DH)[:, None]
    L["kmask"] = (f // HD == np.arange(HH)[None, :]).astype(np.float32)
    L["vmask"] = (np.arange(K3)[:, None] // POS == np.arange(D)[None, :] // HD % H3).astype(np.float32)
    L["ffn_om_w"] = halves_w(np.concatenate([a["L0_ffn_Wo"], a["L0_ffn_Wm"]], 1)).reshape(DH, 2, 2, D)
    L["ffn_om_b"] = np.stack([a["L0_ffn_bo"], a["L0_ffn_bm"]])[None]
    L["ffn_w1"] = halves_w(a["L0_ffn_W1"])
    L["ffn_b1"] = a["L0_ffn_bf1"].reshape(FT, P).T
    L["ffn_w2"] = a["L0_ffn_W2"].reshape(FT, P, D).transpose(1, 0, 2)
    L["ffn_b2"] = a["L0_ffn_bf2"]

    wq, wk, wv = a["L1_attn_w_qkv"].reshape(3, D, D)
    L["rot_swap"] = np.eye(DH, dtype=np.float32)[np.arange(DH) ^ 1]
    L["rot_w"] = halves_w(np.concatenate([wq.T, wk.T, wv.T], 1))
    inv_freq = 1.0 / 10000.0 ** (np.arange(0, HD, 2, dtype=np.float32) / np.float32(HD))
    freqs = np.arange(POS, dtype=np.float32)[:, None] * inv_freq.astype(np.float32)[None, :]
    angle = np.repeat(freqs, 2, -1)[:, np.arange(DH) % HD].T
    sign = np.where(np.arange(DH) % 2 == 0, -1.0, 1.0)[:, None]
    L["rot_cs"] = np.stack([np.cos(angle), sign * np.sin(angle)], 1).astype(np.float32)
    L["proj_w"] = halves_w(a["L1_attn_w_proj"].T)
    L["proj_b"] = a["L1_attn_b_proj"]

    L["gate_w"] = halves_w(a["L1_ffn_gate_w"].T)
    L["gate_b"] = a["L1_ffn_gate_b"]
    for n, k in (("before", EXPERTS), ("before_g", GROUPS)):
        L[n] = (np.arange(k)[None, :] < np.arange(k)[:, None]).astype(np.float32)

    def tiles(w):
        n = w.shape[1]
        w = w.reshape(EXPERTS, n, INTER, 2).transpose(1, 3, 0, 2).reshape(n, 2, QT, P)
        return w.transpose(0, 2, 1, 3)

    w13 = np.concatenate([tiles(a["L1_ffn_W1"]), tiles(a["L1_ffn_W3"])], 2)
    L["e_w13"] = w13.reshape(2, DH, QT, 4, P).transpose(1, 0, 2, 3, 4)
    ws = np.stack([a["L1_ffn_Ws1"][:, 0::2], a["L1_ffn_Ws1"][:, 1::2],
                   a["L1_ffn_Ws3"][:, 0::2], a["L1_ffn_Ws3"][:, 1::2]], 1)
    L["e_ws13"] = ws.reshape(2, DH, 4, INTER).transpose(1, 0, 2, 3)
    b13 = np.zeros((P, QT + 1, 4), np.float32)
    b13[:, :QT] = np.concatenate([tiles(a["L1_ffn_B1"][:, None]), tiles(a["L1_ffn_B3"][:, None])], 2)[0].transpose(2, 0, 1)
    b13[:INTER, QT] = np.stack([a["L1_ffn_Bs1"][0::2], a["L1_ffn_Bs1"][1::2],
                                a["L1_ffn_Bs3"][0::2], a["L1_ffn_Bs3"][1::2]], 1)
    L["e_b13"] = b13
    L["e_w2"] = a["L1_ffn_W2"].reshape(QT, P, D).transpose(1, 0, 2)
    L["e_ws2"] = a["L1_ffn_Ws2"]
    L["e_b2"] = np.concatenate([a["L1_ffn_B2"], a["L1_ffn_Bs2"][None]])
    hidden = np.arange(QT * P).reshape(QT, P) // INTER
    L["e_owner"] = (np.arange(EXPERTS)[:, None, None] == hidden[None]).astype(np.float32)
    return {k: np.ascontiguousarray(v) for k, v in L.items()}


def kernel(**inputs):
    import concourse.bacc as bacc
    from concourse.bass_utils import run_bass_kernel_spmd

    nc = bacc.Bacc("TRN2", target_bir_lowering=False, num_devices=1)
    arrays, A = {}, {}
    for name, v in layouts(inputs).items():
        arrays["in_" + name] = v
        A[name] = nc.dram_tensor("in_" + name, v.shape, F32, kind="ExternalInput").ap()
    out = nc.dram_tensor("tokens_out", [TOK, D], F32, kind="ExternalOutput").ap()
    tower(nc, A, out)
    r = run_bass_kernel_spmd(nc, [arrays], core_ids=[0])
    return r.results[0]["tokens_out"].reshape(IMGS, POS, D)
```
